# Optimizing a Trainium2 kernel written in Bass

```python
import numpy as np
import jax
import jax.numpy as jnp

def _softmax(x, axis=-1):
    return jax.nn.softmax(x, axis=axis)

def _gelu(x):
    return jax.nn.gelu(x, approximate=True)

def _silu(x):
    return jax.nn.silu(x)

def _sigmoid(x):
    return jax.nn.sigmoid(x)

def _layernorm(x, axis=-1, eps=1e-05):
    m = jnp.mean(x, axis=axis, keepdims=True)
    v = jnp.var(x, axis=axis, keepdims=True)
    return (x - m) / jnp.sqrt(v + eps)

def _scatter_add(tgt, idx, src, axis=0):
    return tgt.at[idx].add(src)

def _segment_sum(src, seg, n):
    return jax.ops.segment_sum(src, seg, n)
kernel_name = 'mk_decoder_preln_d4_seqx_r8_d52a82'

def setup_inputs(seed: int=0):
    np.random.seed(seed)
    _w = jnp.asarray

    def _rec_inputs():
        import jax
        import jax.numpy as jnp
        _rk = jax.random.key(seed)
        x = 7.22e-05 + 1 * jax.random.normal(jax.random.fold_in(_rk, 1), (8, 256, 128), jnp.float32)
        _lenS = 256 - jax.random.randint(jax.random.fold_in(_rk, 7), (8,), 0, max(1, 256 // 4) + 1, jnp.int32)
        _lenS2 = 256 - jax.random.randint(jax.random.fold_in(_rk, 8), (8,), 0, max(1, 256 // 4) + 1, jnp.int32)
        _ctx_1024P = jax.random.normal(jax.random.fold_in(_rk, 11), (8, 16, 128), jnp.float32)
        _ctx_1024c = jax.random.dirichlet(jax.random.fold_in(_rk, 511), 0.3 * jnp.ones((16,), jnp.float32), (8, 256))
        _ctx_1024t = jnp.einsum('bsk,bkd->bsd', _ctx_1024c, _ctx_1024P)
        _ctx_1024t = _ctx_1024t * jax.lax.rsqrt(jnp.mean(jnp.square(_ctx_1024t)) + 1e-12) * 0.953939
        ctx_1024 = 4.13588e-05 + 0.999923 * (_ctx_1024t + 0.3 * jax.random.normal(jax.random.fold_in(_rk, 611), (8, 256, 128), jnp.float32))
        return (x, ctx_1024, _lenS2)
    x, ctx_1024, _lenS2 = _rec_inputs()

    def _L0_attn_setup():
        import jax, jax.numpy as jnp
        import numpy as np
        B, N, C, H = (1, 256, 128, 16)
        key = jax.random.key(seed)
        ks = jax.random.split(key, 8)
        scale = 1.0 / np.sqrt(C)
        d = {'x': jax.random.normal(ks[0], (B, N, C), dtype=jnp.float32)}
        for i, name in enumerate(['q1', 'q2', 'k1', 'k2', 'v', 'out']):
            d[f'W_{name}'] = jax.random.normal(ks[1 + i], (C, C), dtype=jnp.float32) * scale
            d[f'b_{name}'] = jnp.zeros((C,), dtype=jnp.float32)
        d['ln_g'] = jnp.ones((C,), dtype=jnp.float32)
        d['ln_b'] = jnp.zeros((C,), dtype=jnp.float32)
        return d
    _L0_attn_all = _L0_attn_setup()
    _L0_attn_in = {k: v for k, v in _L0_attn_all.items() if k in ('W_q1', 'b_q1', 'W_q2', 'b_q2', 'W_k1', 'b_k1', 'W_k2', 'b_k2', 'W_v', 'b_v', 'W_out', 'b_out', 'ln_g', 'ln_b')}
    del _L0_attn_all

    def _L0_xattn_setup():
        import jax, jax.numpy as jnp
        import numpy as np
        TEMPERATURE = 8.0
        D = 128
        key = jax.random.key(seed)
        ks = jax.random.split(key, 11)
        B, S = (4, 256)
        scale = 1.0 / np.sqrt(D)
        return {'q': jax.random.normal(ks[0], (B, S, D), dtype=jnp.float32), 'k': jax.random.normal(ks[1], (B, S, D), dtype=jnp.float32), 'v': jax.random.normal(ks[2], (B, S, D), dtype=jnp.float32), 'Wq': jax.random.normal(ks[3], (D, D), dtype=jnp.float32) * scale, 'bq': jax.random.normal(ks[4], (D,), dtype=jnp.float32) * 0.02, 'Wk': jax.random.normal(ks[5], (D, D), dtype=jnp.float32) * scale, 'bk': jax.random.normal(ks[6], (D,), dtype=jnp.float32) * 0.02, 'Wv': jax.random.normal(ks[7], (D, D), dtype=jnp.float32) * scale, 'bv': jax.random.normal(ks[8], (D,), dtype=jnp.float32) * 0.02, 'Wf': jax.random.normal(ks[9], (D, D), dtype=jnp.float32) * scale, 'bf': jax.random.normal(ks[10], (D,), dtype=jnp.float32) * 0.02}
    _L0_xattn_all = _L0_xattn_setup()
    _L0_xattn_in = {k: v for k, v in _L0_xattn_all.items() if k in ('Wq', 'bq', 'Wk', 'bk', 'Wv', 'bv', 'Wf', 'bf')}
    del _L0_xattn_all

    def _L0_ffn_setup():
        import jax, jax.numpy as jnp
        import numpy as np
        key = jax.random.key(seed)
        kx, kw = jax.random.split(key)
        x = jax.random.normal(kx, (32, 512, 128), dtype=jnp.float32)
        weight = jax.random.normal(kw, (128, 128), dtype=jnp.float32) * 0.01
        return {'x': x, 'weight': weight}
    _L0_ffn_all = _L0_ffn_setup()
    _L0_ffn_in = {k: v for k, v in _L0_ffn_all.items() if k in ('weight',)}
    del _L0_ffn_all

    def _L1_attn_setup():
        import jax, jax.numpy as jnp
        import numpy as np
        B_, L_ = (2, 256)
        D_MODEL, NHEAD, NLAYER, DFF = (128, 16, 4, 256)
        D_STATE, HEADDIM, D_CONV, CHUNK = (128, 64, 4, 32)
        EXPAND = 2
        D_INNER = EXPAND * D_MODEL
        H_SSM = D_INNER // HEADDIM
        CONV_DIM = D_INNER + 2 * D_STATE
        D_IN_PROJ = 2 * D_INNER + 2 * D_STATE + H_SSM
        HD_ATT = D_MODEL // NHEAD
        ALPHA = 1.68
        EPS = 1e-05

        def rmsnorm(x, w, eps=EPS):
            return x * jax.lax.rsqrt(jnp.mean(x * x, axis=-1, keepdims=True) + eps) * w

        def segsum(x):
            T = x.shape[-1]
            lo = jnp.tril(jnp.ones((T, T), bool), -1)
            s = jnp.cumsum(jnp.where(lo, x[..., :, None], 0.0), axis=-2)
            return jnp.where(jnp.tril(jnp.ones((T, T), bool)), s, -jnp.inf)

        def ssd(x, A, B, C, chunk):
            b, l, h, p = x.shape
            n = B.shape[-1]
            c = l // chunk
            xc = x.reshape(b, c, chunk, h, p)
            Bc = B.reshape(b, c, chunk, h, n)
            Cc = C.reshape(b, c, chunk, h, n)
            Ac = A.reshape(b, c, chunk, h).transpose(0, 3, 1, 2)
            Acs = jnp.cumsum(Ac, axis=-1)
            Lmat = jnp.exp(segsum(Ac))
            Y_diag = jnp.einsum('bclhn,bcshn,bhcls,bcshp->bclhp', Cc, Bc, Lmat, xc)
            decay_states = jnp.exp(Acs[..., -1:] - Acs)
            states = jnp.einsum('bclhn,bhcl,bclhp->bchpn', Bc, decay_states, xc)
            states = jnp.concatenate([jnp.zeros_like(states[:, :1]), states], axis=1)
            Alast = jnp.pad(Acs[..., -1], ((0, 0), (0, 0), (1, 0)))
            decay_chunk = jnp.exp(segsum(Alast))
            new_states = jnp.einsum('bhzc,bchpn->bzhpn', decay_chunk, states)
            states = new_states[:, :-1]
            Y_off = jnp.einsum('bclhn,bchpn,bhcl->bclhp', Cc, states, jnp.exp(Acs))
            return (Y_diag + Y_off).reshape(b, l, h, p)

        def mamba2_block(x, in_w, conv_w, conv_b, dt_bias, A_log, D, norm_w, out_w):
            b, l, _ = x.shape
            zxbcdt = x @ in_w.T
            z = zxbcdt[..., :D_INNER]
            xBC = zxbcdt[..., D_INNER:D_INNER + CONV_DIM]
            dt = zxbcdt[..., D_INNER + CONV_DIM:]
            lhs = jnp.pad(xBC, ((0, 0), (D_CONV - 1, 0), (0, 0))).transpose(0, 2, 1)
            y = jax.lax.conv_general_dilated(lhs, conv_w[:, None, :], (1,), 'VALID', feature_group_count=CONV_DIM)
            xBC = jax.nn.silu(y.transpose(0, 2, 1) + conv_b)
            xs = xBC[..., :D_INNER]
            Bm = xBC[..., D_INNER:D_INNER + D_STATE]
            Cm = xBC[..., D_INNER + D_STATE:]
            dt = jax.nn.softplus(dt + dt_bias)
            A = -jnp.exp(A_log)
            xh = xs.reshape(b, l, H_SSM, HEADDIM)
            Bh = jnp.broadcast_to(Bm[:, :, None, :], (b, l, H_SSM, D_STATE))
            Ch = jnp.broadcast_to(Cm[:, :, None, :], (b, l, H_SSM, D_STATE))
            y = ssd(xh * dt[..., None], A * dt, Bh, Ch, CHUNK)
            y = y + D[None, None, :, None] * xh
            y = y.reshape(b, l, D_INNER)
            y = rmsnorm(y * jax.nn.silu(z), norm_w)
            return y @ out_w.T
        key = jax.random.key(seed)
        ks = jax.random.split(key, 12)

        def n(k, shape, s=0.02):
            return (jax.random.normal(k, shape) * s).astype(jnp.float32)
        return {'x': jax.random.normal(ks[0], (B_, L_, D_MODEL), jnp.float32), 'attn_norm_w': jnp.ones((D_MODEL,), jnp.float32), 'Wqkv_w': n(ks[1], (3 * NHEAD * HD_ATT, D_MODEL)), 'Wqkv_b': jnp.zeros((3 * NHEAD * HD_ATT,), jnp.float32), 'attn_out_w': n(ks[2], (D_MODEL, NHEAD * HD_ATT)), 'attn_out_b': jnp.zeros((D_MODEL,), jnp.float32), 'normf_w': jnp.ones((D_MODEL,), jnp.float32), 'm_in_w': n(ks[3], (NLAYER, D_IN_PROJ, D_MODEL)), 'm_conv_w': n(ks[4], (NLAYER, CONV_DIM, D_CONV), 0.2), 'm_conv_b': jnp.zeros((NLAYER, CONV_DIM), jnp.float32), 'm_dt_bias': jnp.log(jnp.expm1(jax.random.uniform(ks[5], (NLAYER, H_SSM), minval=0.001, maxval=0.1))).astype(jnp.float32), 'm_A_log': jnp.log(jax.random.uniform(ks[6], (NLAYER, H_SSM), minval=1.0, maxval=16.0)).astype(jnp.float32), 'm_D': jnp.ones((NLAYER, H_SSM), jnp.float32), 'm_norm_w': jnp.ones((NLAYER, D_INNER), jnp.float32), 'm_out_w': n(ks[7], (NLAYER, D_MODEL, D_INNER)), 'fc1_w': n(ks[8], (2 * DFF, D_MODEL)), 'fc2_w': n(ks[9], (D_MODEL, DFF)), 'final_norm_w': jnp.ones((D_MODEL,), jnp.float32)}
    _L1_attn_all = _L1_attn_setup()
    _L1_attn_in = {k: v for k, v in _L1_attn_all.items() if k in ('attn_norm_w', 'Wqkv_w', 'Wqkv_b', 'attn_out_w', 'attn_out_b', 'normf_w', 'm_in_w', 'm_conv_w', 'm_conv_b', 'm_dt_bias', 'm_A_log', 'm_D', 'm_norm_w', 'm_out_w', 'fc1_w', 'fc2_w', 'final_norm_w')}
    del _L1_attn_all

    def _L1_xattn_setup():
        import jax, jax.numpy as jnp
        import numpy as np
        HEADS = 16
        key = jax.random.key(seed)
        k1, k2, k3, k4 = jax.random.split(key, 4)
        B, T, S, W = (2, 256, 256, 128)
        x = jax.random.normal(k1, (B, T, W), dtype=jnp.float32)
        cond_k = jax.random.normal(k2, (B, S, W), dtype=jnp.float32)
        cond_v = jax.random.normal(k3, (B, S, W), dtype=jnp.float32)
        w_proj = jax.random.normal(k4, (W, W), dtype=jnp.float32) * 0.02
        b_proj = jnp.zeros((W,), dtype=jnp.float32)
        return {'x': x, 'cond_k': cond_k, 'cond_v': cond_v, 'w_proj': w_proj, 'b_proj': b_proj}
    _L1_xattn_all = _L1_xattn_setup()
    _L1_xattn_in = {k: v for k, v in _L1_xattn_all.items() if k in ('w_proj', 'b_proj')}
    del _L1_xattn_all

    def _L1_ffn_setup():
        import jax, jax.numpy as jnp
        import numpy as np
        from jax import lax
        T, B, I, M, O = (32, 64, 128, 128, 128)

        def _xavier(key, shape):
            fan_out, fan_in = shape
            limit = float(np.sqrt(6.0 / (fan_in + fan_out)))
            return jax.random.uniform(key, shape, jnp.float32, -limit, limit)
        key = jax.random.key(seed)
        ks = jax.random.split(key, 9)
        x = jax.random.normal(ks[0], (T, B, I), jnp.float32)
        return {'x': x, 'wf': _xavier(ks[1], (M, I)), 'uf': _xavier(ks[2], (M, M)), 'bf': jnp.zeros((M,), jnp.float32), 'wi': _xavier(ks[3], (M, I)), 'ui': _xavier(ks[4], (M, M)), 'bi': jnp.zeros((M,), jnp.float32), 'wc': _xavier(ks[5], (M, I)), 'uc': _xavier(ks[6], (M, M)), 'bc': jnp.zeros((M,), jnp.float32), 'wo': _xavier(ks[7], (O, I)), 'uo': _xavier(ks[8], (O, M)), 'bo': jnp.zeros((O,), jnp.float32), 'in_c': jnp.zeros((M,), jnp.float32)}
    _L1_ffn_all = _L1_ffn_setup()
    _L1_ffn_in = {k: v for k, v in _L1_ffn_all.items() if k in ('wf', 'uf', 'bf', 'wi', 'ui', 'bi', 'wc', 'uc', 'bc', 'wo', 'uo', 'bo', 'in_c')}
    del _L1_ffn_all

    def _L2_attn_setup():
        import jax, jax.numpy as jnp
        import numpy as np
        B, T, C = (8, 256, 128)
        EPS_LN = 1e-05
        EPS_WKV = 1e-08

        def layer_norm(x, g, b):
            mu = jnp.mean(x, axis=-1, keepdims=True)
            var = jnp.var(x, axis=-1, keepdims=True)
            return (x - mu) * jax.lax.rsqrt(var + EPS_LN) * g + b

        def time_shift(x, ratio):
            x_prev = jnp.pad(x[:, :-1, :], ((0, 0), (1, 0), (0, 0)))
            return x * ratio + x_prev * (1.0 - ratio)

        def wkv(w, u, k, v):
            kT = jnp.swapaxes(k, 0, 1)
            vT = jnp.swapaxes(v, 0, 1)
            aa0 = jnp.zeros((k.shape[0], k.shape[2]), k.dtype)
            ninf = jnp.full_like(aa0, -jnp.inf)

            def step(carry, kv):
                aa, bb, pp = carry
                kk, vv = kv
                ww = u + kk
                p = jnp.maximum(pp, ww)
                e1 = jnp.exp(pp - p)
                e2 = jnp.exp(ww - p)
                out = (e1 * aa + e2 * vv) / (e1 + e2 + EPS_WKV)
                bb_new = w + pp
                p2 = jnp.maximum(pp, kk)
                e1b = jnp.exp(pp - p2)
                e2b = jnp.exp(kk - p2)
                aa_new = e1b * aa + e2b * vv
                pp_new = p2 + jnp.log(e1b + e2b + EPS_WKV)
                return ((aa_new, bb_new, pp_new), out)
            (aa, bb, pp), outT = jax.lax.scan(step, (aa0, ninf, ninf), (kT, vT))
            output = jnp.swapaxes(outT, 0, 1)
            final_state = jnp.stack([aa, bb, pp], axis=2)
            return (output, final_state)

        def _reference_tuple_inner(x, time_decay, time_first, Wk_t, Wv_t, Wr_t, Wk_c, Wv_c, Wr_c, ln1_g, ln1_b, ln2_g, ln2_b, mix_k, mix_v, mix_r, cmix_k, cmix_r):
            h = layer_norm(x, ln1_g, ln1_b)
            k = time_shift(h, mix_k) @ Wk_t.T
            v = time_shift(h, mix_v) @ Wv_t.T
            r = jax.nn.sigmoid(time_shift(h, mix_r) @ Wr_t.T)
            w = -jnp.exp(time_decay)
            wkv_out, new_state = wkv(w, time_first, k, v)
            x = x + r * wkv_out
            h2 = layer_norm(x, ln2_g, ln2_b)
            kc = time_shift(h2, cmix_k) @ Wk_c.T
            rc = jax.nn.sigmoid(time_shift(h2, cmix_r) @ Wr_c.T)
            vv = jnp.square(jax.nn.relu(kc)) @ Wv_c.T
            x = x + rc * vv
            return (x, new_state)
        key = jax.random.key(seed)
        ks = jax.random.split(key, 16)
        s = 1.0 / np.sqrt(C)
        inp = {'x': jax.random.normal(ks[0], (B, T, C), jnp.float32), 'time_decay': jax.random.normal(ks[1], (C,), jnp.float32), 'time_first': jax.random.normal(ks[2], (C,), jnp.float32), 'Wk_t': jax.random.normal(ks[3], (C, C), jnp.float32) * s, 'Wv_t': jax.random.normal(ks[4], (C, C), jnp.float32) * s, 'Wr_t': jax.random.normal(ks[5], (C, C), jnp.float32) * s, 'Wk_c': jax.random.normal(ks[6], (4 * C, C), jnp.float32) * s, 'Wv_c': jax.random.normal(ks[7], (C, 4 * C), jnp.float32) * (0.5 * s), 'Wr_c': jax.random.normal(ks[8], (C, C), jnp.float32) * s, 'ln1_g': jnp.ones((C,), jnp.float32), 'ln1_b': jnp.zeros((C,), jnp.float32), 'ln2_g': jnp.ones((C,), jnp.float32), 'ln2_b': jnp.zeros((C,), jnp.float32), 'mix_k': jnp.ones((C,), jnp.float32), 'mix_v': jnp.ones((C,), jnp.float32), 'mix_r': jnp.ones((C,), jnp.float32), 'cmix_k': jnp.ones((C,), jnp.float32), 'cmix_r': jnp.ones((C,), jnp.float32)}
        return inp
    _L2_attn_all = _L2_attn_setup()
    _L2_attn_in = {k: v for k, v in _L2_attn_all.items() if k in ('time_decay', 'time_first', 'Wk_t', 'Wv_t', 'Wr_t', 'Wk_c', 'Wv_c', 'Wr_c', 'ln1_g', 'ln1_b', 'ln2_g', 'ln2_b', 'mix_k', 'mix_v', 'mix_r', 'cmix_k', 'cmix_r')}
    del _L2_attn_all

    def _L2_xattn_setup():
        import jax, jax.numpy as jnp
        import numpy as np
        DIM, HEADS, HEAD_DIM = (128, 16, 64)
        B, L, S = (4, 256, 256)
        EPS = 1e-05
        NEG_INF = -1000000000.0

        def rms_norm(x, w):
            var = jnp.mean(jnp.square(x), axis=-1, keepdims=True)
            return x * jax.lax.rsqrt(var + EPS) * w
        key = jax.random.key(seed)
        ks = jax.random.split(key, 9)
        hd = HEADS * HEAD_DIM
        scale = 1.0 / np.sqrt(DIM)
        return {'q': jax.random.normal(ks[0], (B, L, DIM), dtype=jnp.float32), 'kv': jax.random.normal(ks[1], (B, S, DIM), dtype=jnp.float32), 'x_seqlens': jax.random.randint(ks[2], (B,), 1, S + 1, dtype=jnp.int32), 'Wq': jax.random.normal(ks[3], (DIM, hd), dtype=jnp.float32) * scale, 'Wk': jax.random.normal(ks[4], (DIM, hd), dtype=jnp.float32) * scale, 'Wv': jax.random.normal(ks[5], (DIM, hd), dtype=jnp.float32) * scale, 'Wo': jax.random.normal(ks[6], (hd, DIM), dtype=jnp.float32) * (1.0 / np.sqrt(hd)), 'q_norm_w': jnp.ones((HEAD_DIM,), dtype=jnp.float32), 'k_norm_w': jnp.ones((HEAD_DIM,), dtype=jnp.float32)}
    _L2_xattn_all = _L2_xattn_setup()
    _L2_xattn_in = {k: v for k, v in _L2_xattn_all.items() if k in ('Wq', 'Wk', 'Wv', 'Wo', 'q_norm_w', 'k_norm_w')}
    del _L2_xattn_all

    def _L2_ffn_setup():
        import jax, jax.numpy as jnp
        import numpy as np
        B, S, D = (4, 512, 128)
        E, K, H = (8, 2, 256)
        key = jax.random.key(seed)
        ks = jax.random.split(key, 6)
        scale_g = 1.0 / np.sqrt(D)
        scale_1 = 1.0 / np.sqrt(D)
        scale_2 = 1.0 / np.sqrt(H)
        return {'x': jax.random.normal(ks[0], (B, S, D), dtype=jnp.float32), 'Wg': jax.random.uniform(ks[1], (D, E), jnp.float32, -scale_g, scale_g), 'W1': jax.random.uniform(ks[2], (E, D, H), jnp.float32, -scale_1, scale_1), 'b1': jax.random.uniform(ks[3], (E, H), jnp.float32, -scale_1, scale_1), 'W2': jax.random.uniform(ks[4], (E, H, D), jnp.float32, -scale_2, scale_2), 'b2': jax.random.uniform(ks[5], (E, D), jnp.float32, -scale_2, scale_2)}
    _L2_ffn_all = _L2_ffn_setup()
    _L2_ffn_in = {k: v for k, v in _L2_ffn_all.items() if k in ('Wg', 'W1', 'b1', 'W2', 'b2')}
    del _L2_ffn_all

    def _L3_attn_setup():
        import jax, jax.numpy as jnp
        import numpy as np
        import math
        B, N, D, H, G = (4, 256, 128, 16, 256)
        HD = D // H
        MAX_SEQ = 256
        STRIDE = (G - 1) / max(MAX_SEQ - 1, 1)

        def _forward(x, Wqkvg, bqkvg, wave_frequency, wave_damping, wave_phase, field_coupling, Wout, bout):
            b, n, d = x.shape
            qkvg = x @ Wqkvg.T + bqkvg
            q, k, v, gate_raw = jnp.split(qkvg, 4, axis=-1)
            to_heads = lambda t: t.reshape(b, n, H, HD).transpose(0, 2, 1, 3)
            q, k, v = (to_heads(q), to_heads(k), to_heads(v))
            seq_pos = jnp.arange(n, dtype=jnp.float32)
            field_pos = jnp.clip(seq_pos * STRIDE, 0.0, G - 2)
            idx_lo = jnp.clip(field_pos.astype(jnp.int32), 0, G - 2)
            idx_hi = idx_lo + 1
            frac = jnp.clip(field_pos - idx_lo.astype(jnp.float32), 0.0, 1.0)
            w_lo = (1.0 - frac)[None, None, :, None]
            w_hi = frac[None, None, :, None]
            q_feat = jax.nn.elu(q) + 1.0
            k_feat = jax.nn.elu(k) + 1.0
            deposit = k_feat * v
            field = jnp.zeros((b, H, G, HD), deposit.dtype)
            field = field.at[:, :, idx_lo, :].add(deposit * w_lo)
            field = field.at[:, :, idx_hi, :].add(deposit * w_hi)
            t = jnp.arange(G, dtype=jnp.float32)
            alpha = jax.nn.softplus(wave_damping)[:, None]
            omega = wave_frequency[:, None]
            phi = wave_phase[:, None]
            kernels = jnp.exp(-alpha * t[None, :]) * jnp.cos(omega * t[None, :] + phi)
            kernels = kernels / jnp.clip(jnp.sum(jnp.abs(kernels), axis=1, keepdims=True), 1e-08)
            kernel_fft = jnp.fft.rfft(kernels, n=2 * G, axis=-1)
            field_fft = jnp.fft.rfft(field, n=2 * G, axis=2)
            convolved = jnp.fft.irfft(field_fft * kernel_fft[None, :, :, None], n=2 * G, axis=2)[:, :, :G, :]
            coupling = jax.nn.softmax(field_coupling, axis=-1)
            field_c = jnp.einsum('ij,bjgd->bigd', coupling, convolved)
            gathered = field_c[:, :, idx_lo, :] * w_lo + field_c[:, :, idx_hi, :] * w_hi
            wave_output = q_feat * gathered
            gate = jax.nn.sigmoid(gate_raw).reshape(b, n, H, HD).transpose(0, 2, 1, 3)
            output = (wave_output * gate).transpose(0, 2, 1, 3).reshape(b, n, d)
            return output @ Wout.T + bout
        key = jax.random.key(seed)
        ks = jax.random.split(key, 5)
        x = jax.random.normal(ks[0], (B, N, D), jnp.float32)
        Wqkvg = jax.random.normal(ks[1], (4 * D, D), jnp.float32) * 0.02
        Wqkvg = Wqkvg.at[3 * D:].set(0.0)
        bqkvg = jnp.concatenate([jnp.zeros(3 * D, jnp.float32), jnp.full((D,), 2.0, jnp.float32)])
        wave_frequency = jnp.linspace(0.3, 4.0, H, dtype=jnp.float32)
        wave_damping = jnp.linspace(-3.0, 0.5, H, dtype=jnp.float32)
        wave_phase = jnp.linspace(0.0, math.pi, H, dtype=jnp.float32)
        field_coupling = jnp.eye(H, dtype=jnp.float32) + jax.random.normal(ks[2], (H, H), jnp.float32) * 0.01
        Wout = jax.random.normal(ks[3], (D, D), jnp.float32) * 0.02
        bout = jnp.zeros(D, jnp.float32)
        return dict(x=x, Wqkvg=Wqkvg, bqkvg=bqkvg, wave_frequency=wave_frequency, wave_damping=wave_damping, wave_phase=wave_phase, field_coupling=field_coupling, Wout=Wout, bout=bout)
    _L3_attn_all = _L3_attn_setup()
    _L3_attn_in = {k: v for k, v in _L3_attn_all.items() if k in ('Wqkvg', 'bqkvg', 'wave_frequency', 'wave_damping', 'wave_phase', 'field_coupling', 'Wout', 'bout')}
    del _L3_attn_all

    def _L3_xattn_setup():
        import jax, jax.numpy as jnp
        import numpy as np
        EMBED_DIM = 128
        NUM_HEADS = 16
        HEAD_DIM = EMBED_DIM // NUM_HEADS
        B, T_Q, T_K = (2, 256, 256)
        key = jax.random.key(seed)
        ks = jax.random.split(key, 11)
        s = 1.0 / np.sqrt(EMBED_DIM)
        return {'query': jax.random.normal(ks[0], (B, T_Q, EMBED_DIM), jnp.float32), 'key': jax.random.normal(ks[1], (B, T_K, EMBED_DIM), jnp.float32), 'value': jax.random.normal(ks[2], (B, T_K, EMBED_DIM), jnp.float32), 'Wq': jax.random.normal(ks[3], (EMBED_DIM, EMBED_DIM), jnp.float32) * s, 'bq': jnp.zeros((EMBED_DIM,), jnp.float32), 'Wk': jax.random.normal(ks[4], (EMBED_DIM, EMBED_DIM), jnp.float32) * s, 'bk': jnp.zeros((EMBED_DIM,), jnp.float32), 'Wv': jax.random.normal(ks[5], (EMBED_DIM, EMBED_DIM), jnp.float32) * s, 'bv': jnp.zeros((EMBED_DIM,), jnp.float32), 'Wo': jax.random.normal(ks[6], (EMBED_DIM, EMBED_DIM), jnp.float32) * s, 'bo': jnp.zeros((EMBED_DIM,), jnp.float32)}
    _L3_xattn_all = _L3_xattn_setup()
    _L3_xattn_in = {k: v for k, v in _L3_xattn_all.items() if k in ('Wq', 'bq', 'Wk', 'bk', 'Wv', 'bv', 'Wo', 'bo')}
    del _L3_xattn_all

    def _L3_ffn_setup():
        import jax, jax.numpy as jnp
        import numpy as np
        B, S = (4, 256)
        D_MODEL, D_FF, N_EXPERTS, TOP_K = (128, 512, 8, 2)
        T = B * S
        CAPACITY_FACTOR, MIN_CAP = (1.25, 4)
        CAP = max(int(CAPACITY_FACTOR * (T * TOP_K / N_EXPERTS)), MIN_CAP)
        key = jax.random.key(seed)
        ks = jax.random.split(key, 6)

        def w(k, shape, fan):
            return jax.random.normal(k, shape, jnp.float32) * fan ** (-0.5)
        return {'x': jax.random.normal(ks[0], (B, S, D_MODEL), jnp.float32), 'Wr': w(ks[1], (D_MODEL, N_EXPERTS), D_MODEL), 'W1': w(ks[2], (N_EXPERTS, D_MODEL, D_FF), D_MODEL), 'b1': jnp.zeros((N_EXPERTS, D_FF), jnp.float32), 'W2': w(ks[3], (N_EXPERTS, D_FF, D_MODEL), D_FF), 'b2': jnp.zeros((N_EXPERTS, D_MODEL), jnp.float32), 'fw1': w(ks[4], (D_MODEL, D_FF), D_MODEL), 'fb1': jnp.zeros((D_FF,), jnp.float32), 'fw2': w(ks[5], (D_FF, D_MODEL), D_FF), 'fb2': jnp.zeros((D_MODEL,), jnp.float32)}
    _L3_ffn_all = _L3_ffn_setup()
    _L3_ffn_in = {k: v for k, v in _L3_ffn_all.items() if k in ('Wr', 'W1', 'b1', 'W2', 'b2', 'fw1', 'fb1', 'fw2', 'fb2')}
    del _L3_ffn_all
    return {'x': x, 'ctx_1024': ctx_1024, '_lenS2': _lenS2, 'L0_attn_W_q1': _L0_attn_in['W_q1'], 'L0_attn_b_q1': _L0_attn_in['b_q1'], 'L0_attn_W_q2': _L0_attn_in['W_q2'], 'L0_attn_b_q2': _L0_attn_in['b_q2'], 'L0_attn_W_k1': _L0_attn_in['W_k1'], 'L0_attn_b_k1': _L0_attn_in['b_k1'], 'L0_attn_W_k2': _L0_attn_in['W_k2'], 'L0_attn_b_k2': _L0_attn_in['b_k2'], 'L0_attn_W_v': _L0_attn_in['W_v'], 'L0_attn_b_v': _L0_attn_in['b_v'], 'L0_attn_W_out': _L0_attn_in['W_out'], 'L0_attn_b_out': _L0_attn_in['b_out'], 'L0_attn_ln_g': _L0_attn_in['ln_g'], 'L0_attn_ln_b': _L0_attn_in['ln_b'], 'L0_xattn_Wq': _L0_xattn_in['Wq'], 'L0_xattn_bq': _L0_xattn_in['bq'], 'L0_xattn_Wk': _L0_xattn_in['Wk'], 'L0_xattn_bk': _L0_xattn_in['bk'], 'L0_xattn_Wv': _L0_xattn_in['Wv'], 'L0_xattn_bv': _L0_xattn_in['bv'], 'L0_xattn_Wf': _L0_xattn_in['Wf'], 'L0_xattn_bf': _L0_xattn_in['bf'], 'L0_ffn_weight': _L0_ffn_in['weight'], 'L1_attn_attn_norm_w': _L1_attn_in['attn_norm_w'], 'L1_attn_Wqkv_w': _L1_attn_in['Wqkv_w'], 'L1_attn_Wqkv_b': _L1_attn_in['Wqkv_b'], 'L1_attn_attn_out_w': _L1_attn_in['attn_out_w'], 'L1_attn_attn_out_b': _L1_attn_in['attn_out_b'], 'L1_attn_normf_w': _L1_attn_in['normf_w'], 'L1_attn_m_in_w': _L1_attn_in['m_in_w'], 'L1_attn_m_conv_w': _L1_attn_in['m_conv_w'], 'L1_attn_m_conv_b': _L1_attn_in['m_conv_b'], 'L1_attn_m_dt_bias': _L1_attn_in['m_dt_bias'], 'L1_attn_m_A_log': _L1_attn_in['m_A_log'], 'L1_attn_m_D': _L1_attn_in['m_D'], 'L1_attn_m_norm_w': _L1_attn_in['m_norm_w'], 'L1_attn_m_out_w': _L1_attn_in['m_out_w'], 'L1_attn_fc1_w': _L1_attn_in['fc1_w'], 'L1_attn_fc2_w': _L1_attn_in['fc2_w'], 'L1_attn_final_norm_w': _L1_attn_in['final_norm_w'], 'L1_xattn_w_proj': _L1_xattn_in['w_proj'], 'L1_xattn_b_proj': _L1_xattn_in['b_proj'], 'L1_ffn_wf': _L1_ffn_in['wf'], 'L1_ffn_uf': _L1_ffn_in['uf'], 'L1_ffn_bf': _L1_ffn_in['bf'], 'L1_ffn_wi': _L1_ffn_in['wi'], 'L1_ffn_ui': _L1_ffn_in['ui'], 'L1_ffn_bi': _L1_ffn_in['bi'], 'L1_ffn_wc': _L1_ffn_in['wc'], 'L1_ffn_uc': _L1_ffn_in['uc'], 'L1_ffn_bc': _L1_ffn_in['bc'], 'L1_ffn_wo': _L1_ffn_in['wo'], 'L1_ffn_uo': _L1_ffn_in['uo'], 'L1_ffn_bo': _L1_ffn_in['bo'], 'L1_ffn_in_c': _L1_ffn_in['in_c'], 'L2_attn_time_decay': _L2_attn_in['time_decay'], 'L2_attn_time_first': _L2_attn_in['time_first'], 'L2_attn_Wk_t': _L2_attn_in['Wk_t'], 'L2_attn_Wv_t': _L2_attn_in['Wv_t'], 'L2_attn_Wr_t': _L2_attn_in['Wr_t'], 'L2_attn_Wk_c': _L2_attn_in['Wk_c'], 'L2_attn_Wv_c': _L2_attn_in['Wv_c'], 'L2_attn_Wr_c': _L2_attn_in['Wr_c'], 'L2_attn_ln1_g': _L2_attn_in['ln1_g'], 'L2_attn_ln1_b': _L2_attn_in['ln1_b'], 'L2_attn_ln2_g': _L2_attn_in['ln2_g'], 'L2_attn_ln2_b': _L2_attn_in['ln2_b'], 'L2_attn_mix_k': _L2_attn_in['mix_k'], 'L2_attn_mix_v': _L2_attn_in['mix_v'], 'L2_attn_mix_r': _L2_attn_in['mix_r'], 'L2_attn_cmix_k': _L2_attn_in['cmix_k'], 'L2_attn_cmix_r': _L2_attn_in['cmix_r'], 'L2_xattn_Wq': _L2_xattn_in['Wq'], 'L2_xattn_Wk': _L2_xattn_in['Wk'], 'L2_xattn_Wv': _L2_xattn_in['Wv'], 'L2_xattn_Wo': _L2_xattn_in['Wo'], 'L2_xattn_q_norm_w': _L2_xattn_in['q_norm_w'], 'L2_xattn_k_norm_w': _L2_xattn_in['k_norm_w'], 'L2_ffn_Wg': _L2_ffn_in['Wg'], 'L2_ffn_W1': _L2_ffn_in['W1'], 'L2_ffn_b1': _L2_ffn_in['b1'], 'L2_ffn_W2': _L2_ffn_in['W2'], 'L2_ffn_b2': _L2_ffn_in['b2'], 'L3_attn_Wqkvg': _L3_attn_in['Wqkvg'], 'L3_attn_bqkvg': _L3_attn_in['bqkvg'], 'L3_attn_wave_frequency': _L3_attn_in['wave_frequency'], 'L3_attn_wave_damping': _L3_attn_in['wave_damping'], 'L3_attn_wave_phase': _L3_attn_in['wave_phase'], 'L3_attn_field_coupling': _L3_attn_in['field_coupling'], 'L3_attn_Wout': _L3_attn_in['Wout'], 'L3_attn_bout': _L3_attn_in['bout'], 'L3_xattn_Wq': _L3_xattn_in['Wq'], 'L3_xattn_bq': _L3_xattn_in['bq'], 'L3_xattn_Wk': _L3_xattn_in['Wk'], 'L3_xattn_bk': _L3_xattn_in['bk'], 'L3_xattn_Wv': _L3_xattn_in['Wv'], 'L3_xattn_bv': _L3_xattn_in['bv'], 'L3_xattn_Wo': _L3_xattn_in['Wo'], 'L3_xattn_bo': _L3_xattn_in['bo'], 'L3_ffn_Wr': _L3_ffn_in['Wr'], 'L3_ffn_W1': _L3_ffn_in['W1'], 'L3_ffn_b1': _L3_ffn_in['b1'], 'L3_ffn_W2': _L3_ffn_in['W2'], 'L3_ffn_b2': _L3_ffn_in['b2'], 'L3_ffn_fw1': _L3_ffn_in['fw1'], 'L3_ffn_fb1': _L3_ffn_in['fb1'], 'L3_ffn_fw2': _L3_ffn_in['fw2'], 'L3_ffn_fb2': _L3_ffn_in['fb2']}

def reference(x, ctx_1024, _lenS2, L0_attn_W_q1, L0_attn_b_q1, L0_attn_W_q2, L0_attn_b_q2, L0_attn_W_k1, L0_attn_b_k1, L0_attn_W_k2, L0_attn_b_k2, L0_attn_W_v, L0_attn_b_v, L0_attn_W_out, L0_attn_b_out, L0_attn_ln_g, L0_attn_ln_b, L0_xattn_Wq, L0_xattn_bq, L0_xattn_Wk, L0_xattn_bk, L0_xattn_Wv, L0_xattn_bv, L0_xattn_Wf, L0_xattn_bf, L0_ffn_weight, L1_attn_attn_norm_w, L1_attn_Wqkv_w, L1_attn_Wqkv_b, L1_attn_attn_out_w, L1_attn_attn_out_b, L1_attn_normf_w, L1_attn_m_in_w, L1_attn_m_conv_w, L1_attn_m_conv_b, L1_attn_m_dt_bias, L1_attn_m_A_log, L1_attn_m_D, L1_attn_m_norm_w, L1_attn_m_out_w, L1_attn_fc1_w, L1_attn_fc2_w, L1_attn_final_norm_w, L1_xattn_w_proj, L1_xattn_b_proj, L1_ffn_wf, L1_ffn_uf, L1_ffn_bf, L1_ffn_wi, L1_ffn_ui, L1_ffn_bi, L1_ffn_wc, L1_ffn_uc, L1_ffn_bc, L1_ffn_wo, L1_ffn_uo, L1_ffn_bo, L1_ffn_in_c, L2_attn_time_decay, L2_attn_time_first, L2_attn_Wk_t, L2_attn_Wv_t, L2_attn_Wr_t, L2_attn_Wk_c, L2_attn_Wv_c, L2_attn_Wr_c, L2_attn_ln1_g, L2_attn_ln1_b, L2_attn_ln2_g, L2_attn_ln2_b, L2_attn_mix_k, L2_attn_mix_v, L2_attn_mix_r, L2_attn_cmix_k, L2_attn_cmix_r, L2_xattn_Wq, L2_xattn_Wk, L2_xattn_Wv, L2_xattn_Wo, L2_xattn_q_norm_w, L2_xattn_k_norm_w, L2_ffn_Wg, L2_ffn_W1, L2_ffn_b1, L2_ffn_W2, L2_ffn_b2, L3_attn_Wqkvg, L3_attn_bqkvg, L3_attn_wave_frequency, L3_attn_wave_damping, L3_attn_wave_phase, L3_attn_field_coupling, L3_attn_Wout, L3_attn_bout, L3_xattn_Wq, L3_xattn_bq, L3_xattn_Wk, L3_xattn_bk, L3_xattn_Wv, L3_xattn_bv, L3_xattn_Wo, L3_xattn_bo, L3_ffn_Wr, L3_ffn_W1, L3_ffn_b1, L3_ffn_W2, L3_ffn_b2, L3_ffn_fw1, L3_ffn_fb1, L3_ffn_fw2, L3_ffn_fb2):
    import jax
    import jax.numpy as jnp

    def _L0_attn_ref(x, W_q1, b_q1, W_q2, b_q2, W_k1, b_k1, W_k2, b_k2, W_v, b_v, W_out, b_out, ln_g, ln_b):
        import jax, jax.numpy as jnp
        import numpy as np
        B, N, C, H = (1, 256, 128, 16)
        Bx, Nx, Cx = x.shape
        hd = Cx // H

        def proj(W, b):
            return x + x @ W + b

        def split_heads(z):
            return z.reshape(Bx, Nx, H, hd).transpose(0, 2, 1, 3)
        q1 = split_heads(proj(W_q1, b_q1))
        q2 = split_heads(proj(W_q2, b_q2))
        k1 = split_heads(proj(W_k1, b_k1))
        k2 = split_heads(proj(W_k2, b_k2))
        v = split_heads(proj(W_v, b_v))
        s = jnp.einsum('bhnd,bhmd->bhnm', q1, k1) * jnp.einsum('bhnd,bhmd->bhnm', q2, k2)
        p = jax.nn.softmax(s, axis=-1)
        o = jnp.einsum('bhnm,bhmd->bhnd', p, v)
        o = o.transpose(0, 2, 1, 3).reshape(Bx, Nx, Cx)
        mu = o.mean(axis=-1, keepdims=True)
        var = ((o - mu) ** 2).mean(axis=-1, keepdims=True)
        o = (o - mu) / jnp.sqrt(var + 1e-05) * ln_g + ln_b
        return o @ W_out + b_out

    def _L0_xattn_ref(q, k, v, Wq, bq, Wk, bk, Wv, bv, Wf, bf):
        import jax, jax.numpy as jnp
        import numpy as np
        TEMPERATURE = 8.0
        D = 128
        residual = v
        qp = jnp.einsum('bsd,ed->bse', q, Wq) + bq
        kp = jnp.einsum('bsd,ed->bse', k, Wk) + bk
        vp = jnp.einsum('bsd,ed->bse', v, Wv) + bv
        attn = jnp.einsum('bqd,bkd->bqk', qp / TEMPERATURE, kp)
        attn = jax.nn.softmax(attn, axis=-1)
        context = jnp.einsum('bqk,bkd->bqd', attn, vp)
        context = jax.nn.gelu(jnp.einsum('bsd,ed->bse', context, Wf) + bf, approximate=False)
        return context + residual

    def _L0_ffn_ref(x, weight):
        import jax, jax.numpy as jnp
        import numpy as np
        b_weight = jnp.sign(weight)
        return jnp.einsum('bsi,oi->bso', x, b_weight)

    def _L1_attn_ref(x, attn_norm_w, Wqkv_w, Wqkv_b, attn_out_w, attn_out_b, normf_w, m_in_w, m_conv_w, m_conv_b, m_dt_bias, m_A_log, m_D, m_norm_w, m_out_w, fc1_w, fc2_w, final_norm_w):
        import jax, jax.numpy as jnp
        import numpy as np
        B_, L_ = (2, 256)
        D_MODEL, NHEAD, NLAYER, DFF = (128, 16, 4, 256)
        D_STATE, HEADDIM, D_CONV, CHUNK = (128, 64, 4, 32)
        EXPAND = 2
        D_INNER = EXPAND * D_MODEL
        H_SSM = D_INNER // HEADDIM
        CONV_DIM = D_INNER + 2 * D_STATE
        D_IN_PROJ = 2 * D_INNER + 2 * D_STATE + H_SSM
        HD_ATT = D_MODEL // NHEAD
        ALPHA = 1.68
        EPS = 1e-05

        def rmsnorm(x, w, eps=EPS):
            return x * jax.lax.rsqrt(jnp.mean(x * x, axis=-1, keepdims=True) + eps) * w

        def segsum(x):
            T = x.shape[-1]
            lo = jnp.tril(jnp.ones((T, T), bool), -1)
            s = jnp.cumsum(jnp.where(lo, x[..., :, None], 0.0), axis=-2)
            return jnp.where(jnp.tril(jnp.ones((T, T), bool)), s, -jnp.inf)

        def ssd(x, A, B, C, chunk):
            b, l, h, p = x.shape
            n = B.shape[-1]
            c = l // chunk
            xc = x.reshape(b, c, chunk, h, p)
            Bc = B.reshape(b, c, chunk, h, n)
            Cc = C.reshape(b, c, chunk, h, n)
            Ac = A.reshape(b, c, chunk, h).transpose(0, 3, 1, 2)
            Acs = jnp.cumsum(Ac, axis=-1)
            Lmat = jnp.exp(segsum(Ac))
            Y_diag = jnp.einsum('bclhn,bcshn,bhcls,bcshp->bclhp', Cc, Bc, Lmat, xc)
            decay_states = jnp.exp(Acs[..., -1:] - Acs)
            states = jnp.einsum('bclhn,bhcl,bclhp->bchpn', Bc, decay_states, xc)
            states = jnp.concatenate([jnp.zeros_like(states[:, :1]), states], axis=1)
            Alast = jnp.pad(Acs[..., -1], ((0, 0), (0, 0), (1, 0)))
            decay_chunk = jnp.exp(segsum(Alast))
            new_states = jnp.einsum('bhzc,bchpn->bzhpn', decay_chunk, states)
            states = new_states[:, :-1]
            Y_off = jnp.einsum('bclhn,bchpn,bhcl->bclhp', Cc, states, jnp.exp(Acs))
            return (Y_diag + Y_off).reshape(b, l, h, p)

        def mamba2_block(x, in_w, conv_w, conv_b, dt_bias, A_log, D, norm_w, out_w):
            b, l, _ = x.shape
            zxbcdt = x @ in_w.T
            z = zxbcdt[..., :D_INNER]
            xBC = zxbcdt[..., D_INNER:D_INNER + CONV_DIM]
            dt = zxbcdt[..., D_INNER + CONV_DIM:]
            lhs = jnp.pad(xBC, ((0, 0), (D_CONV - 1, 0), (0, 0))).transpose(0, 2, 1)
            y = jax.lax.conv_general_dilated(lhs, conv_w[:, None, :], (1,), 'VALID', feature_group_count=CONV_DIM)
            xBC = jax.nn.silu(y.transpose(0, 2, 1) + conv_b)
            xs = xBC[..., :D_INNER]
            Bm = xBC[..., D_INNER:D_INNER + D_STATE]
            Cm = xBC[..., D_INNER + D_STATE:]
            dt = jax.nn.softplus(dt + dt_bias)
            A = -jnp.exp(A_log)
            xh = xs.reshape(b, l, H_SSM, HEADDIM)
            Bh = jnp.broadcast_to(Bm[:, :, None, :], (b, l, H_SSM, D_STATE))
            Ch = jnp.broadcast_to(Cm[:, :, None, :], (b, l, H_SSM, D_STATE))
            y = ssd(xh * dt[..., None], A * dt, Bh, Ch, CHUNK)
            y = y + D[None, None, :, None] * xh
            y = y.reshape(b, l, D_INNER)
            y = rmsnorm(y * jax.nn.silu(z), norm_w)
            return y @ out_w.T
        b, l, _ = x.shape
        h = rmsnorm(x, attn_norm_w)
        qkv = (h @ Wqkv_w.T + Wqkv_b).reshape(b, l, 3, NHEAD, HD_ATT)
        q, k, v = (qkv[:, :, 0], qkv[:, :, 1], qkv[:, :, 2])
        scores = jnp.einsum('blhd,bshd->bhls', q, k) / np.float32(np.sqrt(HD_ATT))
        probs = jax.nn.softmax(scores, axis=-1)
        o = jnp.einsum('bhls,bshd->blhd', probs, v).reshape(b, l, D_MODEL)
        o = o @ attn_out_w.T + attn_out_b
        x = rmsnorm(o + x, normf_w)
        for i in range(NLAYER):
            x = mamba2_block(x, m_in_w[i], m_conv_w[i], m_conv_b[i], m_dt_bias[i], m_A_log[i], m_D[i], m_norm_w[i], m_out_w[i])
        y = x @ fc1_w.T
        y1, gate = jnp.split(y, 2, axis=-1)
        ff = y1 * jax.nn.silu(gate) @ fc2_w.T
        return rmsnorm(ff + ALPHA * x, final_norm_w)

    def _L1_xattn_ref(x, cond_k, cond_v, w_proj, b_proj):
        import jax, jax.numpy as jnp
        import numpy as np
        HEADS = 16
        B, T, W = x.shape
        S = cond_k.shape[1]
        H = HEADS
        d = W // H
        scale = 1.0 / jnp.sqrt(jnp.sqrt(jnp.float32(d)))
        q = x.reshape(B, T, H, d) * scale
        k = cond_k.reshape(B, S, H, d) * scale
        v = cond_v.reshape(B, S, H, d)
        scores = jnp.einsum('bthd,bshd->bhts', q, k)
        w = jax.nn.softmax(scores.astype(jnp.float32), axis=-1).astype(scores.dtype)
        out = jnp.einsum('bhts,bshd->bthd', w, v).reshape(B, T, W)
        return out @ w_proj.T + b_proj

    def _L1_ffn_ref(x, wf, uf, bf, wi, ui, bi, wc, uc, bc, wo, uo, bo, in_c):
        import jax, jax.numpy as jnp
        import numpy as np
        from jax import lax
        T, B, I, M, O = (32, 64, 128, 128, 128)

        def _xavier(key, shape):
            fan_out, fan_in = shape
            limit = float(np.sqrt(6.0 / (fan_in + fan_out)))
            return jax.random.uniform(key, shape, jnp.float32, -limit, limit)
        batch = x.shape[1]
        c0 = jnp.broadcast_to(in_c, (batch, in_c.shape[0]))

        def step(c, xt):
            ft = jax.nn.sigmoid(xt @ wf.T + c @ uf.T + bf)
            it = jax.nn.sigmoid(xt @ wi.T + c @ ui.T + bi)
            gt = jnp.tanh(xt @ wc.T + c @ uc.T + bc)
            c = ft * c + it * gt
            return (c, None)
        c_final, _ = lax.scan(step, c0, x)
        h = jnp.tanh(jnp.einsum('tbi,oi->tbo', x, wo) + c_final @ uo.T + bo)
        return h

    def _L2_attn_ref(x, time_decay, time_first, Wk_t, Wv_t, Wr_t, Wk_c, Wv_c, Wr_c, ln1_g, ln1_b, ln2_g, ln2_b, mix_k, mix_v, mix_r, cmix_k, cmix_r):
        import jax, jax.numpy as jnp
        import numpy as np
        B, T, C = (8, 256, 128)
        EPS_LN = 1e-05
        EPS_WKV = 1e-08

        def layer_norm(x, g, b):
            mu = jnp.mean(x, axis=-1, keepdims=True)
            var = jnp.var(x, axis=-1, keepdims=True)
            return (x - mu) * jax.lax.rsqrt(var + EPS_LN) * g + b

        def time_shift(x, ratio):
            x_prev = jnp.pad(x[:, :-1, :], ((0, 0), (1, 0), (0, 0)))
            return x * ratio + x_prev * (1.0 - ratio)

        def wkv(w, u, k, v):
            kT = jnp.swapaxes(k, 0, 1)
            vT = jnp.swapaxes(v, 0, 1)
            aa0 = jnp.zeros((k.shape[0], k.shape[2]), k.dtype)
            ninf = jnp.full_like(aa0, -jnp.inf)

            def step(carry, kv):
                aa, bb, pp = carry
                kk, vv = kv
                ww = u + kk
                p = jnp.maximum(pp, ww)
                e1 = jnp.exp(pp - p)
                e2 = jnp.exp(ww - p)
                out = (e1 * aa + e2 * vv) / (e1 + e2 + EPS_WKV)
                bb_new = w + pp
                p2 = jnp.maximum(pp, kk)
                e1b = jnp.exp(pp - p2)
                e2b = jnp.exp(kk - p2)
                aa_new = e1b * aa + e2b * vv
                pp_new = p2 + jnp.log(e1b + e2b + EPS_WKV)
                return ((aa_new, bb_new, pp_new), out)
            (aa, bb, pp), outT = jax.lax.scan(step, (aa0, ninf, ninf), (kT, vT))
            output = jnp.swapaxes(outT, 0, 1)
            final_state = jnp.stack([aa, bb, pp], axis=2)
            return (output, final_state)

        def _reference_tuple_inner(x, time_decay, time_first, Wk_t, Wv_t, Wr_t, Wk_c, Wv_c, Wr_c, ln1_g, ln1_b, ln2_g, ln2_b, mix_k, mix_v, mix_r, cmix_k, cmix_r):
            h = layer_norm(x, ln1_g, ln1_b)
            k = time_shift(h, mix_k) @ Wk_t.T
            v = time_shift(h, mix_v) @ Wv_t.T
            r = jax.nn.sigmoid(time_shift(h, mix_r) @ Wr_t.T)
            w = -jnp.exp(time_decay)
            wkv_out, new_state = wkv(w, time_first, k, v)
            x = x + r * wkv_out
            h2 = layer_norm(x, ln2_g, ln2_b)
            kc = time_shift(h2, cmix_k) @ Wk_c.T
            rc = jax.nn.sigmoid(time_shift(h2, cmix_r) @ Wr_c.T)
            vv = jnp.square(jax.nn.relu(kc)) @ Wv_c.T
            x = x + rc * vv
            return (x, new_state)
        return _reference_tuple_inner(x, time_decay, time_first, Wk_t, Wv_t, Wr_t, Wk_c, Wv_c, Wr_c, ln1_g, ln1_b, ln2_g, ln2_b, mix_k, mix_v, mix_r, cmix_k, cmix_r)[0]

    def _L2_xattn_ref(q, kv, x_seqlens, Wq, Wk, Wv, Wo, q_norm_w, k_norm_w):
        import jax, jax.numpy as jnp
        import numpy as np
        DIM, HEADS, HEAD_DIM = (128, 16, 64)
        B, L, S = (4, 256, 256)
        EPS = 1e-05
        NEG_INF = -1000000000.0

        def rms_norm(x, w):
            var = jnp.mean(jnp.square(x), axis=-1, keepdims=True)
            return x * jax.lax.rsqrt(var + EPS) * w
        b, l, _ = q.shape
        s = kv.shape[1]
        qh = (q @ Wq).reshape(b, l, HEADS, HEAD_DIM).transpose(0, 2, 1, 3)
        kh = (kv @ Wk).reshape(b, s, HEADS, HEAD_DIM).transpose(0, 2, 1, 3)
        vh = (kv @ Wv).reshape(b, s, HEADS, HEAD_DIM).transpose(0, 2, 1, 3)
        qh = rms_norm(qh, q_norm_w)
        kh = rms_norm(kh, k_norm_w)
        mask = (jnp.arange(s, dtype=jnp.int32)[None, :] < x_seqlens[:, None])[:, None, None, :]
        scores = jnp.einsum('bhld,bhsd->bhls', qh, kh) * (1.0 / np.sqrt(HEAD_DIM))
        scores = jnp.where(mask, scores, NEG_INF)
        attn = jax.nn.softmax(scores, axis=-1)
        o = jnp.einsum('bhls,bhsd->bhld', attn, vh)
        o = o.transpose(0, 2, 1, 3).reshape(b, l, HEADS * HEAD_DIM)
        return o @ Wo

    def _L2_ffn_ref(x, Wg, W1, b1, W2, b2):
        import jax, jax.numpy as jnp
        import numpy as np
        B, S, D = (4, 512, 128)
        E, K, H = (8, 2, 256)
        logits = jnp.einsum('bsd,de->bse', x, Wg)
        probs = jax.nn.softmax(logits, axis=-1)
        topv, topi = jax.lax.top_k(probs, K)
        cw = topv / (jnp.sum(topv, axis=-1, keepdims=True) + 1e-09)
        we = jnp.sum(jax.nn.one_hot(topi, E, dtype=x.dtype) * cw[..., None], axis=-2)
        y = jnp.zeros_like(x)
        for e in range(E):
            h = jax.nn.relu(jnp.einsum('bsd,dh->bsh', x, W1[e]) + b1[e])
            out_e = jnp.einsum('bsh,hd->bsd', h, W2[e]) + b2[e]
            y = y + we[..., e:e + 1] * out_e
        return y

    def _L3_attn_ref(x, Wqkvg, bqkvg, wave_frequency, wave_damping, wave_phase, field_coupling, Wout, bout):
        import jax, jax.numpy as jnp
        import numpy as np
        import math
        B, N, D, H, G = (4, 256, 128, 16, 256)
        HD = D // H
        MAX_SEQ = 256
        STRIDE = (G - 1) / max(MAX_SEQ - 1, 1)

        def _forward(x, Wqkvg, bqkvg, wave_frequency, wave_damping, wave_phase, field_coupling, Wout, bout):
            b, n, d = x.shape
            qkvg = x @ Wqkvg.T + bqkvg
            q, k, v, gate_raw = jnp.split(qkvg, 4, axis=-1)
            to_heads = lambda t: t.reshape(b, n, H, HD).transpose(0, 2, 1, 3)
            q, k, v = (to_heads(q), to_heads(k), to_heads(v))
            seq_pos = jnp.arange(n, dtype=jnp.float32)
            field_pos = jnp.clip(seq_pos * STRIDE, 0.0, G - 2)
            idx_lo = jnp.clip(field_pos.astype(jnp.int32), 0, G - 2)
            idx_hi = idx_lo + 1
            frac = jnp.clip(field_pos - idx_lo.astype(jnp.float32), 0.0, 1.0)
            w_lo = (1.0 - frac)[None, None, :, None]
            w_hi = frac[None, None, :, None]
            q_feat = jax.nn.elu(q) + 1.0
            k_feat = jax.nn.elu(k) + 1.0
            deposit = k_feat * v
            field = jnp.zeros((b, H, G, HD), deposit.dtype)
            field = field.at[:, :, idx_lo, :].add(deposit * w_lo)
            field = field.at[:, :, idx_hi, :].add(deposit * w_hi)
            t = jnp.arange(G, dtype=jnp.float32)
            alpha = jax.nn.softplus(wave_damping)[:, None]
            omega = wave_frequency[:, None]
            phi = wave_phase[:, None]
            kernels = jnp.exp(-alpha * t[None, :]) * jnp.cos(omega * t[None, :] + phi)
            kernels = kernels / jnp.clip(jnp.sum(jnp.abs(kernels), axis=1, keepdims=True), 1e-08)
            kernel_fft = jnp.fft.rfft(kernels, n=2 * G, axis=-1)
            field_fft = jnp.fft.rfft(field, n=2 * G, axis=2)
            convolved = jnp.fft.irfft(field_fft * kernel_fft[None, :, :, None], n=2 * G, axis=2)[:, :, :G, :]
            coupling = jax.nn.softmax(field_coupling, axis=-1)
            field_c = jnp.einsum('ij,bjgd->bigd', coupling, convolved)
            gathered = field_c[:, :, idx_lo, :] * w_lo + field_c[:, :, idx_hi, :] * w_hi
            wave_output = q_feat * gathered
            gate = jax.nn.sigmoid(gate_raw).reshape(b, n, H, HD).transpose(0, 2, 1, 3)
            output = (wave_output * gate).transpose(0, 2, 1, 3).reshape(b, n, d)
            return output @ Wout.T + bout
        return _forward(x, Wqkvg, bqkvg, wave_frequency, wave_damping, wave_phase, field_coupling, Wout, bout)

    def _L3_xattn_ref(query, key, value, Wq, bq, Wk, bk, Wv, bv, Wo, bo):
        import jax, jax.numpy as jnp
        import numpy as np
        EMBED_DIM = 128
        NUM_HEADS = 16
        HEAD_DIM = EMBED_DIM // NUM_HEADS
        B, T_Q, T_K = (2, 256, 256)
        b, tq, _ = query.shape
        tk = key.shape[1]
        q = (query @ Wq.T + bq).reshape(b, tq, NUM_HEADS, HEAD_DIM).transpose(0, 2, 1, 3)
        k = (key @ Wk.T + bk).reshape(b, tk, NUM_HEADS, HEAD_DIM).transpose(0, 2, 1, 3)
        v = (value @ Wv.T + bv).reshape(b, tk, NUM_HEADS, HEAD_DIM).transpose(0, 2, 1, 3)
        scores = jnp.einsum('bhqd,bhkd->bhqk', q, k) / np.sqrt(HEAD_DIM)
        attn = jax.nn.softmax(scores, axis=-1)
        attn = jnp.nan_to_num(attn, nan=0.0)
        out = jnp.einsum('bhqk,bhkd->bhqd', attn, v)
        out = out.transpose(0, 2, 1, 3).reshape(b, tq, EMBED_DIM)
        return out @ Wo.T + bo

    def _L3_ffn_ref(x, Wr, W1, b1, W2, b2, fw1, fb1, fw2, fb2):
        import jax, jax.numpy as jnp
        import numpy as np
        B, S = (4, 256)
        D_MODEL, D_FF, N_EXPERTS, TOP_K = (128, 512, 8, 2)
        T = B * S
        CAPACITY_FACTOR, MIN_CAP = (1.25, 4)
        CAP = max(int(CAPACITY_FACTOR * (T * TOP_K / N_EXPERTS)), MIN_CAP)
        Bx, Sx, D = x.shape
        Tn = Bx * Sx
        xf = x.reshape(Tn, D)
        logits = xf @ Wr
        probs = jax.nn.softmax(logits, axis=-1)
        scores, experts = jax.lax.top_k(probs, TOP_K)
        scores = scores / jnp.maximum(scores.sum(-1, keepdims=True), 1e-09)
        y_fb = jax.nn.gelu(xf @ fw1 + fb1, approximate=False) @ fw2 + fb2
        y = jnp.zeros_like(xf)
        fb_mask = jnp.zeros((Tn,), bool)
        for e in range(N_EXPERTS):
            assign = experts == e
            w_e = jnp.where(assign, scores, 0.0).sum(-1)
            eligible = assign.any(-1) & ~fb_mask
            rank = jnp.cumsum(eligible.astype(jnp.int32)) - 1
            keep = eligible & (rank < CAP)
            overflow = eligible & ~keep
            fb_mask = fb_mask | overflow
            y = jnp.where(overflow[:, None], y_fb, y)
            idx = jnp.nonzero(keep, size=CAP, fill_value=0)[0]
            valid = jnp.arange(CAP) < keep.sum()
            h = jax.nn.gelu(xf[idx] @ W1[e] + b1[e], approximate=False)
            y_e = h @ W2[e] + b2[e]
            y = y.at[idx].add(y_e * (w_e[idx] * valid)[:, None])
        return y.reshape(Bx, Sx, D)
    x = x + _L0_attn_ref(_layernorm(x, axis=-1), L0_attn_W_q1, L0_attn_b_q1, L0_attn_W_q2, L0_attn_b_q2, L0_attn_W_k1, L0_attn_b_k1, L0_attn_W_k2, L0_attn_b_k2, L0_attn_W_v, L0_attn_b_v, L0_attn_W_out, L0_attn_b_out, L0_attn_ln_g, L0_attn_ln_b)
    x = x + _L0_xattn_ref(_layernorm(x, axis=-1), ctx_1024, ctx_1024, L0_xattn_Wq, L0_xattn_bq, L0_xattn_Wk, L0_xattn_bk, L0_xattn_Wv, L0_xattn_bv, L0_xattn_Wf, L0_xattn_bf)
    x = x + _L0_ffn_ref(_layernorm(x, axis=-1), L0_ffn_weight)
    x = x + _L1_attn_ref(_layernorm(x, axis=-1), L1_attn_attn_norm_w, L1_attn_Wqkv_w, L1_attn_Wqkv_b, L1_attn_attn_out_w, L1_attn_attn_out_b, L1_attn_normf_w, L1_attn_m_in_w, L1_attn_m_conv_w, L1_attn_m_conv_b, L1_attn_m_dt_bias, L1_attn_m_A_log, L1_attn_m_D, L1_attn_m_norm_w, L1_attn_m_out_w, L1_attn_fc1_w, L1_attn_fc2_w, L1_attn_final_norm_w)
    x = x + _L1_xattn_ref(_layernorm(x, axis=-1), ctx_1024, ctx_1024, L1_xattn_w_proj, L1_xattn_b_proj)
    x = x + _L1_ffn_ref(_layernorm(x, axis=-1), L1_ffn_wf, L1_ffn_uf, L1_ffn_bf, L1_ffn_wi, L1_ffn_ui, L1_ffn_bi, L1_ffn_wc, L1_ffn_uc, L1_ffn_bc, L1_ffn_wo, L1_ffn_uo, L1_ffn_bo, L1_ffn_in_c)
    x = x + _L2_attn_ref(_layernorm(x, axis=-1), L2_attn_time_decay, L2_attn_time_first, L2_attn_Wk_t, L2_attn_Wv_t, L2_attn_Wr_t, L2_attn_Wk_c, L2_attn_Wv_c, L2_attn_Wr_c, L2_attn_ln1_g, L2_attn_ln1_b, L2_attn_ln2_g, L2_attn_ln2_b, L2_attn_mix_k, L2_attn_mix_v, L2_attn_mix_r, L2_attn_cmix_k, L2_attn_cmix_r)
    x = x + _L2_xattn_ref(_layernorm(x, axis=-1), ctx_1024, _lenS2, L2_xattn_Wq, L2_xattn_Wk, L2_xattn_Wv, L2_xattn_Wo, L2_xattn_q_norm_w, L2_xattn_k_norm_w)
    x = x + _L2_ffn_ref(_layernorm(x, axis=-1), L2_ffn_Wg, L2_ffn_W1, L2_ffn_b1, L2_ffn_W2, L2_ffn_b2)
    x = x + _L3_attn_ref(_layernorm(x, axis=-1), L3_attn_Wqkvg, L3_attn_bqkvg, L3_attn_wave_frequency, L3_attn_wave_damping, L3_attn_wave_phase, L3_attn_field_coupling, L3_attn_Wout, L3_attn_bout)
    x = x + _L3_xattn_ref(_layernorm(x, axis=-1), ctx_1024, ctx_1024, L3_xattn_Wq, L3_xattn_bq, L3_xattn_Wk, L3_xattn_bk, L3_xattn_Wv, L3_xattn_bv, L3_xattn_Wo, L3_xattn_bo)
    x = x + _L3_ffn_ref(_layernorm(x, axis=-1), L3_ffn_Wr, L3_ffn_W1, L3_ffn_b1, L3_ffn_W2, L3_ffn_b2, L3_ffn_fw1, L3_ffn_fb1, L3_ffn_fw2, L3_ffn_fb2)
    return x

_drawn_inputs = setup_inputs


def setup_inputs(seed=0):
    import zlib

    import numpy as np

    out = dict(_drawn_inputs(seed))
    spreads = {'L0_attn_b_q1': (0.0, 0.1),
     'L0_attn_b_q2': (0.0, 0.1),
     'L0_attn_b_k1': (0.0, 0.1),
     'L0_attn_b_k2': (0.0, 0.1),
     'L0_attn_b_v': (0.0, 0.1),
     'L0_attn_b_out': (0.0, 0.1),
     'L0_attn_ln_g': (1.0, 0.2),
     'L0_attn_ln_b': (0.0, 0.1),
     'L1_attn_attn_norm_w': (1.0, 0.6),
     'L1_attn_Wqkv_b': (0.0, 0.8),
     'L1_attn_attn_out_b': (0.0, 0.629),
     'L1_attn_normf_w': (1.0, 0.6),
     'L1_attn_m_conv_b': (0.0, 0.1),
     'L1_attn_m_D': (1.0, 0.2),
     'L1_attn_m_norm_w': (1.0, 0.2),
     'L1_attn_final_norm_w': (1.0, 0.6),
     'L1_xattn_b_proj': (0.0, 0.761),
     'L1_ffn_bf': (0.0, 0.8),
     'L1_ffn_bi': (0.0, 0.8),
     'L1_ffn_bc': (0.0, 0.8),
     'L1_ffn_bo': (0.0, 0.8),
     'L1_ffn_in_c': (0.0, 0.8),
     'L2_attn_ln1_g': (1.0, 0.535),
     'L2_attn_ln1_b': (0.0, 0.1),
     'L2_attn_ln2_g': (1.0, 0.6),
     'L2_attn_ln2_b': (0.0, 0.8),
     'L2_attn_mix_k': (1.0, 0.6),
     'L2_attn_mix_v': (1.0, 0.6),
     'L2_attn_mix_r': (1.0, 0.6),
     'L2_attn_cmix_k': (1.0, 0.6),
     'L2_attn_cmix_r': (1.0, 0.6),
     'L2_xattn_q_norm_w': (1.0, 0.6),
     'L2_xattn_k_norm_w': (1.0, 0.6),
     'L3_attn_bout': (0.0, 0.8),
     'L3_xattn_bq': (0.0, 0.8),
     'L3_xattn_bk': (0.0, 0.8),
     'L3_xattn_bv': (0.0, 0.8),
     'L3_xattn_bo': (0.0, 0.8),
     'L3_ffn_b1': (0.0, 0.8),
     'L3_ffn_b2': (0.0, 0.8),
     'L3_ffn_fb1': (0.0, 0.8),
     'L3_ffn_fb2': (0.0, 0.8)}
    factors = {'L0_xattn_bq': 8.0,
     'L0_xattn_bk': 8.0,
     'L0_xattn_bv': 6.362,
     'L0_xattn_bf': 5.758,
     'L1_attn_Wqkv_w': 8.0,
     'L1_attn_attn_out_w': 8.0,
     'L1_attn_m_dt_bias': 8.0,
     'L1_attn_m_A_log': 8.0,
     'L1_attn_fc1_w': 8.0,
     'L1_attn_fc2_w': 8.0,
     'L1_xattn_w_proj': 4.003,
     'L1_ffn_wf': 6.643,
     'L1_ffn_uf': 8.0,
     'L1_ffn_wi': 4.866,
     'L1_ffn_ui': 8.0,
     'L1_ffn_uc': 3.983,
     'L2_attn_time_first': 8.0,
     'L2_xattn_Wq': 3.656,
     'L2_xattn_Wk': 3.577,
     'L2_ffn_Wg': 4.328,
     'L2_ffn_W1': 4.696,
     'L2_ffn_b1': 8.0,
     'L2_ffn_W2': 3.908,
     'L2_ffn_b2': 8.0,
     'L3_attn_Wqkvg': 8.0,
     'L3_attn_bqkvg': 8.0,
     'L3_attn_wave_frequency': 8.0,
     'L3_attn_wave_damping': 8.0,
     'L3_attn_wave_phase': 8.0,
     'L3_attn_field_coupling': 8.0,
     'L3_attn_Wout': 8.0,
     'L3_xattn_Wq': 3.362,
     'L3_xattn_Wk': 3.25}
    for name, (base, spread) in spreads.items():
        noise = np.random.default_rng([zlib.crc32(name.encode()), seed]).standard_normal(out[name].shape)
        drawn = base * np.exp(spread * noise) if base else spread * noise
        out[name] = jnp.asarray(drawn.astype(out[name].dtype))
    for name, factor in factors.items():
        out[name] = (out[name] * factor).astype(out[name].dtype)
    return out
```

```python
import numpy as np
import concourse.bass as bass
import concourse.mybir as mybir
from concourse.alu_op_type import AluOpType as ALU
from contextlib import ExitStack

F32 = mybir.dt.float32
BF16 = mybir.dt.bfloat16
ACT = mybir.ActivationFunctionType
AXX = mybir.AxisListType.X

B, S, D = 8, 256, 128
P = 128
HALVES = S // P
NT = B * HALVES
T = B * S
H = 16
HD = D // H
HW = 64
GROUP = 32
NSPREAD = H * GROUP // P
NWIDE = H * HW // P
BANK = 512
QUARTERS = T // BANK
M_LAYERS, D_INNER, D_STATE, H_SSM, D_CONV = 4, 256, 128, 4, 4
HP = D_INNER // H_SSM
CONV_CH = (D_INNER + 2 * D_STATE) // P
DFF = 256
ALPHA = 1.68
E8 = 8
MOE2_H = 256
MOE3_H = 512
CAP = max(int(1.25 * (1024 * 2 / E8)), 4)
NEG_INF = -1e9
BEFORE_ALL = -1e30

CONSTS = [("ident", P), ("upto", P), ("ones", P), ("after", P), ("spread_id", NSPREAD * P),
          ("steps", S), ("head_rows", P), ("same_d", HD), ("before", E8 * E8),
          ("neg_parts", 1), ("lower", 1), ("upper", 1), ("one_row", 1)]
L0_W = [("a_q1", D), ("a_q2", D), ("a_k1", D), ("a_k2", D), ("a_v", D), ("a_out", D),
        ("a_bias_bc", 5 * D), ("a_bout_bc", D), ("a_g", 1), ("a_b", 1),
        ("x_wq", D), ("x_wk", D), ("x_wv", D), ("x_wf", D), ("x_bq", 1), ("x_bk", 1),
        ("x_bv_bc", D), ("x_bf_bc", D), ("f_w", D)]
L1_W = [("s_wq", NSPREAD * P), ("s_wk", NSPREAD * P), ("s_bq", NSPREAD), ("s_bk", NSPREAD),
        ("s_wv", D), ("s_bv_bc", D), ("s_wo", D), ("s_bo_bc", D), ("s_norm", 1), ("s_normf_bc", D),
        ("s_final_bc", D), ("s_fc1", 2 * DFF), ("s_fc2", DFF // P * D)]
M_W = [(f"m{l}_{n}", c) for l in range(M_LAYERS) for n, c in
       [("xbc", CONV_CH * P), ("z", D_INNER), ("dt", H_SSM), ("cw", CONV_CH * D_CONV), ("cb", CONV_CH),
        ("dtb", H_SSM), ("alog", H_SSM), ("dskip_bc", H_SSM), ("norm", D_INNER // P),
        ("out", D_INNER // P * D)]]
L1_W2 = [("c_proj", D), ("c_b_bc", D),
         ("g_wf", D), ("g_uf", D), ("g_wi", D), ("g_ui", D), ("g_wc", D), ("g_uc", D), ("g_wo", D),
         ("g_uo", D), ("g_bf", 1), ("g_bi", 1), ("g_bc", 1), ("g_bo_bc", D), ("g_c0", 1)]
L2_W = [("r_u", 1), ("r_wk", D), ("r_wv", D), ("r_wr", D), ("r_wkc", 4 * D), ("r_wvc", 4 * D),
        ("r_wrc", D), ("r_g1", 1), ("r_b1", 1), ("r_g2", 1), ("r_b2", 1), ("r_mk", 1), ("r_mv", 1),
        ("r_mr", 1), ("r_ck", 1), ("r_cr", 1)]
L2_X = [("w_q", H * HW), ("w_k", H * HW), ("w_v", H * HW), ("w_o", NWIDE * D), ("w_qn", 1), ("w_kn", 2),
        ("w_pos", HALVES)]
L2_F = [("e_wg", E8), ("e_w1", E8 * MOE2_H), ("e_b1", E8 * MOE2_H // P), ("e_w2", E8 * MOE2_H // P * D),
        ("e_b2", D)]
L3_A = [("v_wq", D), ("v_wk", D), ("v_wv", D), ("v_wg", D), ("v_bq", 1), ("v_bkv_bc", 2 * D), ("v_bg", 1),
        ("v_freq", 1), ("v_damp", 1), ("v_phase", 1), ("v_coup", H), ("v_wo", D), ("v_bo_bc", D)]
L3_X = [("y_wq", NSPREAD * P), ("y_wk", NSPREAD * P), ("y_bq", NSPREAD), ("y_bk", NSPREAD), ("y_wv", D),
        ("y_bv_bc", D), ("y_wo", D), ("y_bo_bc", D)]
L3_F = [("z_wr", E8), ("z_w1", E8 * MOE3_H), ("z_b1", E8 * MOE3_H // P), ("z_w2", E8 * MOE3_H // P * D),
        ("z_b2", D), ("z_fw1", MOE3_H), ("z_fb1", MOE3_H // P), ("z_fw2", MOE3_H // P * D), ("z_fb2_bc", D)]
PACKS = [("consts", CONSTS, "keep"), ("l0", L0_W, "early"), ("l1", L1_W, "early"), ("mamba", M_W, "early"),
         ("l1b", L1_W2, "early"), ("l2", L2_W, "keep"), ("l2x", L2_X, "keep"), ("l2f", L2_F, "keep"),
         ("l3a", L3_A, "keep"), ("l3x", L3_X, "keep"), ("l3f", L3_F, "late")]


def columns(pack):
    return sum(c for _, c in pack)


class Step:

    def __init__(self, queue, issue, after):
        self.queue, self.issue, self.after = queue, issue, after
        self.count, self.sem, self.amount = 0, None, 1


class Queue:

    def __init__(self, chained):
        self.steps, self.chained = [], chained
        self.pending = []

    def put(self, issue, after, free=False):
        after = [a for a in after if a is not None]
        if self.pending:
            after += self.pending
            self.pending = []
        if self.chained and not free and self.steps:
            after.append(self.steps[-1])
        step = Step(self, issue, after)
        self.steps.append(step)
        return step

    def emit(self, engine):
        seen = {}
        for step in self.steps:
            need = {}
            for a in step.after:
                if a.count > max(seen.get(id(a.sem), 0), need.get(id(a.sem), (0, None))[0]):
                    need[id(a.sem)] = (a.count, a.sem)
            for key, (count, sem) in need.items():
                engine.wait_ge(sem, count)
                seen[key] = count
            step.issue(engine).then_inc(step.sem, step.amount)


class Ring:

    def __init__(self, bufs):
        self.bufs, self.last, self.at = bufs, [[] for _ in bufs], -1

    def take(self):
        self.at = (self.at + 1) % len(self.bufs)
        assert self.last[self.at] is not None, "the buffer is still in use"
        free, self.last[self.at] = self.last[self.at], None
        return self.bufs[self.at], self.at, free

    def done(self, slot, *readers):
        self.last[slot] = [r for r in readers if r is not None]


class Program:

    def __init__(self, nc, ctx):
        self.nc, self.ctx = nc, ctx
        self.pe, self.dve, self.act, self.pool = Queue(False), Queue(True), Queue(True), Queue(True)
        self.sp = Queue(False)
        self.dmas = []

    def mm(self, out, lhsT, rhs, start, stop, *after):
        return self.pe.put(lambda e: e.matmul(out, lhsT, rhs, start=start, stop=stop, skip_group_check=True), list(after))

    def tr(self, out, in_, ident, *after):
        return self.pe.put(lambda e: e.transpose(out, in_, ident), list(after))

    def tt(self, q, out, a, b, op, *after, free=False):
        return q.put(lambda e: e.tensor_tensor(out, a, b, op), list(after), free)

    def ts(self, q, out, a, s1, s2, op0, op1, *after, free=False):
        if op1 is None:
            return q.put(lambda e: e.tensor_scalar(out, a, s1, None, op0), list(after), free)
        return q.put(lambda e: e.tensor_scalar(out, a, s1, s2, op0, op1), list(after), free)

    def stt(self, q, out, a, s, b, op0, op1, *after, free=False):
        return q.put(lambda e: e.scalar_tensor_tensor(out=out, in0=a, scalar=s, in1=b, op0=op0, op1=op1), list(after), free)

    def cp(self, q, out, a, *after, free=False):
        if q is self.act:
            return q.put(lambda e: e.activation(out, a, ACT.Copy), list(after), free)
        return q.put(lambda e: e.tensor_copy(out, a), list(after), free)

    def af(self, out, a, func, *after, scale=1.0, bias=None, free=False):
        if bias is None:
            return self.act.put(lambda e: e.activation(out, a, func, scale=scale), list(after), free)
        return self.act.put(lambda e: e.activation(out, a, func, scale=scale, bias=bias), list(after), free)

    def red(self, out, a, op, *after, negate=None, mag=None, free=False):
        return self.dve.put(lambda e: e.tensor_reduce(out, a, AXX, op, negate=negate, apply_absolute_value=mag), list(after), free)

    def scan(self, out, a, b, init, op0, op1, *after, free=False):
        return self.dve.put(lambda e: e.tensor_tensor_scan(out, a, b, init, op0, op1), list(after), free)

    def recip(self, out, a, *after, free=False):
        return self.dve.put(lambda e: e.reciprocal(out, a), list(after), free)

    def fill(self, q, out, value, *after, free=False):
        return q.put(lambda e: e.memset(out, value), list(after), free)

    def bnst(self, out, a, *after, free=False):
        return self.dve.put(lambda e: e.bn_stats(out, a), list(after), free)

    def bnag(self, out, a, *after, free=False):
        return self.dve.put(lambda e: e.bn_aggr(out, a), list(after), free)

    def dma(self, out, in_, *after):
        step = self.sp.put(lambda e: e.dma_start(out, in_), list(after))
        step.sem, step.count, step.amount = self.ctx.enter_context(self.nc.semaphore(f"s_dma{len(self.dmas)}")), 16, 16
        self.dmas.append(step)
        return step

    def boundary(self):
        queues = [self.pe, self.dve, self.act, self.pool]
        lasts = [q.steps[-1] for q in queues if q.steps]
        for q in queues + [self.sp]:
            q.pending = [s for s in lasts if s.queue is not q or q.chained]

    def finish(self, block):
        for q, name in ((self.pe, "s_pe"), (self.dve, "s_dve"), (self.act, "s_act"), (self.pool, "s_pool")):
            sem = self.ctx.enter_context(self.nc.semaphore(name))
            for n, step in enumerate(q.steps):
                step.sem, step.count = sem, n + 1
        for q, on in ((self.pe, block.tensor), (self.dve, block.vector), (self.act, block.scalar),
                      (self.pool, block.gpsimd), (self.sp, block.sync)):
            on(lambda engine, q=q: self.run(q, engine))

    def run(self, q, engine):
        q.emit(engine)
        if q is self.sp:
            for step in self.dmas:
                engine.wait_ge(step.sem, step.count)


def alternate(p, n):
    return p.act if n % 2 else p.dve


class Loads:
    pass


class Core:
    pass


def start(core, nc, ctx, packs, x_dram, ctx_dram, ctxt_dram, lens_dram, kern_dram, out_dram, sel_dram):
    core.nc, core.ctx = nc, ctx
    p = core.p = Program(nc, ctx)
    core.out_dram, core.kern_dram = out_dram, kern_dram
    sizes = {r: sum(columns(c) for _, c, where in PACKS if where == r) for r in ("keep", "early", "late")}
    keep = sb(core, "w_keep", [P, sizes["keep"]])
    early = sb(core, "w_early", [P, max(sizes["early"], sizes["late"])])
    core.early, core.keep, core.used2, core.used3 = early, keep, 0, 0
    core.l2x_at = columns(CONSTS) + columns(L2_W)
    core.weights, core.pack_dram = {}, packs
    came = core.came = Loads()
    at = {"keep": 0, "early": 0, "late": 0}
    core.pack_dst = {}
    for name, layout, region in PACKS:
        base, buf = at[region], keep if region == "keep" else early
        core.pack_dst[name] = buf[:, base:base + columns(layout)]
        o = base
        for n, c in layout:
            core.weights[n] = buf[:, o:o + c]
            o += c
        at[region] = o
    core.weights["upto2"] = keep[:, P:3 * P]
    core.X = sb(core, "X", [P, NT, D])
    core.XN = sb(core, "XN", [P, NT, D])
    core.XNT = sb(core, "XNT", [P, T])
    core.CT = sb(core, "CT", [P, T])
    core.CX = sb(core, "CX", [P, NT, D])
    core.SEL = sb(core, "SEL", [P, H, P], BF16)
    core.ONE = sb(core, "ONE", [P, P], BF16)
    core.kern = sb(core, "kern", [H, S])
    core.kern_zero = sb(core, "kern_zero", [H, P])
    core.IDB = sb(core, "IDB", [P, P], BF16)
    core.stats = sb(core, "stats", [P, NT, 6])
    core.mv = sb(core, "mv", [P, NT, 2])
    core.rs = sb(core, "rs", [P, NT])
    left = nc.sbuf_bytes_remaining() if callable(nc.sbuf_bytes_remaining) else nc.sbuf_bytes_remaining
    core.scratch_cols = (left - 2048) // 4
    core.scratch = sb(core, "scratch", [P, core.scratch_cols])
    core.used = 0
    core.banks = [ctx.enter_context(nc.psum_tensor(f"bank{i}", [P, BANK], F32)) for i in range(8)]
    core.work = Ring(core.banks[0:6])
    core.acc = Ring(core.banks[6:8])
    core.x_in = p.dma(core.X[:, :, :], x_dram)
    came.consts = load(core, "consts")
    came.l0 = load(core, "l0")
    core.ctx_in = [p.dma(core.CT[:, :], ctxt_dram), p.dma(core.CX[:, :, :], ctx_dram)]
    core.sel_in = p.dma(core.SEL[:, :, :], sel_dram)
    came.l1 = load(core, "l1")
    came.mamba = load(core, "mamba")
    came.l1b = load(core, "l1b")
    came.l2 = load(core, "l2")
    core.lens_dram = lens_dram
    came.l3a = load(core, "l3a")
    came.l3x = load(core, "l3x")
    one = p.fill(p.pool, core.ONE[:, :], 1.0)
    idb = p.cp(p.dve, core.IDB[:, :], core.weights["ident"], core.came.consts)
    core.const_ready = [one, idb, core.sel_in]


def sb(core, name, shape, dt=F32):
    return core.ctx.enter_context(core.nc.sbuf_tensor(name, shape, dt))


def tmp3(core, cols):
    at, core.used3 = core.used3, core.used3 + cols
    assert core.used3 <= columns(L2_X) + columns(L2_F)
    return core.keep[:, core.l2x_at + at:core.l2x_at + at + cols]


def load(core, name, *after):
    return core.p.dma(core.pack_dst[name], core.pack_dram[name], *after)


def tmp2(core, cols, dt=F32):
    words = cols if dt == F32 else (cols + 1) // 2
    ap = core.early[:, core.used2:core.used2 + words]
    core.used2 += words
    assert core.used2 <= core.early.shape[1]
    return ap if dt == F32 else ap.bitcast(dt)


def tmp(core, cols, dt=F32):
    words = cols if dt == F32 else (cols + 1) // 2
    ap = core.scratch[:, core.used:core.used + words]
    core.used += words
    assert core.used <= core.scratch_cols, ("scratch", core.used, core.scratch_cols)
    return ap if dt == F32 else ap.bitcast(dt)


def stage(core):
    core.p.boundary()
    core.used = core.used2 = core.used3 = 0


def rstd(core, out, var, n, *after):
    p = core.p
    p.ts(p.dve, var, var, 1e-5, None, ALU.add, None, *after)
    a = p.dve.steps[-1]
    s = p.af(out, var, ACT.Sqrt, a)
    return p.recip(out, out, s)


def normalise(core, src, dst, *after):
    p = core.p
    for i in range(NT):
        p.bnst(core.stats[:, i, :], src[:, i, :], *after, free=i > 0)
    for i in range(NT):
        p.bnag(core.mv[:, i, :], core.stats[:, i, :], free=i > 0)
    r = rstd(core, core.rs[:, :], core.mv[:, :, 1], NT)
    out = []
    for i in range(NT):
        out.append(p.ts(p.dve, dst[:, i, :], src[:, i, :], core.mv[:, i, 0:1], core.rs[:, i:i + 1],
                        ALU.subtract, ALU.mult, r, free=i > 0))
    return out


def mean_square(core, tiles, src, width, *after):
    p = core.p
    for i in range(tiles):
        p.bnst(core.stats[:, i, :], src(i), *after, free=i > 0)
    for i in range(tiles):
        p.bnag(core.mv[:, i, :], core.stats[:, i, :], free=i > 0)
    m, v = core.mv[:, 0:tiles, 0], core.mv[:, 0:tiles, 1]
    p.tt(p.dve, m, m, m, ALU.mult)
    p.tt(p.dve, v, v, m, ALU.add)
    return rstd(core, core.rs[:, 0:tiles], v, tiles)


def transpose_all(core, src, dst, after, scale=None, bias=None):
    p, out = core.p, []
    for n in range(QUARTERS):
        bank, slot, free = core.work.take()
        for j in range(BANK // P):
            i = n * (BANK // P) + j
            t = p.tr(bank[:, j * P:(j + 1) * P], src(i), core.weights["ident"], after(i), core.came.consts, *free)
        d = dst(n)
        if scale is None:
            e = p.cp(alternate(p, n), d, bank[:, :], t, free=True)
        elif bias is None:
            e = p.ts(p.dve, d, bank[:, :], scale, None, ALU.mult, None, t, free=True)
        else:
            e = p.ts(p.dve, d, bank[:, :], scale, bias, ALU.mult, ALU.add, t, free=True)
        core.work.done(slot, e)
        out.append(e)
    return out


def pre_norm(core):
    n = normalise(core, core.X, core.XN)
    return transpose_all(core, lambda i: core.XN[:, i, :], lambda q: core.XNT[:, q * BANK:(q + 1) * BANK], lambda i: n[i])


def add_product(core, lhs, weight, after, pieces=1, bias_bc=None, dst=None):
    p = core.p
    dst = core.X if dst is None else dst
    out = []
    for n in range(QUARTERS):
        bank, slot, free = core.work.take()
        for j in range(BANK // P):
            i = n * (BANK // P) + j
            for c in range(pieces):
                m = p.mm(bank[:, j * P:(j + 1) * P], lhs(c, i), weight(c), c == 0, c == pieces - 1,
                         *after(i), *free)
        tiles = dst[:, n * 4:(n + 1) * 4, :]
        b = bank[:, :].rearrange("p (j d) -> p j d", d=D)
        if bias_bc is not None:
            p.tt(p.pool, tiles, tiles, bias_bc.unsqueeze(1).to_broadcast([P, 4, D]), ALU.add, p.dve.steps[-1])
        e = p.tt(p.dve, tiles, tiles, b, ALU.add, m, p.pool.steps[-1] if p.pool.steps else None, free=True)
        core.work.done(slot, e)
        out.append(e)
    return out


def attention(core, heads, width, scale, prepare, store, masked=None, in_rows=False):
    p = core.p
    expo = Ring([tmp(core, BANK) for _ in range(3)])
    vw = width + 1
    per_acc = min(heads, BANK // vw)
    if in_rows:
        pads = [tmp(core, HALVES * NSPREAD * P) for _ in range(2)]
        padded = Ring(pads)
        for x in pads:
            cleared = p.fill(p.pool, x, 0.0)
    else:
        neg = Ring([tmp(core, HALVES * heads) for _ in range(2)])
        pads = [tmp(core, HALVES * P, BF16) for _ in range(2)]
        part = Ring(pads)
        rest = Ring([tmp(core, HALVES * heads) for _ in range(2)])
        negt = Ring([tmp(core, S, BF16) for _ in range(2)])
        for x in pads:
            cleared = p.fill(p.pool, x, 0.0)
    per_bank = min(heads, BANK // S)

    def row_maxima(b):
        q, k, v, ready = prepare(b)
        pd, ps_, pf = padded.take()
        pdv = pd.rearrange("p (t w g r) -> p t w g r", t=HALVES, w=NSPREAD, r=GROUP)
        groups = P // GROUP
        for t in range(HALVES):
            for w in range(0, NSPREAD, per_bank):
                for g in range(groups):
                    bank, slot, free = core.work.take()
                    for j in range(per_bank):
                        h = (w + j) * groups + g
                        m = p.mm(bank[:, j * S:(j + 1) * S], q(h)[:, t * P:(t + 1) * P], k(h), True, True, *free, *ready)
                    r = p.red(pdv[:, t, w:w + per_bank, g, HD], bank[:, :].rearrange("p (h s) -> p h s", s=S),
                              ALU.max, m, *pf, cleared, negate=True, free=True)
                    core.work.done(slot, r)
        for t in range(HALVES):
            bank, slot, free = core.work.take()
            for w in range(NSPREAD):
                m = p.tr(bank[:, w * P:(w + 1) * P], pd[:, (t * NSPREAD + w) * P:(t * NSPREAD + w + 1) * P],
                         core.weights["ident"], r, *free)
            qt = q.whole[:, :, t * P:(t + 1) * P]
            e = p.tt(p.dve, qt, qt, bank[:, :].rearrange("p (w s) -> p w s", s=P), ALU.add, m)
            core.work.done(slot, e)
        padded.done(ps_, m)
        return q, k, v, ready, None, None, e

    def maxima(b):
        if in_rows:
            return row_maxima(b)
        q, k, v, ready = prepare(b)
        ng, ns, nf = neg.take()
        ngv = ng.rearrange("p (t h) -> p t h", h=heads)
        for t in range(HALVES):
            for h0 in range(0, heads, per_bank):
                bank, slot, free = core.work.take()
                if masked is not None:
                    p.mm(bank[:, :], core.ONE[:, :], masked["row"](b), True, False, *free, *masked["ready"])
                for j in range(per_bank):
                    m = p.mm(bank[:, j * S:(j + 1) * S], q(h0 + j)[:, t * P:(t + 1) * P], k(h0 + j),
                             masked is None, True, *free, *ready)
                r = p.red(ngv[:, t, h0:h0 + per_bank], bank[:, 0:per_bank * S].rearrange("p (h s) -> p h s", s=S),
                          ALU.max, m, *nf, negate=True, free=True)
                core.work.done(slot, r)
        pt, ps_, pf = part.take()
        rt, rs_, rf = rest.take()
        ptv = pt.rearrange("p (t n) -> p t n", n=P)
        rtv = rt.rearrange("p (t h) -> p t h", h=heads)
        cut = lambda n: ptv[:, :, n * heads:(n + 1) * heads]
        p.cp(p.dve, cut(0), ngv, *pf, cleared)
        p.tt(p.dve, rtv, ngv, cut(0), ALU.subtract, *rf)
        p.cp(p.dve, cut(1), rtv)
        r2 = p.tt(p.dve, rtv, rtv, cut(1), ALU.subtract)
        made = p.cp(p.dve, cut(2), rtv)
        neg.done(ns, r2)
        rest.done(rs_, made)
        bank, slot, free = core.work.take()
        bankb = bank[:, :].bitcast(BF16)
        for t in range(HALVES):
            m = p.tr(bankb[:, t * P:(t + 1) * P], ptv[:, t, :], core.IDB[:, :], made, *free)
        part.done(ps_, m)
        nt, nts, ntf = negt.take()
        e = p.cp(p.dve, nt, bankb[:, 0:S], m, *ntf)
        core.work.done(slot, e)
        return q, k, v, ready, nt, nts, e

    def weigh(b, state):
        q, k, v, ready, nt, nts, cut = state
        if core.before_weigh is not None:
            ready = [*ready, core.before_weigh(b)]
        outs = [None] * HALVES
        for h0 in range(0, heads, per_acc):
            accs = [core.acc.take() for _ in range(HALVES)]
            pend = None

            def values(h, ex, exs, e):
                for t in range(HALVES):
                    bank, slot, free = accs[t]
                    for c in range(HALVES):
                        m = p.mm(bank[:, (h - h0) * vw:(h - h0 + 1) * vw], ex[:, c * S + t * P:c * S + (t + 1) * P],
                                 v(h, c), c == 0, c == HALVES - 1, e, *free, *ready)
                expo.done(exs, m)
                return m
            for h in range(h0, min(h0 + per_acc, heads)):
                bank, slot, free = core.work.take()
                if not in_rows:
                    sel = core.SEL[:, h, :] if heads == H else core.ONE[:, :]
                    p.mm(bank[:, :], sel, nt.unsqueeze(1).to_broadcast([P, HALVES, S]), True, False, cut, *free)
                for c in range(HALVES):
                    m = p.mm(bank[:, c * S:(c + 1) * S], k(h)[:, c * P:(c + 1) * P], q(h), in_rows, True, cut, *free)
                ex, exs, exf = expo.take()
                if masked is None:
                    e = p.af(ex, bank[:, :], ACT.Exp, m, *exf, scale=scale, free=True)
                else:
                    for c in range(HALVES):
                        e = p.af(ex[:, c * S:(c + 1) * S], bank[:, c * S:(c + 1) * S], ACT.Exp, m, *exf,
                                 scale=scale, bias=masked["column"](b, c), free=True)
                core.work.done(slot, e)
                if pend is not None:
                    values(*pend)
                pend = (h, ex, exs, e)
            last = values(*pend)
            for t in range(HALVES):
                bank, slot, _ = accs[t]
                n = min(h0 + per_acc, heads) - h0
                bv = bank[:, 0:n * vw].rearrange("p (h w) -> p h w", w=vw)
                r = store(b, t, h0, n, bv[:, :, 0:width], bv[:, :, width:vw], last)
                core.acc.done(slot, r)
        if not in_rows:
            negt.done(nts, last)
        return last

    state = maxima(0)
    for b in range(B):
        ahead = maxima(b + 1) if b + 1 < B else None
        last = weigh(b, state)
        yield b, last
        state = ahead


def run_attention(core, heads, width, scale, prepare, store, done, masked=None, in_rows=False):
    for b, last in attention(core, heads, width, scale, prepare, store, masked, in_rows):
        done(b, last)


def divide(core, dst):
    p = core.p
    sums = Ring([tmp(core, H) for _ in range(4)])

    def store(b, t, h0, n, values, total, last):
        inv, slot, free = sums.take()
        width = values.shape[-1]
        inv = inv[:, 0:n].unsqueeze(2)
        p.recip(inv, total, last, *free)
        out = dst(b, t)[:, h0 * width:(h0 + n) * width].rearrange("p (h w) -> p h w", w=width)
        r = p.tt(p.dve, out, values, inv.to_broadcast([P, n, width]), ALU.mult)
        sums.done(slot, r)
        return r
    return store


def narrow(core, qsrc, ksrc, wq, wk, bq, bk, value_of, dst, ready, store=None):
    p = core.p
    qr = Ring([tmp(core, NSPREAD * S) for _ in range(2)])
    kr = Ring([tmp(core, NSPREAD * S) for _ in range(2)])
    vr = Ring([tmp(core, HALVES * H * (HD + 1)) for _ in range(2)])
    ones = [p.fill(p.pool, v.rearrange("p (n w) -> p n w", w=HD + 1)[:, :, HD:HD + 1], 1.0) for v in vr.bufs]
    held = {}

    def spread(src, w, bias, ring, b, n):
        buf, slot, free = ring.take()
        view = buf.rearrange("p (t s) -> p t s", s=S)
        out = []
        for t0 in range(0, NSPREAD, 2):
            bank, bs, bf = core.work.take()
            for j in range(2):
                m = p.mm(bank[:, j * S:(j + 1) * S], w[:, (t0 + j) * P:(t0 + j + 1) * P], src[:, b * S:(b + 1) * S],
                         True, True, *bf, *ready)
            bv = bank[:, :].rearrange("p (t s) -> p t s", s=S)
            if bias is None:
                e = p.cp(p.act, view[:, t0:t0 + 2, :], bv, m, *free, free=True)
            else:
                for j in range(2):
                    e = p.af(view[:, t0 + j, :], bv[:, j, :], ACT.Identity, m, *free, bias=bias[:, t0 + j:t0 + j + 1], free=True)
            core.work.done(bs, e)
            out.append(e)
        return view, slot, out

    def prepare(b):
        q, qs, qe = spread(qsrc, wq, bq, qr, b, 0)
        k, ks, ke = spread(ksrc, wk, bk, kr, b, 1)
        v, vs, vf = vr.take()
        vv = v.rearrange("p (t h w) -> p t h w", t=HALVES, w=HD + 1)
        ve = value_of(b, vv, vf)
        held[b] = (qs, ks, vs)

        def rows(h):
            g = h % (P // GROUP)
            return slice(GROUP * g, GROUP * g + HD + 1), h // (P // GROUP)
        return (Rows(q, rows), lambda h: k[rows(h)[0], rows(h)[1], :],
                lambda h, c: vv[:, c, h, :], [*qe, *ke, ve, *ones])

    def done(b, last):
        qs, ks, vs = held.pop(b)
        qr.done(qs, last)
        kr.done(ks, last)
        vr.done(vs, last)
    run_attention(core, H, HD, HD ** -0.5, prepare, store or divide(core, dst), done, in_rows=True)


def project_values(core, src, w, bias_bc, ready):
    p = core.p

    def value_of(b, vv, free):
        bank, bs, bf = core.work.take()
        for t in range(HALVES):
            m = p.mm(bank[:, t * P:(t + 1) * P], src[:, b * S + t * P:b * S + (t + 1) * P], w, True, True, *bf, *ready)
        e = p.tt(p.dve, vv[:, :, :, 0:HD], bank[:, 0:S].rearrange("p (t h w) -> p t h w", t=HALVES, w=HD),
                 bias_bc.rearrange("p (h w) -> p h w", w=HD).unsqueeze(1).to_broadcast([P, HALVES, H, HD]),
                 ALU.add, m, *free, free=True)
        core.work.done(bs, e)
        return e
    return value_of


def product_attention(core):
    p = core.p
    nt = pre_norm(core)
    O = core.XN
    wsum = tmp(core, 5 * D)
    names = ["a_q1", "a_q2", "a_k1", "a_k2", "a_v"]
    for n, name in enumerate(names):
        weff = p.tt(p.pool, wsum[:, n * D:(n + 1) * D], core.weights[name], core.weights["ident"], ALU.add,
                    core.came.l0, core.came.consts, free=True)
    bias = core.weights["a_bias_bc"]
    flatr = Ring([tmp(core, 4 * D) for _ in range(2)])
    kron = Ring([tmp(core, H * HW) for _ in range(2)])
    qr = Ring([tmp(core, NWIDE * S) for _ in range(2)])
    kr = Ring([tmp3(core, 2 * NWIDE * S) for _ in range(2)])
    vr = Ring([tmp(core, HALVES * H * (HD + 1)) for _ in range(2)])
    ones = [p.fill(p.pool, v.rearrange("p (n w) -> p n w", w=HD + 1)[:, :, HD:HD + 1], 1.0) for v in vr.bufs]
    held = {}

    def prepare(b):
        bufs = [r.take() for r in (qr, kr)]
        v, vs, vf = vr.take()
        vv = v.rearrange("p (t h w) -> p t h w", t=HALVES, w=HD + 1)
        ready = []
        for t in range(HALVES):
            i = b * HALVES + t
            x = core.XNT[:, i * P:(i + 1) * P]
            bank, bs, bf = core.work.take()
            m = p.mm(bank[:, :], x, wsum[:, 0:4 * D], True, True, *bf, weff, *nt)
            fl, fs, ff = flatr.take()
            e = p.tt(p.dve, fl, bank[:, :], bias[:, 0:4 * D], ALU.add, m, *ff, core.came.l0, free=True)
            core.work.done(bs, e)
            bank, bs, bf = core.work.take()
            m = p.mm(bank[:, 0:D], x, wsum[:, 4 * D:5 * D], True, True, *bf)
            ev = p.tt(p.dve, vv[:, t, :, 0:HD], bank[:, 0:D].rearrange("p (h w) -> p h w", w=HD),
                      bias[:, 4 * D:5 * D].rearrange("p (h w) -> p h w", w=HD), ALU.add, m, *vf, free=True)
            core.work.done(bs, ev)
            ready.append(ev)
            used = []
            for n, q in ((0, p.dve), (1, p.pool)):
                kb, kbs, kf = kron.take()
                a = fl[:, 2 * n * D:(2 * n + 1) * D].rearrange("p (h i) -> p h i", i=HD).unsqueeze(3).to_broadcast([P, H, HD, HD])
                c = fl[:, (2 * n + 1) * D:(2 * n + 2) * D].rearrange("p (h j) -> p h j", j=HD).unsqueeze(2).to_broadcast([P, H, HD, HD])
                o = p.tt(q, kb.rearrange("p (h i j) -> p h i j", i=HD, j=HD), a, c, ALU.mult, e, *kf)
                used.append(o)
                dst, _, df = bufs[n]
                dv = dst.rearrange("p (w s) -> p w s", s=S) if n == 0 else dst.rearrange("p (w o s) -> p o w s", o=2, s=S)
                for g in range(0, NWIDE, 4):
                    bank, bs, bf = core.work.take()
                    for j in range(4):
                        m = p.tr(bank[:, j * P:(j + 1) * P], kb[:, (g + j) * P:(g + j + 1) * P], core.weights["ident"], o, *bf)
                    bv = bank[:, :].rearrange("p (w s) -> p w s", s=P)
                    if n == 0:
                        ee = p.cp(p.act, dv[:, g:g + 4, t * P:(t + 1) * P], bv, m, *df, free=True)
                    else:
                        for o2, mask in enumerate(("lower", "upper")):
                            ee = p.af(dv[:, o2, g:g + 4, t * P:(t + 1) * P], bv, ACT.Copy, m, *df, scale=core.weights[mask], free=True)
                    core.work.done(bs, ee)
                    ready.append(ee)
                kron.done(kbs, m)
            flatr.done(fs, *used)
        q = bufs[0][0].rearrange("p (w s) -> p w s", s=S)
        k = bufs[1][0].rearrange("p (h s) -> p h s", s=S)
        held[b] = (bufs[0][1], bufs[1][1], vs)
        return (lambda h: q[:, h // 2, :], lambda h: k[:, h, :],
                lambda h, c: vv[:, c, h, :], [*ready, *ones])

    def done(b, last):
        for ring, slot in zip((qr, kr, vr), held.pop(b)):
            ring.done(slot, last)
    run_attention(core, H, HD, 1.0, prepare, divide(core, lambda b, t: O[:, b * HALVES + t, :]), done)
    n = normalise(core, O, O)
    g = transpose_all(core, lambda i: O[:, i, :], lambda q: core.XNT[:, q * BANK:(q + 1) * BANK], lambda i: n[i],
                  core.weights["a_g"], core.weights["a_b"])
    add_product(core, lambda c, i: core.XNT[:, i * P:(i + 1) * P], lambda c: core.weights["a_out"],
                     lambda i: [g[i // 4]], bias_bc=core.weights["a_bout_bc"])


def context_attention(core):
    p = core.p
    nt = pre_norm(core)
    O = tmp(core, NT * D).rearrange("p (i d) -> p i d", d=D)
    qr = Ring([tmp(core, S) for _ in range(2)])
    kr = Ring([tmp(core, S) for _ in range(2)])
    vr = Ring([tmp(core, HALVES * (D + 1)) for _ in range(2)])
    ones = [p.fill(p.pool, v.rearrange("p (n w) -> p n w", w=D + 1)[:, :, D:D + 1], 1.0) for v in vr.bufs]
    held = {}
    ready = [*nt, *core.ctx_in, core.came.l0]

    def prepare(b):
        out, slots, aps = [], [], []
        for ring, src, w, bias in ((qr, core.XNT, "x_wq", "x_bq"), (kr, core.CT, "x_wk", "x_bk")):
            buf, slot, free = ring.take()
            bank, bs, bf = core.work.take()
            m = p.mm(bank[:, 0:S], core.weights[w], src[:, b * S:(b + 1) * S], True, True, *bf, *ready)
            e = p.af(buf, bank[:, 0:S], ACT.Identity, m, *free, bias=core.weights[bias], free=True)
            core.work.done(bs, e)
            out.append(e)
            slots.append(slot)
            aps.append(buf)
        v, vs, vf = vr.take()
        vv = v.rearrange("p (t w) -> p t w", t=HALVES)
        bank, bs, bf = core.work.take()
        for t in range(HALVES):
            m = p.mm(bank[:, t * P:(t + 1) * P], core.CT[:, b * S + t * P:b * S + (t + 1) * P], core.weights["x_wv"], True, True, *bf)
        e = p.tt(p.dve, vv[:, :, 0:D], bank[:, 0:S].rearrange("p (t w) -> p t w", t=HALVES),
                 core.weights["x_bv_bc"].unsqueeze(1).to_broadcast([P, HALVES, D]), ALU.add, m, *vf, free=True)
        core.work.done(bs, e)
        held[b] = (*slots, vs)
        q, k = aps
        return lambda h: q, lambda h: k, lambda h, c: vv[:, c, :], [*out, e, *ones]

    def done(b, last):
        for ring, slot in zip((qr, kr, vr), held.pop(b)):
            ring.done(slot, last)
    run_attention(core, 1, D, 1.0 / 8.0, prepare, divide(core, lambda b, t: O[:, b * HALVES + t, :]), done)
    made = p.dve.steps[-1]
    g = transpose_all(core, lambda i: O[:, i, :], lambda q: core.XNT[:, q * BANK:(q + 1) * BANK], lambda i: made)
    act_in = Ring([tmp(core, BANK) for _ in range(2)])
    for n in range(QUARTERS):
        bank, slot, free = core.work.take()
        for j in range(4):
            i = 4 * n + j
            m = p.mm(bank[:, j * P:(j + 1) * P], core.XNT[:, i * P:(i + 1) * P], core.weights["x_wf"], True, True, *free, g[n])
        buf, bs, bf = act_in.take()
        bv = buf.rearrange("p (j d) -> p j d", d=D)
        a = p.tt(p.dve, bv, bank[:, :].rearrange("p (j d) -> p j d", d=D),
                 core.weights["x_bf_bc"].unsqueeze(1).to_broadcast([P, 4, D]), ALU.add, m, *bf)
        core.work.done(slot, a)
        e = p.af(buf, buf, ACT.Gelu, a)
        tiles = core.X[:, 4 * n:4 * n + 4, :]
        p.tt(p.dve, tiles, tiles, bv, ALU.add, e)
        r = p.tt(p.dve, tiles, tiles, core.CX[:, 4 * n:4 * n + 4, :], ALU.add)
        act_in.done(bs, r)


def sign_product(core):
    p = core.p
    nt = pre_norm(core)
    pos, sign = tmp(core, D), tmp(core, D)
    p.ts(p.dve, pos, core.weights["f_w"], 0.0, None, ALU.is_gt, None, core.came.l0)
    s = p.stt(p.dve, sign, core.weights["f_w"], 0.0, pos, ALU.is_lt, ALU.subtract)
    s = p.ts(p.dve, sign, sign, -1.0, None, ALU.mult, None)
    add_product(core, lambda c, i: core.XNT[:, i * P:(i + 1) * P], lambda c: sign, lambda i: [nt[i // 4], s])


def softplus(core, out, v, width, rows=P):
    p = core.p
    z, w, w2, s = (tmp(core, width)[0:rows, :] for _ in range(4))
    p.ts(p.dve, z, v, -1.0, None, ALU.mult, None)
    a = p.tt(p.dve, z, z, v, ALU.min)
    e = p.af(z, z, ACT.Exp, a)
    p.ts(p.dve, w, z, 2.0, None, ALU.add, None, e)
    p.recip(w, w)
    p.tt(p.dve, w, w, z, ALU.mult)
    p.tt(p.dve, w2, w, w, ALU.mult)
    p.ts(p.dve, s, w2, 1.0 / 17, None, ALU.mult, None)
    for n in (15, 13, 11, 9, 7, 5, 3):
        p.stt(p.dve, s, s, 1.0 / n, w2, ALU.add, ALU.mult)
    p.stt(p.dve, s, s, 1.0, w, ALU.add, ALU.mult)
    p.ts(p.dve, z, v, 0.0, None, ALU.max, None)
    return p.stt(p.dve, out, s, 2.0, z, ALU.mult, ALU.add)


def hybrid(core):
    p = core.p
    nt = pre_norm(core)
    O = tmp(core, NT * D).rearrange("p (i d) -> p i d", d=D)
    HT = tmp(core, T)
    r = mean_square(core, NT, lambda i: core.XN[:, i, :], D)
    for i in range(NT):
        n = p.ts(p.dve, O[:, i, :], core.XN[:, i, :], core.rs[:, i:i + 1], None, ALU.mult, None, r, free=i > 0)
    h = transpose_all(core, lambda i: O[:, i, :], lambda q: HT[:, q * BANK:(q + 1) * BANK], lambda i: n, core.weights["s_norm"])
    ready = [*h, core.came.l1]
    narrow(core, HT, HT, core.weights["s_wq"], core.weights["s_wk"], core.weights["s_bq"], core.weights["s_bk"],
                project_values(core, HT, core.weights["s_wv"], core.weights["s_bv_bc"], ready),
                lambda b, t: O[:, b * HALVES + t, :], ready)
    made = p.dve.steps[-1]
    g = transpose_all(core, lambda i: O[:, i, :], lambda q: HT[:, q * BANK:(q + 1) * BANK], lambda i: made)
    add_product(core, lambda c, i: HT[:, i * P:(i + 1) * P], lambda c: core.weights["s_wo"], lambda i: [g[i // 4]],
                     bias_bc=core.weights["s_bo_bc"], dst=core.XN)
    r = mean_square(core, NT, lambda i: core.XN[:, i, :], D)
    for i in range(NT):
        n = p.stt(p.dve, core.XN[:, i, :], core.XN[:, i, :], core.rs[:, i:i + 1], core.weights["s_normf_bc"],
                  ALU.mult, ALU.mult, r, free=i > 0)
    transpose_all(core, lambda i: core.XN[:, i, :], lambda q: core.XNT[:, q * BANK:(q + 1) * BANK], lambda i: n)
    for layer in range(M_LAYERS):
        stage(core)
        state_space(core, layer)
    stage(core)
    G = tmp(core, DFF // P * T).rearrange("p (c t) -> p c t", t=T)
    sg = Ring([tmp(core, BANK) for _ in range(2)])
    for c in range(DFF // P):
        for n in range(QUARTERS):
            gate, gs, gf = core.work.take()
            m = p.mm(gate[:, :], core.weights["s_fc1"][:, DFF + c * P:DFF + (c + 1) * P], core.XNT[:, n * BANK:(n + 1) * BANK],
                     True, True, *gf)
            buf, bs, bf = sg.take()
            e = p.af(buf, gate[:, :], ACT.Silu, m, *bf, free=True)
            core.work.done(gs, e)
            y, ys, yf = core.work.take()
            m = p.mm(y[:, :], core.weights["s_fc1"][:, c * P:(c + 1) * P], core.XNT[:, n * BANK:(n + 1) * BANK], True, True, *yf)
            ff = p.tt(p.dve, G[:, c, n * BANK:(n + 1) * BANK], y[:, :], buf, ALU.mult, m, e, free=True)
            core.work.done(ys, ff)
            sg.done(bs, ff)
    scaled = tmp(core, D)
    a = p.ts(p.pool, scaled, core.weights["ident"], ALPHA, None, ALU.mult, None)
    for n in range(QUARTERS):
        bank, slot, free = core.work.take()
        for j in range(4):
            i = 4 * n + j
            o = bank[:, j * P:(j + 1) * P]
            for c in range(DFF // P):
                p.mm(o, G[:, c, i * P:(i + 1) * P], core.weights["s_fc2"][:, c * D:(c + 1) * D], c == 0, False, ff, *free)
            m = p.mm(o, core.XNT[:, i * P:(i + 1) * P], scaled, False, True, a)
        e = p.cp(p.act, core.XN[:, 4 * n:4 * n + 4, :], bank[:, :].rearrange("p (j d) -> p j d", d=D), m)
        core.work.done(slot, e)
    r = mean_square(core, NT, lambda i: core.XN[:, i, :], D, e)
    for i in range(NT):
        n = p.stt(p.dve, core.XN[:, i, :], core.XN[:, i, :], core.rs[:, i:i + 1], core.weights["s_final_bc"],
                  ALU.mult, ALU.mult, r, free=i > 0)
    p.tt(p.dve, core.X[:, :, :], core.X[:, :, :], core.XN[:, :, :], ALU.add)


def state_space(core, layer):
    p = core.p
    w = lambda n: core.weights[f"m{layer}_{n}"]
    XC = tmp(core, CONV_CH * T).rearrange("p (c b s) -> p c b s", c=CONV_CH, s=S)
    Z = tmp(core, NT * D_INNER).rearrange("p (i z) -> p i z", z=D_INNER)
    dt = tmp(core, NT * H_SSM)
    a = tmp(core, NT * H_SSM)
    negA = tmp(core, H_SSM)
    mark = core.used
    bank, slot, free = core.work.take()
    for i in range(NT):
        m = p.mm(bank[:, i * H_SSM:(i + 1) * H_SSM], core.XNT[:, i * P:(i + 1) * P], w("dt"), True, True, *free,
                 core.came.mamba)
    dt3 = dt.rearrange("p (i h) -> p i h", h=H_SSM)
    e = p.tt(p.dve, dt3, bank[:, 0:NT * H_SSM].rearrange("p (i h) -> p i h", h=H_SSM),
             w("dtb").unsqueeze(1).to_broadcast([P, NT, H_SSM]), ALU.add, m)
    core.work.done(slot, e)
    softplus(core, dt, dt, NT * H_SSM)
    e = p.af(negA, w("alog"), ACT.Exp)
    a3 = a.rearrange("p (i h) -> p i h", h=H_SSM)
    p.stt(p.dve, a3, dt3, -1.0, negA.unsqueeze(1).to_broadcast([P, NT, H_SSM]), ALU.mult, ALU.mult, e)
    a_made = p.dve.steps[-1]
    core.used = mark
    pad = D_CONV - 1
    xp = Ring([tmp3(core, CONV_CH * (S + pad)) for _ in range(2)])
    conv = Ring([tmp3(core, CONV_CH * S) for _ in range(2)])
    zero = [p.fill(p.pool, x.rearrange("p (c s) -> p c s", c=CONV_CH)[:, :, 0:pad], 0.0, a_made) for x in xp.bufs]
    for b in range(B):
        x, xs, xf = xp.take()
        xv = x.rearrange("p (c s) -> p c s", c=CONV_CH)
        ev = []
        for c0 in range(0, CONV_CH, 2):
            bank, slot, free = core.work.take()
            for c in (c0, c0 + 1):
                m = p.mm(bank[:, (c - c0) * S:(c - c0 + 1) * S], w("xbc")[:, c * P:(c + 1) * P],
                         core.XNT[:, b * S:(b + 1) * S], True, True, *free)
            e = p.cp(p.act, xv[:, c0:c0 + 2, pad:pad + S], bank[:, :].rearrange("p (c s) -> p c s", s=S), m, a_made, *xf, free=True)
            core.work.done(slot, e)
            ev.append(e)
        y, ys, yf = conv.take()
        yv = y.rearrange("p (c s) -> p c s", c=CONV_CH)
        tap = lambda c, k: w("cw")[:, c * D_CONV + k:c * D_CONV + k + 1]
        for k in range(D_CONV):
            for c in range(CONV_CH):
                first = c == 0
                if k == 0:
                    o = p.ts(p.dve, yv[:, c, :], xv[:, c, 0:S], tap(c, 0), None, ALU.mult, None, ev[c // 2], *yf, *zero, free=not first)
                else:
                    o = p.stt(p.dve, yv[:, c, :], xv[:, c, k:k + S], tap(c, k), yv[:, c, :], ALU.mult, ALU.add,
                              free=not first)
        xp.done(xs, o)
        for c in range(CONV_CH):
            e = p.af(XC[:, c, b, :], yv[:, c, :], ACT.Silu, o, bias=w("cb")[:, c:c + 1], free=True)
        conv.done(ys, e)
        bank, slot, free = core.work.take()
        for t in range(HALVES):
            i = b * HALVES + t
            m = p.mm(bank[:, t * D_INNER:(t + 1) * D_INNER], core.XNT[:, i * P:(i + 1) * P], w("z"), True, True, *free)
        zc = p.af(Z[:, b * HALVES:(b + 1) * HALVES, :], bank[:, :].rearrange("p (t z) -> p t z", z=D_INNER), ACT.Silu, m, free=True)
        core.work.done(slot, zc)
    conv_made = zc
    core.used, core.used3 = mark, 0
    TRI = 3 * P
    early = Ring([core.XN[:, 8 * n:8 * n + 8, :].rearrange("p i d -> p (i d)") for n in range(2)])
    gm = Ring([tmp(core, TRI) for _ in range(2)])
    xt = Ring([tmp3(core, HALVES * D_INNER) for _ in range(2)])
    xd = Ring([tmp3(core, HALVES * D_INNER) for _ in range(2)])
    skip = Ring([tmp3(core, HALVES * D_INNER) for _ in range(2)])
    wt = Ring([tmp(core, TRI) for _ in range(2)])
    upto, ones = core.weights["upto"], core.weights["ones"]
    first = True
    for b in range(B):
        i0 = b * HALVES
        lead = [conv_made, p.dve.steps[-1]] if first else []
        el, es, ef = early.take()
        elv = el.rearrange("p (t h s) -> p t h s", t=HALVES, h=H_SSM)
        el_made = p.tt(p.pool, elv, core.weights["after"].unsqueeze(1).unsqueeze(1).to_broadcast([P, HALVES, H_SSM, P]),
                       a3[:, i0:i0 + HALVES, :].unsqueeze(3).to_broadcast([P, HALVES, H_SSM, P]), ALU.mult, *ef, *lead)
        bank, slot, free = core.work.take()
        BT, CTt = XC[:, 2, b, :], XC[:, 3, b, :]
        p.mm(bank[:, 0:S], BT[:, 0:P], CTt, True, True, conv_made, *free)
        m = p.mm(bank[:, S:TRI], BT[:, P:S], CTt[:, P:S], True, True)
        g, gs, gf = gm.take()
        p.tt(p.dve, g[:, 0:P], bank[:, 0:P], upto, ALU.mult, m, *gf, *lead)
        p.cp(p.dve, g[:, P:S], bank[:, P:S], free=True)
        g_made = p.tt(p.dve, g[:, S:TRI], bank[:, S:TRI], upto, ALU.mult, free=True)
        core.work.done(slot, g_made)
        bank, slot, free = core.work.take()
        for t in range(HALVES):
            for c in range(D_INNER // P):
                m = p.tr(bank[:, t * D_INNER + c * P:t * D_INNER + (c + 1) * P], XC[:, c, b, t * P:(t + 1) * P],
                         core.weights["ident"], conv_made, *free)
        xtb, xts, xtf = xt.take()
        xe = p.cp(p.act, xtb, bank[:, :], m, *xtf, *lead)
        core.work.done(slot, xe)
        v4 = lambda ap: ap.rearrange("p (t h w) -> p t h w", t=HALVES, h=H_SSM)
        xdb, xds, xdf = xd.take()
        xd_made = p.tt(p.pool, v4(xdb), v4(xtb), a_bc(dt3, i0), ALU.mult, xe, *xdf)
        sk, sks, skf = skip.take()
        sk_made = p.tt(p.pool, v4(sk), v4(xtb),
                       w("dskip_bc").unsqueeze(1).unsqueeze(3).to_broadcast([P, HALVES, H_SSM, HP]), ALU.mult, *skf)
        xt.done(xts, sk_made)
        out, oslot, ofree = core.acc.take()
        for h in range(H_SSM):
            bank, slot, free = core.work.take()
            p.mm(bank[:, 0:S], elv[:, 0, h, :], core.weights["upto2"], True, False, el_made, *free)
            p.mm(bank[:, P:S], a3[:, i0 + 1, h:h + 1].to_broadcast([P, P]), upto, False, True)
            m = p.mm(bank[:, S:TRI], elv[:, 1, h, :], upto, True, True)
            wb, ws, wf = wt.take()
            e = p.af(wb, bank[:, 0:TRI], ACT.Exp, m, *wf, *lead, free=not lead)
            core.work.done(slot, e)
            e = p.tt(p.dve, wb, wb, g, ALU.mult, e, g_made, free=True)
            xh = lambda t: xdb[:, t * D_INNER + h * HP:t * D_INNER + (h + 1) * HP]
            o = lambda t: out[:, t * D_INNER + h * HP:t * D_INNER + (h + 1) * HP]
            p.mm(o(0), wb[:, 0:P], xh(0), True, True, e, xd_made, *ofree)
            p.mm(o(1), wb[:, P:S], xh(0), True, False)
            m = p.mm(o(1), wb[:, S:TRI], xh(1), False, True)
            wt.done(ws, m)
        early.done(es, m)
        gm.done(gs, e)
        xd.done(xds, m)
        zb = Z[:, i0:i0 + HALVES, :]
        y3 = sk.rearrange("p (t z) -> p t z", t=HALVES)
        y = p.tt(p.dve, y3, out[:, :].rearrange("p (t z) -> p t z", t=HALVES), y3, ALU.add, m, sk_made)
        core.acc.done(oslot, y)
        y = p.tt(p.pool, zb, y3, zb, ALU.mult, y)
        skip.done(sks, y)
        first = False
    core.used = mark
    r = mean_square(core, NT, lambda i: Z[:, i, :], D_INNER, y)
    for i in range(NT):
        yn = p.ts(p.dve, Z[:, i, :], Z[:, i, :], core.rs[:, i:i + 1], None, ALU.mult, None, r, free=i > 0)
    yt = Ring([tmp(core, D_INNER // P * S) for _ in range(2)])
    for b in range(B):
        bank, slot, free = core.work.take()
        buf, bs, bf = yt.take()
        bv = buf.rearrange("p (c s) -> p c s", s=S)
        for c in range(D_INNER // P):
            for t in range(HALVES):
                m = p.tr(bank[:, c * S + t * P:c * S + (t + 1) * P], Z[:, b * HALVES + t, c * P:(c + 1) * P],
                         core.weights["ident"], yn, *free)
        for c in range(D_INNER // P):
            e = p.ts(p.dve, bv[:, c, :], bank[:, c * S:(c + 1) * S], w("norm")[:, c:c + 1], None, ALU.mult, None, m, *bf, m, free=True)
        core.work.done(slot, e)
        bank, slot, free = core.work.take()
        for c in range(D_INNER // P):
            m = p.mm(bank[:, 0:S], w("out")[:, c * D:(c + 1) * D], bv[:, c, :], c == 0, c == D_INNER // P - 1, e, *free)
        yt.done(bs, m)
        e = p.cp(p.act, core.XNT[:, b * S:(b + 1) * S], bank[:, 0:S], m)
        core.work.done(slot, e)


def raw_attention(core):
    p = core.p
    nt = pre_norm(core)
    O = tmp(core, NT * D).rearrange("p (i d) -> p i d", d=D)
    ready = [*nt, *core.ctx_in]

    def value_of(b, vv, free):
        return p.cp(p.pool, vv[:, :, :, 0:HD], core.CX[:, b * HALVES:(b + 1) * HALVES, :].rearrange("p t (h w) -> p t h w", w=HD),
                    *free, *ready)
    narrow(core, core.XNT, core.CT, core.weights["spread_id"], core.weights["spread_id"], None, core.weights["one_row"].to_broadcast([P, NSPREAD]), value_of,
                lambda b, t: O[:, b * HALVES + t, :], ready)
    made = p.dve.steps[-1]
    g = transpose_all(core, lambda i: O[:, i, :], lambda q: core.XNT[:, q * BANK:(q + 1) * BANK], lambda i: made)
    add_product(core, lambda c, i: core.XNT[:, i * P:(i + 1) * P], lambda c: core.weights["c_proj"], lambda i: [g[i // 4]],
                     bias_bc=core.weights["c_b_bc"])


def recurrence(core):
    p = core.p
    pre_norm(core)
    cell = Ring([tmp(core, S) for _ in range(2)])
    f, i_, g = (tmp(core, S) for _ in range(3))
    c, cs, _ = cell.take()
    made = p.cp(p.dve, c, core.weights["g_c0"].to_broadcast([P, S]), core.came.l1b)
    for b in range(B):
        ends = []
        for wn, un, bias, dst, func in (("g_wf", "g_uf", "g_bf", f, ACT.Sigmoid), ("g_wi", "g_ui", "g_bi", i_, ACT.Sigmoid),
                                        ("g_wc", "g_uc", "g_bc", g, ACT.Tanh)):
            bank, slot, free = core.work.take()
            p.mm(bank[:, 0:S], core.weights[wn], core.XNT[:, b * S:(b + 1) * S], True, False, *free, *p.act.steps[-1:],
                 *p.dve.steps[-1:])
            m = p.mm(bank[:, 0:S], core.weights[un], c, False, True, made)
            e = p.af(dst, bank[:, 0:S], func, m, made, bias=core.weights[bias], free=True)
            core.work.done(slot, e)
            ends.append(e)
        n, ns, _ = cell.take()
        p.tt(p.dve, n, f, c, ALU.mult, *ends)
        p.tt(p.dve, i_, i_, g, ALU.mult)
        made = p.tt(p.dve, n, n, i_, ALU.add)
        cell.done(cs, made)
        c, cs = n, ns
    out = Ring([tmp(core, BANK) for _ in range(2)])
    for n in range(QUARTERS):
        bank, slot, free = core.work.take()
        for j in range(4):
            i = 4 * n + j
            o = bank[:, j * P:(j + 1) * P]
            p.mm(o, core.XNT[:, i * P:(i + 1) * P], core.weights["g_wo"], True, False, *free)
            m = p.mm(o, c[:, (i % HALVES) * P:(i % HALVES + 1) * P], core.weights["g_uo"], False, True, made)
        buf, bs, bf = out.take()
        bv = buf.rearrange("p (j d) -> p j d", d=D)
        a = p.tt(p.dve, bv, bank[:, :].rearrange("p (j d) -> p j d", d=D),
                 core.weights["g_bo_bc"].unsqueeze(1).to_broadcast([P, 4, D]), ALU.add, m, *bf)
        core.work.done(slot, a)
        e = p.af(buf, buf, ACT.Tanh, a)
        tiles = core.X[:, 4 * n:4 * n + 4, :]
        r = p.tt(p.dve, tiles, tiles, bv, ALU.add, e)
        out.done(bs, r)


def time_mixing(core):
    p = core.p
    normalise(core, core.X, core.XN)
    PADDED = S + 1
    HT = tmp(core, B * PADDED).rearrange("p (b s) -> p b s", s=PADDED)
    zero = p.fill(p.pool, HT[:, :, 0:1], 0.0)
    O = tmp(core, NT * D).rearrange("p (i d) -> p i d", d=D)
    folded = {}
    for name, mix, cols in (("r_wk", "r_mk", D), ("r_wv", "r_mv", D), ("r_wr", "r_mr", D), ("r_wkc", "r_ck", 4 * D),
                            ("r_wrc", "r_cr", D)):
        now, prev, less = tmp2(core, cols), tmp2(core, cols), tmp2(core, 1)
        p.ts(p.pool, less, core.weights[mix], -1.0, 1.0, ALU.mult, ALU.add, core.came.l2)
        p.ts(p.pool, now, core.weights[name], core.weights[mix], None, ALU.mult, None)
        made = p.ts(p.pool, prev, core.weights[name], less, None, ALU.mult, None)
        folded[name] = (now, prev, made)

    def affine_turn(src, n, gname, bname):
        out = []
        for q in range(QUARTERS):
            bank, slot, free = core.work.take()
            for j in range(4):
                i = 4 * q + j
                m = p.tr(bank[:, j * P:(j + 1) * P], src[:, i, :], core.weights["ident"], n, *free)
            e = p.ts(p.dve, HT[:, 2 * q:2 * q + 2, 1:PADDED], bank[:, :].rearrange("p (b s) -> p b s", s=S),
                     core.weights[gname], core.weights[bname], ALU.mult, ALU.add, m, free=True)
            core.work.done(slot, e)
            out.append(e)
        return out
    n = normalise(core, core.XN, O)[-1]
    h = affine_turn(O, n, "r_g1", "r_b1")
    HALF = B // 2
    N = HALF * S
    mark = core.used
    k, v, r, pm, d, c, m_, num = (tmp(core, N) for _ in range(8))
    b3 = lambda ap: ap.rearrange("p (b s) -> p b s", s=S)
    pads = [tmp2(core, HALF * PADDED) for _ in range(3)]
    pmp, sp, aap = (x.rearrange("p (b s) -> p b s", s=PADDED) for x in pads)
    p.fill(p.pool, pmp[:, :, 0:1], BEFORE_ALL)
    p.fill(p.pool, sp[:, :, 0:1], 0.0)
    z = p.fill(p.pool, aap[:, :, 0:1], 0.0)
    last_use = []
    for half in range(2):
        b0 = half * HALF
        for name, dst, func in (("r_wk", k, ACT.Copy), ("r_wv", v, ACT.Copy), ("r_wr", r, ACT.Sigmoid)):
            now, prev, made = folded[name]
            for n2 in range(N // BANK):
                bb = b0 + 2 * n2
                bank, slot, free = core.work.take()
                p.mm(bank[:, :], now, HT[:, bb:bb + 2, 1:PADDED], True, False, *free, made, zero, *h)
                m = p.mm(bank[:, :], prev, HT[:, bb:bb + 2, 0:S], False, True)
                e = p.af(dst[:, n2 * BANK:(n2 + 1) * BANK], bank[:, :], func, m, *last_use, free=True)
                core.work.done(slot, e)
        proj = e
        k3, v3 = b3(k), b3(v)
        P1, S1, A1 = pmp[:, :, 1:PADDED], sp[:, :, 1:PADDED], aap[:, :, 1:PADDED]
        P0, S0, A0 = pmp[:, :, 0:S], sp[:, :, 0:S], aap[:, :, 0:S]
        for j in range(HALF):
            p.scan(pmp[:, j, 1:PADDED], k3[:, j, :], k3[:, j, :], BEFORE_ALL, ALU.max, ALU.max, proj, z, free=j > 0)
        p.tt(p.dve, b3(d), P0, P1, ALU.subtract)
        a = p.tt(p.dve, b3(c), k3, P1, ALU.subtract)
        p.af(d, d, ACT.Exp, a)
        e = p.af(c, c, ACT.Exp)
        for j in range(HALF):
            p.scan(sp[:, j, 1:PADDED], b3(d)[:, j, :], b3(c)[:, j, :], 0.0, ALU.mult, ALU.add, e, free=j > 0)
        p.tt(p.dve, b3(m_), b3(d), S0, ALU.mult)
        p.tt(p.dve, m_, m_, c, ALU.max)
        p.stt(p.dve, c, m_, 1e-8, c, ALU.mult, ALU.add)
        for j in range(HALF):
            s = p.scan(sp[:, j, 1:PADDED], b3(d)[:, j, :], b3(c)[:, j, :], 0.0, ALU.mult, ALU.add, free=j > 0)
        e = p.af(b3(m_), S1, ACT.Ln, s)
        p.tt(p.dve, P1, P1, b3(m_), ALU.add, e)
        p.tt(p.dve, b3(m_), P0, k3, ALU.max)
        p.tt(p.dve, b3(d), P0, b3(m_), ALU.subtract)
        a = p.tt(p.dve, c, k, m_, ALU.subtract)
        p.af(d, d, ACT.Exp, a)
        e = p.af(c, c, ACT.Exp)
        p.tt(p.dve, c, c, v, ALU.mult, e)
        for j in range(HALF):
            p.scan(aap[:, j, 1:PADDED], b3(d)[:, j, :], b3(c)[:, j, :], 0.0, ALU.mult, ALU.add, free=j > 0)
        p.ts(p.dve, k, k, core.weights["r_u"], None, ALU.add, None)
        p.tt(p.dve, b3(m_), P0, k3, ALU.max)
        p.tt(p.dve, b3(d), P0, b3(m_), ALU.subtract)
        a = p.tt(p.dve, c, k, m_, ALU.subtract)
        p.af(d, d, ACT.Exp, a)
        e = p.af(c, c, ACT.Exp)
        p.tt(p.dve, b3(num), b3(d), A0, ALU.mult, e)
        p.tt(p.dve, v, v, c, ALU.mult)
        p.tt(p.dve, num, num, v, ALU.add)
        p.stt(p.dve, d, d, 1e-8, c, ALU.add, ALU.add)
        p.recip(d, d)
        p.tt(p.dve, num, num, d, ALU.mult)
        o = p.tt(p.dve, num, num, r, ALU.mult)
        for n2 in range(N // BANK):
            bank, slot, free = core.work.take()
            for j in range(4):
                m = p.tr(bank[:, j * P:(j + 1) * P], num[:, n2 * BANK + j * P:n2 * BANK + (j + 1) * P], core.weights["ident"], o, *free)
            i = b0 * HALVES + 4 * n2
            xn = core.XN[:, i:i + 4, :]
            e = p.tt(p.dve, xn, xn, bank[:, :].rearrange("p (j d) -> p j d", d=D), ALU.add, m, free=True)
            core.work.done(slot, e)
        last_use = [e]
    core.used = mark
    n = normalise(core, core.XN, O)[-1]
    h = affine_turn(O, n, "r_g2", "r_b2")
    KC = Ring([tmp(core, 4 * BANK) for _ in range(2)])
    RC = Ring([tmp(core, BANK) for _ in range(2)])
    now, prev, made = folded["r_wkc"]
    rnow, rprev, rmade = folded["r_wrc"]
    for q in range(QUARTERS):
        kc, ks, kf = KC.take()
        for g in range(4):
            bank, slot, free = core.work.take()
            p.mm(bank[:, :], now[:, g * P:(g + 1) * P], HT[:, 2 * q:2 * q + 2, 1:PADDED], True, False, *free, made, *h)
            m = p.mm(bank[:, :], prev[:, g * P:(g + 1) * P], HT[:, 2 * q:2 * q + 2, 0:S], False, True)
            kg = kc[:, g * BANK:(g + 1) * BANK]
            a = p.af(kg, bank[:, :], ACT.Relu, m, *kf, *h, free=True)
            core.work.done(slot, a)
            sq = p.tt(p.pool, kg, kg, kg, ALU.mult, a, free=True)
        vb, vs, vf = core.work.take()
        rb, rs_, rf = core.work.take()
        for j in range(4):
            bb, s0 = 2 * q + j // 2, (j % 2) * P
            for g in range(4):
                m = p.mm(vb[:, j * P:(j + 1) * P], kc[:, g * BANK + j * P:g * BANK + (j + 1) * P],
                         core.weights["r_wvc"][:, g * D:(g + 1) * D], g == 0, g == 3, sq, *vf)
            p.mm(rb[:, j * P:(j + 1) * P], HT[:, bb, 1 + s0:1 + s0 + P], rnow, True, False, *rf, rmade)
            m = p.mm(rb[:, j * P:(j + 1) * P], HT[:, bb, s0:s0 + P], rprev, False, True)
        KC.done(ks, m)
        rc, rcs, rcf = RC.take()
        e = p.af(rc, rb[:, :], ACT.Sigmoid, m, *rcf, free=True)
        core.work.done(rs_, e)
        x = p.tt(p.dve, rc, rc, vb[:, :], ALU.mult, e, m)
        core.work.done(vs, x)
        tiles, xn = core.X[:, 4 * q:4 * q + 4, :], core.XN[:, 4 * q:4 * q + 4, :]
        p.tt(p.pool, tiles, tiles, xn, ALU.add)
        x = p.tt(p.dve, tiles, tiles, rc.rearrange("p (j d) -> p j d", d=D), ALU.add, p.pool.steps[-1])
        RC.done(rcs, x)


def wide_attention(core):
    p = core.p
    nt = pre_norm(core)
    SCALE = HW ** -0.5
    qr = Ring([tmp(core, NWIDE * S) for _ in range(2)])
    kr = Ring([tmp2(core, 2 * NWIDE * S) for _ in range(2)])
    vr = Ring([tmp(core, HALVES * H * (HW + 1))])
    ones = [p.fill(p.pool, v.rearrange("p (n w) -> p n w", w=HW + 1)[:, :, HW:HW + 1], 1.0) for v in vr.bufs]
    lens_i = tmp(core, B)
    lens = tmp(core, B)
    got = p.dma(lens_i.bitcast(mybir.dt.int32), core.lens_dram)
    p.cp(p.dve, lens, lens_i.bitcast(mybir.dt.int32), got)
    rowm = tmp(core, B * S, BF16).rearrange("p (b s) -> p b s", s=S)
    colm = tmp(core, B * HALVES).rearrange("p (b t) -> p b t", t=HALVES)
    keep = tmp(core, B * S, BF16).rearrange("p (b s) -> p b s", s=S)
    beyond = tmp(core, S)
    steps = core.weights["steps"]
    for b in range(B):
        p.ts(p.dve, keep[:, b, :], steps, lens[:, b:b + 1], None, ALU.is_lt, None)
        p.ts(p.dve, beyond, steps, lens[:, b:b + 1], core.weights["neg_parts"], ALU.is_ge, ALU.mult)
        p.cp(p.dve, rowm[:, b, :], beyond)
        masks = p.ts(p.dve, colm[:, b, :], core.weights["w_pos"], lens[:, b:b + 1], NEG_INF, ALU.is_ge, ALU.mult, core.came.l2x)
    masked = {"row": lambda b: rowm[:, b, :].unsqueeze(1).to_broadcast([P, BANK // S, S]), "ready": [masks, *core.const_ready],
              "column": lambda b, c: colm[:, b, c:c + 1]}
    raw = Ring([core.XN[:, 8 * n:8 * n + 8, :].rearrange("p i d -> p (i d)") for n in range(2)])
    sq = Ring([tmp2(core, H * HW)])
    ms = Ring([tmp(core, H) for _ in range(2)])
    otr = Ring([tmp2(core, NWIDE * P) for _ in range(1)])
    held = {}
    ready0 = [*nt, *core.ctx_in, core.came.l2x, masks, *ones]

    def heads_of(src, wname, norm, ring, b, keys):
        buf, slot, free = ring.take()
        view = buf.rearrange("p (w o s) -> p o w s", o=2, s=S) if keys else buf.rearrange("p (w s) -> p w s", s=S)
        out = []
        for t in range(HALVES):
            x, xs, xf = raw.take()
            s2, ss, sf = sq.take()
            for n in range(H * HW // BANK):
                bank, bs, bf = core.work.take()
                cols = slice(n * BANK, (n + 1) * BANK)
                m = p.mm(bank[:, :], src[:, b * S + t * P:b * S + (t + 1) * P], core.weights[wname][:, cols], True, True, *bf, *ready0)
                e = p.cp(p.act, x[:, cols], bank[:, :], m, *xf, free=True)
                core.work.done(bs, e)
            s_ = p.tt(p.pool, s2, x, x, ALU.mult, e, *sf)
            r, rs_, rf = ms.take()
            a = p.red(r, s2.rearrange("p (h w) -> p h w", w=HW), ALU.add, s_, *rf)
            sq.done(ss, a)
            p.ts(p.dve, r, r, 1.0 / HW, 1e-5, ALU.mult, ALU.add)
            a = p.dve.steps[-1]
            a = p.af(r, r, ACT.Sqrt, a)
            p.recip(r, r, a)
            x3 = x.rearrange("p (h w) -> p h w", w=HW)
            o = p.tt(p.dve, x3, x3, r.unsqueeze(2).to_broadcast([P, H, HW]), ALU.mult)
            ms.done(rs_, o)
            for g in range(0, NWIDE, 4):
                bank, bs, bf = core.work.take()
                for j in range(4):
                    m = p.tr(bank[:, j * P:(j + 1) * P], x[:, (g + j) * P:(g + j + 1) * P], core.weights["ident"], o, *bf)
                bv = bank[:, :].rearrange("p (w s) -> p w s", s=P)
                if keys:
                    for o2 in range(2):
                        e = p.stt(p.dve, view[:, o2, g:g + 4, t * P:(t + 1) * P], bv, core.weights[norm][:, o2:o2 + 1],
                                  keep[:, b, t * P:(t + 1) * P].unsqueeze(1).to_broadcast([P, 4, P]),
                                  ALU.mult, ALU.mult, m, *free, free=True)
                else:
                    e = p.af(view[:, g:g + 4, t * P:(t + 1) * P], bv, ACT.Copy, m, *free, scale=core.weights[norm], free=True)
                core.work.done(bs, e)
                out.append(e)
            raw.done(xs, m)
        return view, slot, out

    def prepare(b):
        q, qs, qe = heads_of(core.XNT, "w_q", "w_qn", qr, b, False)
        k, ks, ke = heads_of(core.CT, "w_k", "w_kn", kr, b, True)
        held[b] = [qs, ks, None]
        v = vr.bufs[0].rearrange("p (t h w) -> p t h w", t=HALVES, w=HW + 1)

        k = kr.bufs[ks].rearrange("p (h s) -> p h s", s=S)
        return (lambda h: q[:, h // 2, :], lambda h: k[:, h, :],
                lambda h, c: v[:, c, h, :], [*qe, *ke, *ones])
    O = Ring([tmp(core, H * HW) for _ in range(HALVES)])
    outs = {}
    base_store = divide(core, lambda b, t: outs[(b, t)][0])

    def store(b, t, h0, n, values, total, last):
        if h0 == 0:
            buf, slot, free = O.take()
            outs[(b, t)] = (buf, slot)
            p.dve.pending = list(free)
        r = base_store(b, t, h0, n, values, total, last)
        if h0 + n == H:
            buf, slot = outs.pop((b, t))
            ot, os_, of = otr.take()
            for g in range(0, NWIDE, 4):
                bank, bs, bf = core.work.take()
                for j in range(4):
                    m = p.tr(bank[:, j * P:(j + 1) * P], buf[:, (g + j) * P:(g + j + 1) * P], core.weights["ident"], r, *bf)
                e = p.cp(p.act, ot[:, g * P:(g + 4) * P], bank[:, :], m, *of, free=True)
                core.work.done(bs, e)
            O.done(slot, m)
            bank, bs, bf = core.work.take()
            for w in range(NWIDE):
                m = p.mm(bank[:, 0:D], ot[:, w * P:(w + 1) * P], core.weights["w_o"][:, w * D:(w + 1) * D], w == 0, w == NWIDE - 1, e, *bf)
            otr.done(os_, m)
            x = core.X[:, b * HALVES + t, :]
            e = p.tt(p.dve, x, x, bank[:, 0:D], ALU.add, m)
            core.work.done(bs, e)
        return r

    def values_now(b):
        v, vs, vf = vr.take()
        vv = v.rearrange("p (t h w) -> p t h w", t=HALVES, w=HW + 1)
        for t in range(HALVES):
            for n in range(H * HW // BANK):
                bank, bs, bf = core.work.take()
                m = p.mm(bank[:, :], core.CT[:, b * S + t * P:b * S + (t + 1) * P], core.weights["w_v"][:, n * BANK:(n + 1) * BANK],
                         True, True, *bf, *ready0)
                e = p.cp(p.act, vv[:, t, n * 8:(n + 1) * 8, 0:HW], bank[:, :].rearrange("p (h w) -> p h w", w=HW), m, *vf, free=True)
                core.work.done(bs, e)
        held[b][2] = vs
        return e

    def done(b, last):
        qs, ks, vs = held.pop(b)
        qr.done(qs, last)
        kr.done(ks, last)
        vr.done(vs, last)
    core.before_weigh = values_now
    run_attention(core, H, HW, SCALE, prepare, store, done, masked)
    core.before_weigh = None


def route(core, wr, floor):
    p = core.p
    N = NT * E8
    e3 = lambda ap: ap.rearrange("p (i e) -> p i e", e=E8)
    pr, sel, wgt, m, s = tmp(core, N), tmp(core, N), tmp(core, N), tmp(core, NT), tmp(core, NT)
    bank, slot, free = core.work.take()
    for i in range(NT):
        k = p.mm(bank[:, i * E8:(i + 1) * E8], core.XNT[:, i * P:(i + 1) * P], wr, True, True, *free)
    bc = lambda ap: ap.unsqueeze(2).to_broadcast([P, NT, E8])
    p.red(m, e3(bank[:, 0:N]), ALU.max, k)
    a = p.tt(p.dve, e3(pr), e3(bank[:, 0:N]), bc(m), ALU.subtract)
    core.work.done(slot, a)
    e = p.af(pr, pr, ACT.Exp, a)
    p.red(s, e3(pr), ALU.add, e)
    p.recip(s, s)
    p.tt(p.dve, e3(pr), e3(pr), bc(s), ALU.mult)
    cmp_ = tmp(core, N * E8).rearrange("p (i e j) -> p i e j", e=E8, j=E8)
    eq = tmp(core, N * E8).rearrange("p (i e j) -> p i e j", e=E8, j=E8)
    pj = e3(pr).unsqueeze(2).to_broadcast([P, NT, E8, E8])
    pe_ = e3(pr).unsqueeze(3).to_broadcast([P, NT, E8, E8])
    p.tt(p.dve, cmp_, pj, pe_, ALU.is_gt)
    p.tt(p.dve, eq, pj, pe_, ALU.is_equal)
    before = core.weights["before"].rearrange("p (e j) -> p e j", j=E8).unsqueeze(1).to_broadcast([P, NT, E8, E8])
    p.tt(p.dve, eq, eq, before, ALU.mult)
    p.tt(p.dve, cmp_, cmp_, eq, ALU.add)
    p.red(e3(sel), cmp_, ALU.add)
    p.ts(p.dve, sel, sel, 2.0, None, ALU.is_lt, None)
    p.tt(p.dve, wgt, sel, pr, ALU.mult)
    p.red(s, e3(wgt), ALU.add)
    p.ts(p.dve, s, s, 1e-9, None, floor, None)
    p.recip(s, s)
    r = p.tt(p.dve, e3(wgt), e3(wgt), bc(s), ALU.mult)
    return e3(sel), e3(wgt), r


def expert(core, width, w1, b1, w2, func, weight, Y, first, ready, hid):
    p = core.p
    chunks = width // P
    for n in range(QUARTERS):
        buf, bs, bf = hid.take()
        ev = []
        for c in range(chunks):
            bank, slot, free = core.work.take()
            m = p.mm(bank[:, :], w1[:, c * P:(c + 1) * P], core.XNT[:, n * BANK:(n + 1) * BANK], True, True, *free, *ready)
            h = buf[:, c * BANK:(c + 1) * BANK]
            if func is ACT.Relu and c % 2:
                e = p.ts(p.dve, h, bank[:, :], b1[:, c:c + 1], 0.0, ALU.add, ALU.max, m, *bf, free=True)
            else:
                e = p.af(h, bank[:, :], func, m, *bf, bias=b1[:, c:c + 1], free=True)
            core.work.done(slot, e)
            ev.append(e)
        bank, slot, free = core.acc.take()
        for j in range(4):
            for c in range(chunks):
                m = p.mm(bank[:, j * P:(j + 1) * P], buf[:, c * BANK + j * P:c * BANK + (j + 1) * P],
                         w2[:, c * D:(c + 1) * D], c == 0, c == chunks - 1, *free, *ev)
        hid.done(bs, m)
        for j in range(4):
            i = 4 * n + j
            y = Y[:, i, :]
            e = p.stt(p.dve, y, bank[:, j * P:(j + 1) * P], weight(i), y, ALU.mult, ALU.add, m, *first, free=j > 0)
        core.acc.done(slot, e)


def expert_biases(core, wgt, made, b2, Y, ready):
    p = core.p
    wt = tmp(core, T)
    for n in range(QUARTERS):
        bank, slot, free = core.work.take()
        for j in range(4):
            m = p.tr(bank[0:E8, j * P:(j + 1) * P], wgt[:, 4 * n + j, :], core.weights["ident"], made, *free)
        e = p.cp(p.act, wt[0:E8, n * BANK:(n + 1) * BANK], bank[0:E8, :], m, free=True)
        core.work.done(slot, e)
    out = []
    for n in range(QUARTERS):
        bank, slot, free = core.work.take()
        for j in range(4):
            i = 4 * n + j
            m = p.mm(bank[:, j * P:(j + 1) * P], wt[0:E8, i * P:(i + 1) * P], b2[0:E8, :], True, True, e, *free, *ready)
        y = Y[:, 4 * n:4 * n + 4, :]
        e2 = p.tt(p.dve, y, y, bank[:, :].rearrange("p (j d) -> p j d", d=D), ALU.add, m)
        core.work.done(slot, e2)
    return e2


def mixture(core):
    p = core.p
    nt = pre_norm(core)
    p.pe.pending = [*nt, core.came.l2f]
    sel, wgt, made = route(core, core.weights["e_wg"], ALU.add)
    hid = Ring([tmp(core, MOE2_H // P * BANK) for _ in range(2)])
    y = expert_biases(core, wgt, made, core.weights["e_b2"], core.X, [])
    C = MOE2_H // P
    for e in range(E8):
        expert(core, MOE2_H, core.weights["e_w1"][:, e * MOE2_H:(e + 1) * MOE2_H], core.weights["e_b1"][:, e * C:(e + 1) * C],
                    core.weights["e_w2"][:, e * C * D:(e + 1) * C * D], ACT.Relu, lambda i: wgt[:, i, e:e + 1], core.X, [y],
                    [], hid)


def wave_kernels(core):
    p = core.p
    got = core.came.l3a
    col = lambda n: core.weights[n][0:H, :]
    t = core.weights["steps"][0:H, :]
    alpha, damp = tmp(core, 1)[0:H, :], tmp(core, 1)[0:H, :]
    p.cp(p.dve, damp, col("v_damp"), got)
    a = softplus(core, alpha, damp, 1, H)
    p.ts(p.dve, alpha, alpha, -1.0, None, ALU.mult, None)
    env, arg, n, ker, s = tmp(core, S)[0:H, :], tmp(core, S)[0:H, :], tmp(core, S)[0:H, :], core.kern[:, :], tmp(core, 1)[0:H, :]
    a = p.dve.steps[-1]
    e = p.af(env, t, ACT.Exp, a, scale=alpha)
    p.ts(p.dve, arg, t, col("v_freq"), col("v_phase"), ALU.mult, ALU.add)
    ROUND = 12582912.0
    p.ts(p.dve, n, arg, 1.0 / (2 * np.pi), 0.25, ALU.mult, ALU.add)
    p.ts(p.dve, n, n, ROUND, None, ALU.add, None)
    p.ts(p.dve, n, n, -ROUND, None, ALU.add, None)
    c1 = 6.28125
    c2 = float(np.float32(np.round((2 * np.pi - c1) * 2 ** 21) / 2 ** 21))
    c3 = float(2 * np.pi - c1 - c2)
    for c in (c1, c2, c3):
        p.stt(p.dve, arg, n, -c, arg, ALU.mult, ALU.add)
    top = float(np.nextafter(np.float32(np.pi), np.float32(0)))
    p.ts(p.dve, arg, arg, float(np.pi / 2), top, ALU.add, ALU.min)
    a = p.ts(p.dve, arg, arg, -top, None, ALU.max, None)
    e2 = p.af(arg, arg, ACT.Sin, a)
    p.tt(p.dve, ker, env, arg, ALU.mult, e, e2)
    p.red(s, ker, ALU.add, mag=True)
    p.ts(p.dve, s, s, 1e-8, None, ALU.max, None)
    p.recip(s, s)
    k = p.ts(p.dve, ker, ker, s, None, ALU.mult, None)
    zero = core.kern_zero[:, :]
    z = p.fill(p.pool, zero, 0.0)
    core.kern_out = [p.dma(core.kern_dram[:, P:P + S], ker, k), p.dma(core.kern_dram[:, 0:P], zero, z)]


def wave(core):
    p = core.p
    nt = pre_norm(core)
    T0 = tmp3(core, H * S).rearrange("p (h s) -> p h s", s=S)
    T1 = tmp3(core, H * P).rearrange("p (h s) -> p h s", s=P)
    kd = core.kern_dram
    diag = lambda parts, shift, n: diagonals(kd, parts, 1 + shift, n)
    there = [*core.kern_out, core.came.l2x, core.came.l2f]
    toe = [p.dma(T0[:, :, :], diag(P, 0, S), *there),
           p.dma(T1[1:P, :, :], diag(P - 1, 1, P), *there),
           p.dma(T1[0:1, :, :], diag(1, 1, P), *there)]
    p.cp(p.pool, T0[:, :, S - 1:S], T0[:, :, S - 2:S - 1], *toe)
    toe = p.cp(p.pool, T1[:, :, P - 1:P], T1[:, :, P - 2:P - 1])
    turned = tmp(core, T)
    by_tile = lambda a: a.rearrange("p (i n) -> p i n", n=P)
    turn = p.cp(p.dve, by_tile(turned), backwards(by_tile(core.XNT[:, :])), *nt)
    F = tmp(core, NT * D).rearrange("p (i d) -> p i d", d=D)
    t1 = Ring([tmp(core, 2 * BANK) for _ in range(2)])
    t2 = Ring([tmp(core, BANK) for _ in range(2)])
    wl = core.came.l3a
    for q in range(NT // 2):
        bank, slot, free = core.work.take()
        for j in range(2):
            i = 2 * q + j
            for n, w in enumerate(("v_wk", "v_wv")):
                m = p.mm(bank[:, n * 2 * P + j * P:n * 2 * P + (j + 1) * P], turned[:, i * P:(i + 1) * P], core.weights[w], True, True, *free, turn, wl)
        kv, ks, kf = t1.take()
        e = p.tt(p.dve, kv[:, 0:BANK].rearrange("p (n j d) -> p n j d", n=2, d=D), bank[:, :].rearrange("p (n j d) -> p n j d", n=2, d=D),
                 core.weights["v_bkv_bc"].rearrange("p (n d) -> p n d", d=D).unsqueeze(2).to_broadcast([P, 2, 2, D]), ALU.add, m, *kf)
        core.work.done(slot, e)
        k, v = kv[:, 0:2 * P], kv[:, 2 * P:4 * P]
        x = kv[:, BANK:BANK + 2 * P]
        a = p.ts(p.dve, x, k, 0.0, None, ALU.min, None)
        e = p.af(x, x, ACT.Exp, a)
        p.stt(p.dve, x, k, 0.0, x, ALU.max, ALU.add, e)
        f = p.tt(p.dve, F[:, 2 * q:2 * q + 2, :], x.rearrange("p (j d) -> p j d", d=D), v.rearrange("p (j d) -> p j d", d=D), ALU.mult)
        t1.done(ks, f)
    Fv = F.rearrange("p (b t) (h d) -> p b t h d", t=HALVES, d=HD)
    CV = tmp(core, NT * D).rearrange("p (i d) -> p i d", d=D)
    CVv = CV.rearrange("p (b t) (h d) -> p t h b d", t=HALVES, d=HD)
    for t in range(HALVES):
        for h0 in range(0, H, 8):
            bank, slot, free = core.work.take()
            for h in range(h0, h0 + 8):
                o = bank[:, (h - h0) * HW:(h - h0 + 1) * HW].rearrange("p (b d) -> p b d", d=HD)
                m = p.mm(o, T0[:, h, t * P:(t + 1) * P], Fv[:, :, 0, h, :], True, t == 0, *free, toe, f)
                if t:
                    m = p.mm(o, T1[:, h, :], Fv[:, :, 1, h, :], False, True)
            q = alternate(p, h0 // 8)
            e = p.cp(q, CVv[:, t, h0:h0 + 8, :, :], bank[:, :].rearrange("p (h b d) -> p h b d", h=8, d=HD), m)
            core.work.done(slot, e)
    convolved = [p.dve.steps[-1], p.act.steps[-1]]
    cp_, cm, ct = tmp(core, H)[0:H, :], tmp(core, 1)[0:H, :], tmp(core, H)[0:H, :]
    C = core.weights["v_coup"][0:H, :]
    p.red(cm, C, ALU.max)
    a = p.ts(p.dve, cp_, C, cm, None, ALU.subtract, None)
    e = p.af(cp_, cp_, ACT.Exp, a)
    p.red(cm, cp_, ALU.add, e)
    p.recip(cm, cm)
    a = p.ts(p.dve, cp_, cp_, cm, None, ALU.mult, None)
    bank, slot, free = core.work.take()
    m = p.tr(bank[0:H, 0:H], cp_, core.weights["ident"][0:H, 0:H], a, *free)
    e = p.cp(p.act, ct, bank[0:H, 0:H], m)
    core.work.done(slot, e)
    bank, slot, free = core.work.take()
    m = p.mm(bank[:, 0:H], core.weights["head_rows"][0:H, :], ct, True, True, e, *free)
    mix = tmp(core, D)
    u = tmp(core, H)
    e = p.cp(p.act, u, bank[:, 0:H], m)
    core.work.done(slot, e)
    mixed = p.tt(p.dve, mix.rearrange("p (i d) -> p i d", d=HD), u.unsqueeze(2).to_broadcast([P, H, HD]),
                 core.weights["same_d"].unsqueeze(1).to_broadcast([P, H, HD]), ALU.mult, e)
    CT_ = tmp(core, T)
    cv = transpose_all(core, lambda i: CV[:, i, :], lambda q: CT_[:, q * BANK:(q + 1) * BANK], lambda i: convolved[0])
    p.pe.pending = convolved
    G = tmp(core, T)
    for q in range(QUARTERS):
        cols = slice(q * BANK, (q + 1) * BANK)
        bank, slot, free = core.work.take()
        m = p.mm(bank[:, :], core.weights["v_wg"], core.XNT[:, cols], True, True, *free)
        e = p.af(G[:, cols], bank[:, :], ACT.Sigmoid, m, bias=core.weights["v_bg"], free=True)
        core.work.done(slot, e)
    for q in range(QUARTERS):
        cols = slice(q * BANK, (q + 1) * BANK)
        bank, slot, free = core.work.take()
        m = p.mm(bank[:, :], core.weights["v_wq"], core.XNT[:, cols], True, True, *free)
        kv, ks, kf = t1.take()
        x, y = kv[:, 0:BANK], kv[:, BANK:2 * BANK]
        p.ts(p.dve, x, bank[:, :], core.weights["v_bq"], 0.0, ALU.add, ALU.min, m, *kf)
        a = p.ts(p.dve, y, bank[:, :], core.weights["v_bq"], 0.0, ALU.add, ALU.max)
        core.work.done(slot, a)
        e2 = p.af(x, x, ACT.Exp, a)
        p.tt(p.dve, x, x, y, ALU.add, e2)
        g = p.tt(p.dve, G[:, cols], G[:, cols], x, ALU.mult, e)
        t1.done(ks, g)
        bank, slot, free = core.work.take()
        m = p.mm(bank[:, :], mix, CT_[:, cols], True, True, mixed, cv[q], *free)
        g = p.tt(p.dve, G[:, cols], G[:, cols], bank[:, :], ALU.mult, m)
        core.work.done(slot, g)
    add_product(core, lambda c, i: G[:, i * P:(i + 1) * P], lambda c: core.weights["v_wo"], lambda i: [g], bias_bc=core.weights["v_bo_bc"])


def guarded_attention(core):
    p = core.p
    nt = pre_norm(core)
    O = tmp(core, NT * D).rearrange("p (i d) -> p i d", d=D)
    ready = [*nt, core.came.l3x]
    narrow(core, core.XNT, core.CT, core.weights["y_wq"], core.weights["y_wk"], core.weights["y_bq"], core.weights["y_bk"],
                project_values(core, core.CT, core.weights["y_wv"], core.weights["y_bv_bc"], ready),
                lambda b, t: O[:, b * HALVES + t, :], ready)
    t = tmp(core, NT * D).rearrange("p (i d) -> p i d", d=D)
    p.ts(p.dve, t, O, 0.0, None, ALU.max, None)
    made = p.stt(p.dve, O, O, 0.0, t, ALU.min, ALU.add)
    g = transpose_all(core, lambda i: O[:, i, :], lambda q: core.XNT[:, q * BANK:(q + 1) * BANK], lambda i: made)
    add_product(core, lambda c, i: core.XNT[:, i * P:(i + 1) * P], lambda c: core.weights["y_wo"], lambda i: [g[i // 4]],
                     bias_bc=core.weights["y_bo_bc"])


def capped_mixture(core):
    p = core.p
    nt = pre_norm(core)
    p.pe.pending = [*nt, core.came.l3f]
    sel, wgt, made = route(core, core.weights["z_wr"], ALU.max)
    N = NT
    el, keep, inc, rank, live = (tmp(core, N) for _ in range(5))
    p.fill(p.dve, live, 1.0)
    for e in range(E8):
        a = p.tt(p.dve, el, sel[:, :, e], live, ALU.mult)
        bank, slot, free = core.work.take()
        p.mm(bank[:, 0:N], core.weights["upto"], el, True, True, a, *free)
        m = p.mm(bank[:, N:2 * N], core.weights["ones"], el, True, True)
        p.cp(p.dve, rank, bank[:, N:2 * N], m)
        p.scan(inc, core.weights["ones"][:, 0:N], rank, 0.0, ALU.mult, ALU.add)
        p.tt(p.dve, rank, inc, rank, ALU.subtract)
        r = p.tt(p.dve, rank, rank, bank[:, 0:N], ALU.add)
        core.work.done(slot, r)
        p.stt(p.dve, keep, rank, float(CAP), el, ALU.is_le, ALU.mult)
        p.tt(p.dve, wgt[:, :, e], wgt[:, :, e], keep, ALU.mult)
        p.tt(p.dve, el, el, keep, ALU.subtract)
        p.tt(p.dve, live, live, el, ALU.subtract)
    made = p.tt(p.dve, wgt, wgt, live.unsqueeze(2).to_broadcast([P, NT, E8]), ALU.mult)
    lost = tmp(core, N)
    p.ts(p.dve, lost, live, -1.0, 1.0, ALU.mult, ALU.add)
    y = expert_biases(core, wgt, made, core.weights["z_b2"], core.X, [])
    for i in range(NT):
        y = p.stt(p.dve, core.X[:, i, :], core.weights["z_fb2_bc"], lost[:, i:i + 1], core.X[:, i, :], ALU.mult, ALU.add, y, free=i > 0)
    hid = Ring([tmp(core, MOE3_H // P * BANK) for _ in range(2)])
    C = MOE3_H // P
    for e in range(E8):
        expert(core, MOE3_H, core.weights["z_w1"][:, e * MOE3_H:(e + 1) * MOE3_H], core.weights["z_b1"][:, e * C:(e + 1) * C],
                    core.weights["z_w2"][:, e * C * D:(e + 1) * C * D], ACT.Gelu, lambda i: wgt[:, i, e:e + 1], core.X, [y], [], hid)
    expert(core, MOE3_H, core.weights["z_fw1"], core.weights["z_fb1"], core.weights["z_fw2"], ACT.Gelu, lambda i: lost[:, i:i + 1], core.X, [y], [], hid)


def begin(core, steps):
    for q in (core.p.pe, core.p.dve, core.p.act, core.p.pool):
        q.pending += steps


def run_blocks(core, blocks):
    p = core.p
    p.dve.pending = [core.x_in]
    p.act.pending = list(core.const_ready)
    p.pool.pending = [core.x_in]
    p.pe.pending = list(core.const_ready)
    core.before_weigh = None
    stage(core)
    every = [(product_attention, lambda came: []),
             (context_attention, lambda came: [came.l0]),
             (sign_product, lambda came: [came.l0]),
             (hybrid, lambda came: [came.l1, came.mamba]),
             (raw_attention, lambda came: [came.l1b]),
             (recurrence, lambda came: [came.l1b]),
             (time_mixing, lambda came: [came.l2]),
             (wide_attention, lambda came: [came.l2x]),
             (mixture, lambda came: [came.l2f]),
             (wave, lambda came: [came.l3a]),
             (guarded_attention, lambda came: [came.l3x]),
             (capped_mixture, lambda came: [came.l3f])]
    wave_kernels(core)
    for n, (block, needs) in enumerate(every):
        stage(core)
        if n in blocks:
            if n > 0:
                begin(core, needs(core.came))
            block(core)
        if n == 5:
            stage(core)
            core.came.l2x = load(core, "l2x")
            core.came.l2f = load(core, "l2f")
        if n == 7:
            stage(core)
            core.came.l3f = load(core, "l3f")
    stage(core)
    p.dma(core.out_dram, core.X[:, :, :])


def diagonals(kern, parts, first, n):
    return bass.AP(kern.tensor, kern.offset + first, [[1, parts], [P + S, H], [1, n]])


def backwards(ap):
    *outer, (step, n) = ap.ap
    return bass.AP(ap.tensor, ap.offset + step * (n - 1), [*outer, (-step, n)])


class Rows:

    def __init__(self, whole, rows):
        self.whole, self.rows = whole, rows

    def __call__(self, h):
        rows, tile = self.rows(h)
        return self.whole[rows, tile, :]


def a_bc(dt3, i0):
    return dt3[:, i0:i0 + HALVES, :].unsqueeze(3).to_broadcast([P, HALVES, H_SSM, HP])


def build(nc, x, ctx_tok, ctx_feat, lens, sel, packs, out, blocks=tuple(range(12))):
    ctx = ExitStack()
    with ctx:
        kern = nc.dram_tensor("wave_kernels", [H, P + S], F32, kind="Internal").ap()
        core = Core()
        start(core, nc, ctx, packs, x, ctx_tok, ctx_feat, lens, kern, out, sel)
        run_blocks(core, blocks)
        block = ctx.enter_context(nc.Block())
        core.p.finish(block)


def tiled(a):
    return np.ascontiguousarray(a.reshape(NT, P, D).transpose(1, 0, 2))


def spread(w):
    out = np.zeros((w.shape[0], NSPREAD, P // GROUP, GROUP), w.dtype)
    out[:, :, :, :HD] = w.reshape(w.shape[0], NSPREAD, P // GROUP, HD)
    return out.reshape(w.shape[0], NSPREAD * P)


def spread_bias(b, ones=False):
    out = spread(b[None, :]).reshape(NSPREAD, P // GROUP, GROUP)
    if ones:
        out[:, :, HD] = 1
    return np.ascontiguousarray(out.reshape(NSPREAD, P).T)


def col(b):
    return np.ascontiguousarray(b.reshape(-1, P).T) if b.size >= P else b.reshape(-1, 1)


def rep(b):
    return np.broadcast_to(b.reshape(1, -1), (P, b.size))


def chunks(w):
    k, n = w.shape
    return w.reshape(k // P, P, n).transpose(1, 0, 2).reshape(P, -1)


def kernel(**inputs):
    import concourse.bacc as _bacc
    from concourse.bass_utils import run_bass_kernel_spmd as _run
    g = {k: np.asarray(v) for k, v in inputs.items()}
    s = np.arange(S, dtype=np.float32)
    i = np.arange(P)
    vals = {"ident": np.eye(P), "upto": i[:, None] <= i[None, :], "ones": np.ones((P, P)), "after": i[:, None] > i[None, :],
            "spread_id": spread(np.eye(P)), "steps": np.broadcast_to(s, (P, S)),
            "head_rows": (i[None, :] // HD) == np.arange(H)[:, None], "same_d": (i[:, None] % HD) == np.arange(HD)[None, :],
            "before": np.broadcast_to((np.arange(E8)[None, :] < np.arange(E8)[:, None]).reshape(1, -1), (P, E8 * E8)),
            "w_pos": np.stack([i, i + P], 1), "lower": (i < HW)[:, None], "upper": (i >= HW)[:, None],
            "one_row": (i % GROUP == HD)[:, None]}
    rest, parts = np.float32(NEG_INF * HW ** 0.5), []
    for _ in range(3):
        parts.append((np.array([rest]).view(np.uint32) & 0xFFFF0000).view(np.float32)[0])
        rest = np.float32(rest - parts[-1])
    vals["neg_parts"] = np.array(parts)[:, None]
    a = "L0_attn_"
    for n in ("q1", "q2", "k1", "k2", "v", "out"):
        vals["a_" + n] = g[a + "W_" + n]
    vals["a_bias_bc"] = rep(np.concatenate([g[a + "b_" + n] for n in ("q1", "q2", "k1", "k2", "v")]))
    vals.update(a_bout_bc=rep(g[a + "b_out"]), a_g=col(g[a + "ln_g"]), a_b=col(g[a + "ln_b"]))
    a = "L0_xattn_"
    vals.update(x_wq=g[a + "Wq"].T, x_wk=g[a + "Wk"].T, x_wv=g[a + "Wv"].T, x_wf=g[a + "Wf"].T, x_bq=col(g[a + "bq"]),
                x_bk=col(g[a + "bk"]), x_bv_bc=rep(g[a + "bv"]), x_bf_bc=rep(g[a + "bf"]), f_w=g["L0_ffn_weight"].T)
    a = "L1_attn_"
    w, b = g[a + "Wqkv_w"].T, g[a + "Wqkv_b"]
    vals.update(s_wq=spread(w[:, :D]), s_wk=spread(w[:, D:2 * D]), s_wv=w[:, 2 * D:], s_bq=spread_bias(b[:D]),
                s_bk=spread_bias(b[D:2 * D], True), s_bv_bc=rep(b[2 * D:]), s_wo=g[a + "attn_out_w"].T, s_bo_bc=rep(g[a + "attn_out_b"]),
                s_norm=col(g[a + "attn_norm_w"]), s_normf_bc=rep(g[a + "normf_w"]), s_final_bc=rep(g[a + "final_norm_w"]),
                s_fc1=g[a + "fc1_w"].T, s_fc2=chunks(g[a + "fc2_w"].T))
    conv = D_INNER + 2 * D_STATE
    for l in range(M_LAYERS):
        w = g[a + "m_in_w"][l].T
        m = {"z": w[:, :D_INNER], "xbc": w[:, D_INNER:D_INNER + conv], "dt": w[:, D_INNER + conv:],
             "cw": g[a + "m_conv_w"][l].reshape(CONV_CH, P, D_CONV).transpose(1, 0, 2).reshape(P, -1),
             "cb": col(g[a + "m_conv_b"][l]), "dtb": rep(g[a + "m_dt_bias"][l]), "alog": rep(g[a + "m_A_log"][l]),
             "dskip_bc": rep(g[a + "m_D"][l]), "norm": col(g[a + "m_norm_w"][l]), "out": chunks(g[a + "m_out_w"][l].T)}
        vals.update({f"m{l}_{k}": v for k, v in m.items()})
    a = "L1_ffn_"
    vals.update(c_proj=g["L1_xattn_w_proj"].T, c_b_bc=rep(g["L1_xattn_b_proj"]), g_c0=col(g[a + "in_c"]), g_bo_bc=rep(g[a + "bo"]))
    for n in "fico":
        vals["g_w" + n], vals["g_u" + n] = g[a + "w" + n].T, g[a + "u" + n].T
        if n != "o":
            vals["g_b" + n] = col(g[a + "b" + n])
    a = "L2_attn_"
    vals.update(r_u=col(g[a + "time_first"]), r_wk=g[a + "Wk_t"].T, r_wv=g[a + "Wv_t"].T, r_wr=g[a + "Wr_t"].T,
                r_wkc=g[a + "Wk_c"].T, r_wvc=chunks(g[a + "Wv_c"].T), r_wrc=g[a + "Wr_c"].T, r_g1=col(g[a + "ln1_g"]),
                r_b1=col(g[a + "ln1_b"]), r_g2=col(g[a + "ln2_g"]), r_b2=col(g[a + "ln2_b"]), r_mk=col(g[a + "mix_k"]),
                r_mv=col(g[a + "mix_v"]), r_mr=col(g[a + "mix_r"]), r_ck=col(g[a + "cmix_k"]), r_cr=col(g[a + "cmix_r"]))
    a = "L2_xattn_"
    vals.update(w_q=g[a + "Wq"], w_k=g[a + "Wk"], w_v=g[a + "Wv"], w_o=chunks(g[a + "Wo"]),
                w_qn=np.concatenate([g[a + "q_norm_w"]] * 2)[:, None], w_kn=np.stack([np.pad(g[a + "k_norm_w"], (0, HW)), np.pad(g[a + "k_norm_w"], (HW, 0))], 1))
    a = "L2_ffn_"
    vals.update(e_wg=g[a + "Wg"], e_w1=g[a + "W1"].transpose(1, 0, 2).reshape(P, -1), e_b1=col(g[a + "b1"].ravel()),
                e_w2=np.concatenate([chunks(w) for w in g[a + "W2"]], 1), e_b2=g[a + "b2"])
    a = "L3_attn_"
    w, b = g[a + "Wqkvg"].T, g[a + "bqkvg"]
    vals.update(v_wq=w[:, :D], v_wk=w[:, D:2 * D], v_wv=w[:, 2 * D:3 * D], v_wg=w[:, 3 * D:], v_bq=col(b[:D]),
                v_bkv_bc=rep(b[D:3 * D]), v_bg=col(b[3 * D:]), v_freq=col(g[a + "wave_frequency"]),
                v_damp=col(g[a + "wave_damping"]), v_phase=col(g[a + "wave_phase"]), v_coup=g[a + "field_coupling"],
                v_wo=g[a + "Wout"].T, v_bo_bc=rep(g[a + "bout"]))
    a = "L3_xattn_"
    vals.update(y_wq=spread(g[a + "Wq"].T), y_wk=spread(g[a + "Wk"].T), y_bq=spread_bias(g[a + "bq"]),
                y_bk=spread_bias(g[a + "bk"], True), y_wv=g[a + "Wv"].T, y_bv_bc=rep(g[a + "bv"]), y_wo=g[a + "Wo"].T,
                y_bo_bc=rep(g[a + "bo"]))
    a = "L3_ffn_"
    vals.update(z_wr=g[a + "Wr"], z_w1=g[a + "W1"].transpose(1, 0, 2).reshape(P, -1), z_b1=col(g[a + "b1"].ravel()),
                z_w2=np.concatenate([chunks(w) for w in g[a + "W2"]], 1), z_b2=g[a + "b2"], z_fw1=g[a + "fw1"],
                z_fb1=col(g[a + "fb1"]), z_fw2=chunks(g[a + "fw2"]), z_fb2_bc=rep(g[a + "fb2"]))

    nc = _bacc.Bacc("TRN2", target_bir_lowering=False, num_devices=1)
    arrays = {"x": tiled(g["x"]), "ctx_tok": tiled(g["ctx_1024"]), "ctx_feat": np.ascontiguousarray(g["ctx_1024"].reshape(T, D).T),
              "lens": np.ascontiguousarray(np.broadcast_to(g["_lenS2"][None, :], (P, B)))}
    for name, layout, _ in PACKS:
        pack = np.zeros((P, columns(layout)), np.float32)
        o = 0
        for n, c in layout:
            v = vals[n]
            assert v.shape[1] == c, (n, v.shape, c)
            pack[:v.shape[0], o:o + c] = v
            o += c
        arrays["pack_" + name] = pack
    sel = np.zeros((P, H, P), mybir.dt.np(BF16))
    for h in range(H):
        sel[h:3 * H:H, h, :] = 1
    arrays["sel"] = sel
    dram = {k: nc.dram_tensor(k, v.shape, mybir.dt.from_np(v.dtype), kind="ExternalInput").ap() for k, v in arrays.items()}
    out = nc.dram_tensor("out", (P, NT, D), F32, kind="ExternalOutput").ap()
    build(nc, dram["x"], dram["ctx_tok"], dram["ctx_feat"], dram["lens"], dram["sel"],
          {name: dram["pack_" + name] for name, _, _ in PACKS}, out)
    r = _run(nc, [arrays], core_ids=[0])
    y = r.results[0]["out"]
    return np.ascontiguousarray(y.transpose(1, 0, 2)).reshape(B, S, D)
```

```python
import numpy as np
import concourse.bass as bass
import concourse.mybir as mybir
from concourse.alu_op_type import AluOpType as ALU
from contextlib import ExitStack

F32 = mybir.dt.float32
BF16 = mybir.dt.bfloat16
ACT = mybir.ActivationFunctionType
AXX = mybir.AxisListType.X

B, S, D = 8, 256, 128
P = 128
HALVES = S // P
NT = B * HALVES
T = B * S
H = 16
HD = D // H
HW = 64
GROUP = 32
QUERY_PARTS = (0, 0, 1, 1, 0, 2, 1, 2)
KEY_PARTS = (0, 1, 0, 1, 2, 0, 2, 1)
SPREADS = 2 * 2 * 3
NWIDE = H * HW // P
BANK = 512
QUARTERS = T // BANK
M_LAYERS, D_INNER, D_STATE, H_SSM, D_CONV = 4, 256, 128, 4, 4
HP = D_INNER // H_SSM
CONV_CH = (D_INNER + 2 * D_STATE) // P
DFF = 256
ALPHA = 1.68
E8 = 8
MOE2_H = 256
MOE3_H = 512
CAP = max(int(1.25 * (1024 * 2 / E8)), 4)
NEG_INF = -1e9
BEFORE_ALL = -1e30

CONSTS = [("ident", P), ("upto", P), ("ones", P), ("after", P), 
          ("steps", S), ("head_rows", P), ("same_d", HD), ("before", E8 * E8),
          ("neg_parts", 1), ("lower", 1), ("upper", 1)]
L0_W = [("a_q1", D), ("a_q2", D), ("a_k1", D), ("a_k2", D), ("a_v", D), ("a_out", D),
        ("a_bias_bc", 5 * D), ("a_bout_bc", D), ("a_g", 1), ("a_b", 1),
        ("x_wq", D), ("x_wk", D), ("x_wv", D), ("x_wf", D), ("x_bq", 1), ("x_bk", 1),
        ("x_bv_bc", D), ("x_bf_bc", D), ("f_w", D)]
L1_W = [("s_wq", D), ("s_wk", D), ("s_bq", 1), ("s_bk", 1),
        ("s_wv", D), ("s_bv_bc", D), ("s_wo", D), ("s_bo_bc", D), ("s_norm", 1), ("s_normf_bc", D),
        ("s_final_bc", D), ("s_fc1", 2 * DFF), ("s_fc2", DFF // P * D)]
M_W = [(f"m{l}_{n}", c) for l in range(M_LAYERS) for n, c in
       [("xbc", CONV_CH * P), ("z", D_INNER), ("dt", H_SSM), ("cw", CONV_CH * D_CONV), ("cb", CONV_CH),
        ("dtb", H_SSM), ("alog", H_SSM), ("dskip_bc", H_SSM), ("norm", D_INNER // P),
        ("out", D_INNER // P * D)]]
L1_W2 = [("c_proj", D), ("c_b_bc", D),
         ("g_wf", D), ("g_uf", D), ("g_wi", D), ("g_ui", D), ("g_wc", D), ("g_uc", D), ("g_wo", D),
         ("g_uo", D), ("g_bf", 1), ("g_bi", 1), ("g_bc", 1), ("g_bo_bc", D), ("g_c0", 1)]
L2_W = [("r_u", 1), ("r_wk", D), ("r_wv", D), ("r_wr", D), ("r_wkc", 4 * D), ("r_wvc", 4 * D),
        ("r_wrc", D), ("r_g1", 1), ("r_b1", 1), ("r_g2", 1), ("r_b2", 1), ("r_mk", 1), ("r_mv", 1),
        ("r_mr", 1), ("r_ck", 1), ("r_cr", 1)]
L2_X = [("w_q", H * HW), ("w_k", H * HW), ("w_v", H * HW), ("w_o", NWIDE * D), ("w_qn", 1), ("w_kn", 1),
        ("w_pos", HALVES)]
L2_F = [("e_wg", E8), ("e_w1", E8 * MOE2_H), ("e_b1", E8 * MOE2_H // P), ("e_w2", E8 * MOE2_H // P * D),
        ("e_b2", D)]
L3_A = [("v_wq", D), ("v_wk", D), ("v_wv", D), ("v_wg", D), ("v_bq", 1), ("v_bkv_bc", 2 * D), ("v_bg", 1),
        ("v_freq", 1), ("v_damp", 1), ("v_phase", 1), ("v_coup", H), ("v_wo", D), ("v_bo_bc", D)]
L3_X = [("y_wq", D), ("y_wk", D), ("y_bq", 1), ("y_bk", 1), ("y_wv", D),
        ("y_bv_bc", D), ("y_wo", D), ("y_bo_bc", D)]
L3_F = [("z_wr", E8), ("z_w1", E8 * MOE3_H), ("z_b1", E8 * MOE3_H // P), ("z_w2", E8 * MOE3_H // P * D),
        ("z_b2", D), ("z_fw1", MOE3_H), ("z_fb1", MOE3_H // P), ("z_fw2", MOE3_H // P * D), ("z_fb2_bc", D)]
PACKS = [("consts", CONSTS, "keep"), ("l0", L0_W, "early"), ("l1", L1_W, "early"), ("mamba", M_W, "early"),
         ("l1b", L1_W2, "early"), ("l2", L2_W, "keep"), ("l2x", L2_X, "keep"), ("l2f", L2_F, "keep"),
         ("l3a", L3_A, "keep"), ("l3x", L3_X, "keep"), ("l3f", L3_F, "late")]


def columns(pack):
    return sum(c for _, c in pack)


class Step:

    def __init__(self, queue, issue, after):
        self.queue, self.issue, self.after = queue, issue, after
        self.count, self.sem, self.amount = 0, None, 1


class Queue:

    def __init__(self, chained):
        self.steps, self.chained = [], chained
        self.pending = []

    def put(self, issue, after, free=False):
        after = [a for a in after if a is not None]
        if self.pending:
            after += self.pending
            self.pending = []
        if self.chained and not free and self.steps:
            after.append(self.steps[-1])
        step = Step(self, issue, after)
        self.steps.append(step)
        return step

    def emit(self, engine):
        seen = {}
        for step in self.steps:
            need = {}
            for a in step.after:
                if a.count > max(seen.get(id(a.sem), 0), need.get(id(a.sem), (0, None))[0]):
                    need[id(a.sem)] = (a.count, a.sem)
            for key, (count, sem) in need.items():
                engine.wait_ge(sem, count)
                seen[key] = count
            step.issue(engine).then_inc(step.sem, step.amount)


class Ring:

    def __init__(self, bufs):
        self.bufs, self.last, self.at = bufs, [[] for _ in bufs], -1

    def take(self):
        self.at = (self.at + 1) % len(self.bufs)
        assert self.last[self.at] is not None, "the buffer is still in use"
        free, self.last[self.at] = self.last[self.at], None
        return self.bufs[self.at], self.at, free

    def done(self, slot, *readers):
        self.last[slot] = [r for r in readers if r is not None]


class Program:

    def __init__(self, nc, ctx):
        self.nc, self.ctx = nc, ctx
        self.pe, self.dve, self.act, self.pool = Queue(False), Queue(True), Queue(True), Queue(True)
        self.sp = Queue(False)
        self.dmas = []

    def mm(self, out, lhsT, rhs, start, stop, *after):
        return self.pe.put(lambda e: e.matmul(out, lhsT, rhs, start=start, stop=stop, skip_group_check=True), list(after))

    def tr(self, out, in_, ident, *after):
        return self.pe.put(lambda e: e.transpose(out, in_, ident), list(after))

    def tt(self, q, out, a, b, op, *after, free=False):
        return q.put(lambda e: e.tensor_tensor(out, a, b, op), list(after), free)

    def ts(self, q, out, a, s1, s2, op0, op1, *after, free=False):
        if op1 is None:
            return q.put(lambda e: e.tensor_scalar(out, a, s1, None, op0), list(after), free)
        return q.put(lambda e: e.tensor_scalar(out, a, s1, s2, op0, op1), list(after), free)

    def stt(self, q, out, a, s, b, op0, op1, *after, free=False):
        return q.put(lambda e: e.scalar_tensor_tensor(out=out, in0=a, scalar=s, in1=b, op0=op0, op1=op1), list(after), free)

    def cp(self, q, out, a, *after, free=False):
        if q is self.act:
            return q.put(lambda e: e.activation(out, a, ACT.Copy), list(after), free)
        return q.put(lambda e: e.tensor_copy(out, a), list(after), free)

    def af(self, out, a, func, *after, scale=1.0, bias=None, free=False):
        if bias is None:
            return self.act.put(lambda e: e.activation(out, a, func, scale=scale), list(after), free)
        return self.act.put(lambda e: e.activation(out, a, func, scale=scale, bias=bias), list(after), free)

    def red(self, out, a, op, *after, negate=None, mag=None, free=False):
        return self.dve.put(lambda e: e.tensor_reduce(out, a, AXX, op, negate=negate, apply_absolute_value=mag), list(after), free)

    def scan(self, out, a, b, init, op0, op1, *after, free=False):
        return self.dve.put(lambda e: e.tensor_tensor_scan(out, a, b, init, op0, op1), list(after), free)

    def recip(self, out, a, *after, free=False):
        return self.dve.put(lambda e: e.reciprocal(out, a), list(after), free)

    def fill(self, q, out, value, *after, free=False):
        return q.put(lambda e: e.memset(out, value), list(after), free)

    def bnst(self, out, a, *after, free=False):
        return self.dve.put(lambda e: e.bn_stats(out, a), list(after), free)

    def bnag(self, out, a, *after, free=False):
        return self.dve.put(lambda e: e.bn_aggr(out, a), list(after), free)

    def dma(self, out, in_, *after):
        step = self.sp.put(lambda e: e.dma_start(out, in_), list(after))
        step.sem, step.count, step.amount = self.ctx.enter_context(self.nc.semaphore(f"s_dma{len(self.dmas)}")), 16, 16
        self.dmas.append(step)
        return step

    def boundary(self):
        queues = [self.pe, self.dve, self.act, self.pool]
        lasts = [q.steps[-1] for q in queues if q.steps]
        for q in queues + [self.sp]:
            q.pending = q.pending + [s for s in lasts if s.queue is not q or q.chained]

    def finish(self, block):
        for q, name in ((self.pe, "s_pe"), (self.dve, "s_dve"), (self.act, "s_act"), (self.pool, "s_pool")):
            sem = self.ctx.enter_context(self.nc.semaphore(name))
            for n, step in enumerate(q.steps):
                step.sem, step.count = sem, n + 1
        for q, on in ((self.pe, block.tensor), (self.dve, block.vector), (self.act, block.scalar),
                      (self.pool, block.gpsimd), (self.sp, block.sync)):
            on(lambda engine, q=q: self.run(q, engine))

    def run(self, q, engine):
        q.emit(engine)
        if q is self.sp:
            for step in self.dmas:
                engine.wait_ge(step.sem, step.count)


def alternate(p, n):
    return p.act if n % 2 else p.dve


class Loads:
    pass


class Core:
    pass


def start(core, nc, ctx, packs, x_dram, ctx_dram, ctxt_dram, lens_dram, kern_dram, out_dram, sel_dram):
    core.nc, core.ctx = nc, ctx
    p = core.p = Program(nc, ctx)
    core.out_dram, core.kern_dram = out_dram, kern_dram
    sizes = {r: sum(columns(c) for _, c, where in PACKS if where == r) for r in ("keep", "early", "late")}
    keep = sb(core, "w_keep", [P, sizes["keep"]])
    early = sb(core, "w_early", [P, max(sizes["early"], sizes["late"])])
    core.early, core.keep, core.used2, core.used3 = early, keep, 0, 0
    core.l2x_at = columns(CONSTS) + columns(L2_W)
    core.weights, core.pack_dram = {}, packs
    came = core.came = Loads()
    at = {"keep": 0, "early": 0, "late": 0}
    core.pack_dst = {}
    for name, layout, region in PACKS:
        base, buf = at[region], keep if region == "keep" else early
        core.pack_dst[name] = buf[:, base:base + columns(layout)]
        o = base
        for n, c in layout:
            core.weights[n] = buf[:, o:o + c]
            o += c
        at[region] = o
    core.weights["upto2"] = keep[:, P:3 * P]
    core.X = sb(core, "X", [P, NT, D])
    core.XN = sb(core, "XN", [P, NT, D])
    core.XNT = sb(core, "XNT", [P, T])
    core.CT = sb(core, "CT", [P, T])
    core.CX = sb(core, "CX", [P, NT, D])
    core.SEL = sb(core, "SEL", [P, H, P], BF16)
    core.SPREAD = sb(core, "SPREAD", [P, SPREADS, P], BF16)
    core.ONE = sb(core, "ONE", [P, P], BF16)
    core.kern = sb(core, "kern", [H, S])
    core.kern_zero = sb(core, "kern_zero", [H, P])
    core.IDB = sb(core, "IDB", [P, P], BF16)
    core.stats = sb(core, "stats", [P, NT, 6])
    core.mv = sb(core, "mv", [P, NT, 2])
    core.rs = sb(core, "rs", [P, NT])
    left = nc.sbuf_bytes_remaining() if callable(nc.sbuf_bytes_remaining) else nc.sbuf_bytes_remaining
    core.scratch_cols = (left - 2048) // 4
    core.scratch = sb(core, "scratch", [P, core.scratch_cols])
    core.used = 0
    core.banks = [ctx.enter_context(nc.psum_tensor(f"bank{i}", [P, BANK], F32)) for i in range(8)]
    core.work = Ring(core.banks[0:6])
    core.acc = Ring(core.banks[6:8])
    core.x_in = p.dma(core.X[:, :, :], x_dram)
    came.consts = load(core, "consts")
    core.sel_in = p.dma(core.SEL[:, :, :], sel_dram[:, 0:H, :])
    core.spread_in = p.dma(core.SPREAD[:, :, :], sel_dram[:, H:H + SPREADS, :])
    came.l0 = load(core, "l0")
    core.ctx_in = [p.dma(core.CT[:, :], ctxt_dram), p.dma(core.CX[:, :, :], ctx_dram)]
    came.l1 = load(core, "l1")
    came.mamba = load(core, "mamba")
    came.l1b = load(core, "l1b")
    came.l2 = load(core, "l2")
    core.lens_dram = lens_dram
    came.l3a = load(core, "l3a")
    came.l3x = load(core, "l3x")
    one = p.fill(p.pool, core.ONE[:, :], 1.0)
    idb = p.cp(p.dve, core.IDB[:, :], core.weights["ident"], core.came.consts)
    core.const_ready = [one, idb, core.sel_in, core.spread_in]


def sb(core, name, shape, dt=F32):
    return core.ctx.enter_context(core.nc.sbuf_tensor(name, shape, dt))


def tmp3(core, cols):
    at, core.used3 = core.used3, core.used3 + cols
    assert core.used3 <= columns(L2_X) + columns(L2_F)
    return core.keep[:, core.l2x_at + at:core.l2x_at + at + cols]


def load(core, name, *after):
    return core.p.dma(core.pack_dst[name], core.pack_dram[name], *after)


def tmp2(core, cols, dt=F32):
    words = cols if dt == F32 else (cols + 1) // 2
    ap = core.early[:, core.used2:core.used2 + words]
    core.used2 += words
    assert core.used2 <= core.early.shape[1]
    return ap if dt == F32 else ap.bitcast(dt)


def tmp(core, cols, dt=F32):
    words = cols if dt == F32 else (cols + 1) // 2
    ap = core.scratch[:, core.used:core.used + words]
    core.used += words
    assert core.used <= core.scratch_cols, ("scratch", core.used, core.scratch_cols)
    return ap if dt == F32 else ap.bitcast(dt)


def stage(core):
    core.p.boundary()
    core.used = core.used2 = core.used3 = 0


def rstd(core, out, var, n, *after):
    p = core.p
    p.ts(p.dve, var, var, 1e-5, None, ALU.add, None, *after)
    a = p.dve.steps[-1]
    s = p.af(out, var, ACT.Sqrt, a)
    return p.recip(out, out, s)


def normalise(core, src, dst, *after):
    p = core.p
    for i in range(NT):
        p.bnst(core.stats[:, i, :], src[:, i, :], *after, free=i > 0)
    for i in range(NT):
        p.bnag(core.mv[:, i, :], core.stats[:, i, :], free=i > 0)
    r = rstd(core, core.rs[:, :], core.mv[:, :, 1], NT)
    out = []
    for i in range(NT):
        out.append(p.ts(p.dve, dst[:, i, :], src[:, i, :], core.mv[:, i, 0:1], core.rs[:, i:i + 1],
                        ALU.subtract, ALU.mult, r, free=i > 0))
    return out


def mean_square(core, tiles, src, width, *after):
    p = core.p
    for i in range(tiles):
        p.bnst(core.stats[:, i, :], src(i), *after, free=i > 0)
    for i in range(tiles):
        p.bnag(core.mv[:, i, :], core.stats[:, i, :], free=i > 0)
    m, v = core.mv[:, 0:tiles, 0], core.mv[:, 0:tiles, 1]
    p.tt(p.dve, m, m, m, ALU.mult)
    p.tt(p.dve, v, v, m, ALU.add)
    return rstd(core, core.rs[:, 0:tiles], v, tiles)


def transpose_all(core, src, dst, after, scale=None, bias=None):
    p, out = core.p, []
    for n in range(QUARTERS):
        bank, slot, free = core.work.take()
        for j in range(BANK // P):
            i = n * (BANK // P) + j
            t = p.tr(bank[:, j * P:(j + 1) * P], src(i), core.weights["ident"], after(i), core.came.consts, *free)
        d = dst(n)
        if scale is None:
            e = p.cp(alternate(p, n), d, bank[:, :], t, free=True)
        elif bias is None:
            e = p.ts(p.dve, d, bank[:, :], scale, None, ALU.mult, None, t, free=True)
        else:
            e = p.ts(p.dve, d, bank[:, :], scale, bias, ALU.mult, ALU.add, t, free=True)
        core.work.done(slot, e)
        out.append(e)
    return out


def pre_norm(core):
    n = normalise(core, core.X, core.XN)
    return transpose_all(core, lambda i: core.XN[:, i, :], lambda q: core.XNT[:, q * BANK:(q + 1) * BANK], lambda i: n[i])


def add_product(core, lhs, weight, after, pieces=1, bias_bc=None, dst=None):
    p = core.p
    dst = core.X if dst is None else dst
    out = []
    for n in range(QUARTERS):
        bank, slot, free = core.work.take()
        for j in range(BANK // P):
            i = n * (BANK // P) + j
            for c in range(pieces):
                m = p.mm(bank[:, j * P:(j + 1) * P], lhs(c, i), weight(c), c == 0, c == pieces - 1,
                         *after(i), *free)
        tiles = dst[:, n * 4:(n + 1) * 4, :]
        b = bank[:, :].rearrange("p (j d) -> p j d", d=D)
        if bias_bc is not None:
            p.tt(p.pool, tiles, tiles, bias_bc.unsqueeze(1).to_broadcast([P, 4, D]), ALU.add, p.dve.steps[-1])
        e = p.tt(p.dve, tiles, tiles, b, ALU.add, m, p.pool.steps[-1] if p.pool.steps else None, free=True)
        core.work.done(slot, e)
        out.append(e)
    return out


def merge(*works):
    works = [[g, n, 0] for g, n in works]
    while works:
        w = min(works, key=lambda w: w[2] / w[1])
        w[2] += 1
        try:
            next(w[0])
        except StopIteration:
            works.remove(w)


def finished(work):
    while True:
        try:
            next(work)
        except StopIteration as end:
            return end.value


def attention(core, heads, group, scale, prepare, values, finish, done, pieces, deep=False, masked=None, exps=4):
    p = core.p
    expo = Ring([tmp(core, BANK) for _ in range(exps)])
    per_bank = min(heads, BANK // S)
    neg = Ring([tmp(core, HALVES * heads) for _ in range(2)])
    pads = [tmp(core, HALVES * P, BF16) for _ in range(2)]
    part = Ring(pads)
    rest = Ring([tmp(core, HALVES * heads) for _ in range(2)])
    negt = Ring([tmp(core, S, BF16) for _ in range(3)])
    for x in pads:
        cleared = p.fill(p.pool, x, 0.0)
    made = {}
    look = min(heads, 2)
    pending, accs, follow = [], {}, []

    def prepared(b):
        made[b] = [(yield from prepare(b))]

    def maxima(b):
        made[b].append((yield from values(b)))
        q, k, ready = made[b][0]
        ng, ns, nf = neg.take()
        ngv = ng.rearrange("p (t h) -> p t h", h=heads)
        for t in range(HALVES):
            for n in range(heads // per_bank):
                bank, slot, free = core.work.take()
                if masked is not None:
                    p.mm(bank[:, :], core.ONE[:, :], masked["row"](b), True, False, *free, *masked["ready"])
                if heads > 1:
                    mine, dst = [4 * (n // 2) + n % 2, 4 * (n // 2) + n % 2 + 2], \
                        ngv[:, t, :].rearrange("p (a g) -> p g a", g=2)[:, n % 2, 2 * (n // 2):2 * (n // 2) + 2]
                else:
                    mine, dst = [0], ngv[:, t, :]
                for j, h in enumerate(mine):
                    m = p.mm(bank[:, j * S:(j + 1) * S], q(h)[:, t * P:(t + 1) * P], k(h), masked is None, True, *free, *ready)
                r = p.red(dst, bank[:, 0:per_bank * S].rearrange("p (h s) -> p h s", s=S),
                          ALU.max, m, *nf, negate=True, free=True)
                core.work.done(slot, r)
                yield
        pt, ps_, pf = part.take()
        rt, rs_, rf = rest.take()
        ptv = pt.rearrange("p (t n) -> p t n", n=P)
        rtv = rt.rearrange("p (t h) -> p t h", h=heads)
        cut = lambda n: ptv[:, :, n * heads:(n + 1) * heads]
        x = p.cp(p.dve, cut(0), ngv, r, *pf, cleared, free=True)
        x = p.tt(p.dve, rtv, ngv, cut(0), ALU.subtract, x, *rf, free=True)
        y = p.cp(p.dve, cut(1), rtv, x, free=True)
        x = p.tt(p.dve, rtv, rtv, cut(1), ALU.subtract, y, free=True)
        y = p.cp(p.dve, cut(2), rtv, x, free=True)
        neg.done(ns, x)
        rest.done(rs_, y)
        yield
        yield
        bank, slot, free = core.work.take()
        bankb = bank[:, :].bitcast(BF16)
        for t in range(HALVES):
            m = p.tr(bankb[:, t * P:(t + 1) * P], ptv[:, t, :], core.IDB[:, :], y, *free)
        part.done(ps_, m)
        nt, nts, ntf = negt.take()
        e = p.cp(p.dve, nt, bankb[:, 0:S], m, *ntf, free=True)
        core.work.done(slot, e)
        made[b] += [nt, nts, e]

    def weigh(b):
        (q, k, _), (v, ready), nt, nts, cut = made.pop(b)

        def weighted(h, ex, exs, e):
            n = h // (2 * group)
            if (b, n) not in accs:
                accs[b, n] = core.acc.take()
            acc, slot, free = accs[b, n]
            for half, operand in v(h):
                for c in range(HALVES):
                    m = p.mm(acc[:, half * S:(half + 1) * S], operand(c), ex[:, c * S:(c + 1) * S],
                             c == 0 and h % group == 0, c == HALVES - 1 and h % group == group - 1, e, *free, *ready)
            expo.done(exs, m)
            if h == heads - 1 or (h + 1) % (2 * group) == 0:
                r, then = finish(b, n, acc, m)
                core.acc.done(slot, r)
                if then is not None:
                    follow.append([2, then])
            if h == heads - 1:
                negt.done(nts, m)
                done(b, m)
        for h in range(heads):
            bank, slot, free = core.work.take()
            sel = core.SEL[:, h, :] if heads == H else core.ONE[:, :]
            p.mm(bank[:, :], sel, nt.unsqueeze(1).to_broadcast([P, HALVES, S]), True, False, cut, *free)
            for c in range(HALVES):
                m = p.mm(bank[:, c * S:(c + 1) * S], k(h)[:, c * P:(c + 1) * P], q(h), False, True, cut, *free)
            ex, exs, exf = expo.take()
            if masked is None:
                e = p.af(ex, bank[:, :], ACT.Exp, m, *exf, scale=scale, free=True)
            else:
                for c in range(HALVES):
                    e = p.af(ex[:, c * S:(c + 1) * S], bank[:, c * S:(c + 1) * S], ACT.Exp, m, *exf,
                             scale=scale, bias=masked["column"](b, c), free=True)
            core.work.done(slot, e)
            pending.append((weighted, h, ex, exs, e))
            drain(look)
            yield

    def drain(left):
        while len(pending) > left:
            weighted, *head = pending.pop(0)
            weighted(*head)
        for f in follow:
            f[0] -= 1
        while follow and (follow[0][0] <= 0 or not left):
            follow.pop(0)[1]()

    def prepare_and_maxima(b):
        yield from prepared(b)
        yield from maxima(b)
    first = heads // per_bank * HALVES + 3
    if deep:
        merge((prepared(0), 1))
        merge((maxima(0), first), (prepared(1), pieces))
    else:
        merge((prepare_and_maxima(0), 1))
    for b in range(B):
        weighing = weigh(b)
        for _ in range(look if heads > 1 else 0):
            next(weighing)
        works = [(weighing, heads)]
        if deep:
            if b + 1 < B:
                works.append((maxima(b + 1), first + 2))
            if b + 2 < B:
                works.append((prepared(b + 2), pieces))
        elif b + 1 < B:
            works.append((prepare_and_maxima(b + 1), first + pieces))
        merge(*works)
    drain(0)


def divided(core, dst):
    p = core.p
    inverse = Ring([tmp(core, S) for _ in range(2)])

    def finish(b, n, bank, last):
        inv, slot, free = inverse.take()
        low, high = slice(0, HW), slice(HW, P)
        out = dst(b, n)
        p.cp(p.act, inv[low, :], bank[high, 0:S], last, *free, free=True)
        r = p.cp(p.act, inv[high, :], bank[low, S:2 * S], last, free=True)
        r = p.recip(inv, inv, r, free=True)
        p.tt(p.dve, out[low, :], bank[low, 0:S], inv[low, :], ALU.mult, r, free=True)
        r = p.tt(p.dve, out[high, :], bank[high, S:2 * S], inv[high, :], ALU.mult, r, free=True)
        inverse.done(slot, r)
        return r, None
    return finish


def columns_of(buf, first, *dims):
    return bass.AP(buf.tensor, buf.offset + first, [buf.ap[0], *([step, n] for step, n in dims)])


class NarrowValues:

    COLS = HALVES * H * P

    def __init__(self, core, bufs):
        p = core.p
        self.ring, self.ones = Ring(bufs), []
        half, head = H // 2 * P, P + HD
        for buf in bufs:
            zero = p.fill(p.pool, buf, 0.0)
            for t in range(HALVES):
                self.ones.append(p.fill(p.pool, columns_of(buf, t * H * P + HW, (half - HW, 2), (head, H // 2), (1, HD)), 1.0, zero))

    def place(self, buf, t):
        return columns_of(buf, t * H * P, (H // 2 * P + HW, 2), (P + HD, H // 2), (1, HD))

    def operand(self, buf):
        return lambda h: [(h // (H // 2), lambda c: buf[:, (c * H + h) * P:(c * H + h + 1) * P])]



def narrow(core, qsrc, ksrc, wq, wk, bq, bk, value_of, dst, ready):
    p = core.p
    WIDE = H // 2
    stacks = Ring([tmp(core, 2 * WIDE * S, BF16) for _ in range(3)])
    flat = Ring([tmp(core, 2 * S) for _ in range(2)])
    pieces = Ring([tmp(core, 3 * 2 * S, BF16) for _ in range(2)])
    narrow_values = NarrowValues(core, [tmp3(core, NarrowValues.COLS) for _ in range(2)])
    held = {}

    def prepare(b):
        cols = slice(b * S, (b + 1) * S)
        fl, fs, ff = flat.take()
        x, got = fl.rearrange("p (n s) -> p n s", s=S), []
        if wq is None:
            for n, src in enumerate((qsrc, ksrc)):
                got.append(p.cp(p.pool, x[:, n, :], src[:, cols], *ff, *ready, free=True))
        else:
            bank, bs, bf = core.work.take()
            for n, (src, w) in enumerate(((qsrc, wq), (ksrc, wk))):
                m = p.mm(bank[:, n * S:(n + 1) * S], w, src[:, cols], True, True, *bf, *ready)
            for n, bias in enumerate((bq, bk)):
                got.append(p.af(x[:, n, :], bank[:, n * S:(n + 1) * S], ACT.Identity, m, *ff, bias=bias, free=True))
            core.work.done(bs, got[-1])
        yield
        yield
        pc, pcs, pcf = pieces.take()
        part = lambda c: pc[:, c * 2 * S:(c + 1) * 2 * S]
        o = p.cp(p.dve, part(0), fl, *got, *pcf, free=True)
        o = p.tt(p.dve, fl, fl, part(0), ALU.subtract, o, free=True)
        yield
        o = p.cp(p.dve, part(1), fl, o, free=True)
        o = p.tt(p.dve, part(2), fl, part(1), ALU.subtract, o, free=True)
        flat.done(fs, o)
        yield
        yield
        st, ss, sf = stacks.take()
        view = st.rearrange("p (n w s) -> p n w s", n=2, s=S)
        out = []
        for n in range(2):
            for w0 in range(0, WIDE, 2):
                rows = slice(w0 // 2 * GROUP, (w0 // 2 + 1) * GROUP)
                bank, bs, bf = core.work.take()
                for j in range(2):
                    for c in range(3):
                        m = p.mm(bank[:, j * S:(j + 1) * S], core.SPREAD[rows, (n * 2 + j) * 3 + c, :],
                                 part(c)[rows, n * S:(n + 1) * S], c == 0, c == 2, o, *bf)
                e = p.cp(p.act, view[:, n, w0:w0 + 2, :], bank[:, :].rearrange("p (w s) -> p w s", s=S), m, *sf, free=True)
                core.work.done(bs, e)
                out.append(e)
                yield
        pieces.done(pcs, m)
        held[b] = [ss]
        at = lambda n, h: view[HW * (h % 2):HW * (h % 2 + 1), n, h // 2, :]
        return (lambda h: at(0, h)), (lambda h: at(1, h)), out

    def values(b):
        buf, slot, free = narrow_values.ring.take()
        e = value_of(b, lambda t: narrow_values.place(buf, t), [*free, *narrow_values.ones])
        held[b].append(slot)
        yield
        return narrow_values.operand(buf), e

    def done(b, last):
        for ring, slot in zip((stacks, narrow_values.ring), held.pop(b)):
            ring.done(slot, last)
    attention(core, H, H // 2, HD ** -0.5, prepare, values, divided(core, dst), done, 14, deep=True)


def project_values(core, src, w, bias_bc, ready):
    p = core.p

    def value_of(b, place, free):
        bank, bs, bf = core.work.take()
        for t in range(HALVES):
            m = p.mm(bank[:, t * P:(t + 1) * P], src[:, b * S + t * P:b * S + (t + 1) * P], w, True, True, *bf, *ready)
        split = lambda ap: ap.rearrange("p (g h w) -> p g h w", g=2, w=HD)
        out = [p.tt(p.dve, place(t), split(bank[:, t * P:(t + 1) * P]), split(bias_bc), ALU.add, m, *free, free=True)
               for t in range(HALVES)]
        core.work.done(bs, *out)
        return out
    return value_of


def product_attention(core):
    p = core.p
    nt = pre_norm(core)
    O = core.XN
    wsum = tmp(core, 5 * D)
    names = ["a_q1", "a_q2", "a_k1", "a_k2", "a_v"]
    for n, name in enumerate(names):
        weff = p.tt(p.pool, wsum[:, n * D:(n + 1) * D], core.weights[name], core.weights["ident"], ALU.add,
                    core.came.l0, core.came.consts, free=True)
    bias = core.weights["a_bias_bc"]
    flatr = Ring([tmp(core, 4 * D) for _ in range(2)])
    kron = Ring([tmp(core, H * HW) for _ in range(2)])
    qr = Ring([tmp(core, NWIDE * S) for _ in range(2)])
    kr = Ring([tmp3(core, NWIDE * S) for _ in range(2)])
    narrow_values = NarrowValues(core, [tmp(core, NarrowValues.COLS), tmp3(core, NarrowValues.COLS)])
    held = {}

    def prepare(b):
        bufs = [r.take() for r in (qr, kr)]
        ready = []
        for t in range(HALVES):
            i = b * HALVES + t
            x = core.XNT[:, i * P:(i + 1) * P]
            bank, bs, bf = core.work.take()
            m = p.mm(bank[:, :], x, wsum[:, 0:4 * D], True, True, *bf, weff, *nt)
            fl, fs, ff = flatr.take()
            e = p.tt(p.dve, fl, bank[:, :], bias[:, 0:4 * D], ALU.add, m, *ff, core.came.l0, free=True)
            core.work.done(bs, e)
            yield
            used = []
            for n, q in ((0, p.dve), (1, p.pool)):
                kb, kbs, kf = kron.take()
                a = fl[:, 2 * n * D:(2 * n + 1) * D].rearrange("p (h i) -> p h i", i=HD).unsqueeze(3).to_broadcast([P, H, HD, HD])
                c = fl[:, (2 * n + 1) * D:(2 * n + 2) * D].rearrange("p (h j) -> p h j", j=HD).unsqueeze(2).to_broadcast([P, H, HD, HD])
                o = p.tt(q, kb.rearrange("p (h i j) -> p h i j", i=HD, j=HD), a, c, ALU.mult, e, *kf)
                used.append(o)
                dst, _, df = bufs[n]
                dv = dst.rearrange("p (w s) -> p w s", s=S)
                for g in range(0, NWIDE, 4):
                    bank, bs, bf = core.work.take()
                    for j in range(4):
                        m = p.tr(bank[:, j * P:(j + 1) * P], kb[:, (g + j) * P:(g + j + 1) * P], core.weights["ident"], o, *bf)
                    bv = bank[:, :].rearrange("p (w s) -> p w s", s=P)
                    ee = p.cp(p.act, dv[:, g:g + 4, t * P:(t + 1) * P], bv, m, *df, free=True)
                    core.work.done(bs, ee)
                    ready.append(ee)
                    yield
                kron.done(kbs, m)
            flatr.done(fs, *used)
        q = bufs[0][0].rearrange("p (w s) -> p w s", s=S)
        k = bufs[1][0].rearrange("p (w s) -> p w s", s=S)
        held[b] = [bufs[0][1], bufs[1][1]]
        at = lambda tiles, h: tiles[HW * (h % 2):HW * (h % 2 + 1), h // 2, :]
        return (lambda h: at(q, h)), (lambda h: at(k, h)), ready
    project = project_values(core, core.XNT, wsum[:, 4 * D:5 * D], bias[:, 4 * D:5 * D], [weff, *nt, core.came.l0])

    def values(b):
        buf, slot, free = narrow_values.ring.take()
        e = project(b, lambda t: narrow_values.place(buf, t), [*free, *narrow_values.ones])
        held[b].append(slot)
        yield
        return narrow_values.operand(buf), e

    def done(b, last):
        for ring, slot in zip((qr, kr, narrow_values.ring), held.pop(b)):
            ring.done(slot, last)
    attention(core, H, H // 2, 1.0, prepare, values, divided(core, lambda b, n: core.XNT[:, b * S:(b + 1) * S]), done, 10)
    last = p.dve.steps[-1]
    tr = transpose_all(core, lambda i: core.XNT[:, i * P:(i + 1) * P], lambda q: O[:, 4 * q:4 * q + 4, :].rearrange("p i d -> p (i d)"),
                       lambda i: last)
    p.dve.pending = list(tr)
    n = normalise(core, O, O)
    g = transpose_all(core, lambda i: O[:, i, :], lambda q: core.XNT[:, q * BANK:(q + 1) * BANK], lambda i: n[i],
                  core.weights["a_g"], core.weights["a_b"])
    add_product(core, lambda c, i: core.XNT[:, i * P:(i + 1) * P], lambda c: core.weights["a_out"],
                     lambda i: [g[i // 4]], bias_bc=core.weights["a_bout_bc"])


def context_attention(core):
    p = core.p
    nt = pre_norm(core)
    qr = Ring([tmp(core, S) for _ in range(4)])
    kr = Ring([tmp(core, S) for _ in range(4)])
    vr = Ring([tmp(core, HALVES * D) for _ in range(3)])
    inverse = Ring([tmp(core, S) for _ in range(2)])
    held = {}
    ready = [*nt, *core.ctx_in, core.came.l0]

    def prepare(b):
        out, slots, aps = [], [], []
        for ring, src, w, bias in ((qr, core.XNT, "x_wq", "x_bq"), (kr, core.CT, "x_wk", "x_bk")):
            buf, slot, free = ring.take()
            bank, bs, bf = core.work.take()
            m = p.mm(bank[:, 0:S], core.weights[w], src[:, b * S:(b + 1) * S], True, True, *bf, *ready)
            e = p.af(buf, bank[:, 0:S], ACT.Identity, m, *free, bias=core.weights[bias], free=True)
            core.work.done(bs, e)
            out.append(e)
            slots.append(slot)
            aps.append(buf)
            yield
        held[b] = slots
        q, k = aps
        return (lambda h: q), (lambda h: k), out

    def values(b):
        v, slot, free = vr.take()
        bank, bs, bf = core.work.take()
        for t in range(HALVES):
            m = p.mm(bank[:, t * P:(t + 1) * P], core.CT[:, b * S + t * P:b * S + (t + 1) * P], core.weights["x_wv"], True, True, *bf)
        vv = v.rearrange("p (t w) -> p t w", t=HALVES)
        e = p.tt(p.dve, vv, bank[:, 0:S].rearrange("p (t w) -> p t w", t=HALVES),
                 core.weights["x_bv_bc"].unsqueeze(1).to_broadcast([P, HALVES, D]), ALU.add, m, *free, free=True)
        core.work.done(bs, e)
        held[b].append(slot)
        yield
        return (lambda h: [(0, lambda c: vv[:, c, :]), (1, lambda c: core.weights["ones"])]), [e]

    def finish(b, n, bank, last):
        inv, slot, free = inverse.take()
        r = p.recip(inv, bank[:, S:2 * S], last, *free, free=True)
        r = p.tt(p.dve, core.XNT[:, b * S:(b + 1) * S], bank[:, 0:S], inv, ALU.mult, r, free=True)
        inverse.done(slot, r)
        return r, None

    def done(b, last):
        for ring, slot in zip((qr, kr, vr), held.pop(b)):
            ring.done(slot, last)
    attention(core, 1, 1, 1.0 / 8.0, prepare, values, finish, done, 3, deep=True)
    made = p.dve.steps[-1]
    act_in = Ring([tmp(core, BANK) for _ in range(2)])
    for n in range(QUARTERS):
        bank, slot, free = core.work.take()
        for j in range(4):
            i = 4 * n + j
            m = p.mm(bank[:, j * P:(j + 1) * P], core.XNT[:, i * P:(i + 1) * P], core.weights["x_wf"], True, True, *free, made)
        buf, bs, bf = act_in.take()
        bv = buf.rearrange("p (j d) -> p j d", d=D)
        a = p.tt(p.dve, bv, bank[:, :].rearrange("p (j d) -> p j d", d=D),
                 core.weights["x_bf_bc"].unsqueeze(1).to_broadcast([P, 4, D]), ALU.add, m, *bf)
        core.work.done(slot, a)
        e = p.af(buf, buf, ACT.Gelu, a)
        tiles = core.X[:, 4 * n:4 * n + 4, :]
        p.tt(p.dve, tiles, tiles, bv, ALU.add, e)
        r = p.tt(p.dve, tiles, tiles, core.CX[:, 4 * n:4 * n + 4, :], ALU.add)
        act_in.done(bs, r)


def sign_product(core):
    p = core.p
    nt = pre_norm(core)
    pos, sign = tmp(core, D), tmp(core, D)
    p.ts(p.dve, pos, core.weights["f_w"], 0.0, None, ALU.is_gt, None, core.came.l0)
    s = p.stt(p.dve, sign, core.weights["f_w"], 0.0, pos, ALU.is_lt, ALU.subtract)
    s = p.ts(p.dve, sign, sign, -1.0, None, ALU.mult, None)
    add_product(core, lambda c, i: core.XNT[:, i * P:(i + 1) * P], lambda c: sign, lambda i: [nt[i // 4], s])


def softplus(core, out, v, bufs, ready):
    p = core.p
    z, w, w2, s = bufs
    o = p.ts(p.dve, z, v, -1.0, None, ALU.mult, None, *ready, free=True)
    o = p.tt(p.dve, z, z, v, ALU.min, o, free=True)
    yield
    o = p.af(z, z, ACT.Exp, o, free=True)
    yield
    o = p.ts(p.dve, w, z, 2.0, None, ALU.add, None, o, free=True)
    o = p.recip(w, w, o, free=True)
    o = p.tt(p.dve, w, w, z, ALU.mult, o, free=True)
    yield
    o = p.tt(p.dve, w2, w, w, ALU.mult, o, free=True)
    o = p.ts(p.dve, s, w2, 1.0 / 17, None, ALU.mult, None, o, free=True)
    yield
    for n in (15, 13, 11, 9, 7, 5, 3):
        o = p.stt(p.dve, s, s, 1.0 / n, w2, ALU.add, ALU.mult, o, free=True)
        if n % 4 == 3:
            yield
    o = p.stt(p.dve, s, s, 1.0, w, ALU.add, ALU.mult, o, free=True)
    o = p.ts(p.dve, z, v, 0.0, None, ALU.max, None, o, free=True)
    return p.stt(p.dve, out, s, 2.0, z, ALU.mult, ALU.add, o, free=True)


def hybrid(core):
    p = core.p
    nt = pre_norm(core)
    O = tmp(core, NT * D).rearrange("p (i d) -> p i d", d=D)
    HT = tmp(core, T)
    r = mean_square(core, NT, lambda i: core.XN[:, i, :], D)
    for i in range(NT):
        n = p.ts(p.dve, O[:, i, :], core.XN[:, i, :], core.rs[:, i:i + 1], None, ALU.mult, None, r, free=i > 0)
    h = transpose_all(core, lambda i: O[:, i, :], lambda q: HT[:, q * BANK:(q + 1) * BANK], lambda i: n, core.weights["s_norm"])
    ready = [*h, core.came.l1]
    narrow(core, HT, HT, core.weights["s_wq"], core.weights["s_wk"], core.weights["s_bq"], core.weights["s_bk"],
                project_values(core, HT, core.weights["s_wv"], core.weights["s_bv_bc"], ready),
                lambda b, n: HT[:, b * S:(b + 1) * S], ready)
    made = p.dve.steps[-1]
    add_product(core, lambda c, i: HT[:, i * P:(i + 1) * P], lambda c: core.weights["s_wo"], lambda i: [made],
                     bias_bc=core.weights["s_bo_bc"], dst=core.XN)
    r = mean_square(core, NT, lambda i: core.XN[:, i, :], D)
    for i in range(NT):
        n = p.stt(p.dve, core.XN[:, i, :], core.XN[:, i, :], core.rs[:, i:i + 1], core.weights["s_normf_bc"],
                  ALU.mult, ALU.mult, r, free=i > 0)
    transpose_all(core, lambda i: core.XN[:, i, :], lambda q: core.XNT[:, q * BANK:(q + 1) * BANK], lambda i: n)
    stage(core)
    state_space(core)
    stage(core)
    G = tmp(core, DFF // P * T).rearrange("p (c t) -> p c t", t=T)
    sg = Ring([tmp(core, BANK) for _ in range(2)])
    for c in range(DFF // P):
        for n in range(QUARTERS):
            gate, gs, gf = core.work.take()
            m = p.mm(gate[:, :], core.weights["s_fc1"][:, DFF + c * P:DFF + (c + 1) * P], core.XNT[:, n * BANK:(n + 1) * BANK],
                     True, True, *gf)
            buf, bs, bf = sg.take()
            e = p.af(buf, gate[:, :], ACT.Silu, m, *bf, free=True)
            core.work.done(gs, e)
            y, ys, yf = core.work.take()
            m = p.mm(y[:, :], core.weights["s_fc1"][:, c * P:(c + 1) * P], core.XNT[:, n * BANK:(n + 1) * BANK], True, True, *yf)
            ff = p.tt(p.dve, G[:, c, n * BANK:(n + 1) * BANK], y[:, :], buf, ALU.mult, m, e, free=True)
            core.work.done(ys, ff)
            sg.done(bs, ff)
    scaled = tmp(core, D)
    a = p.ts(p.pool, scaled, core.weights["ident"], ALPHA, None, ALU.mult, None)
    for n in range(QUARTERS):
        bank, slot, free = core.work.take()
        for j in range(4):
            i = 4 * n + j
            o = bank[:, j * P:(j + 1) * P]
            for c in range(DFF // P):
                p.mm(o, G[:, c, i * P:(i + 1) * P], core.weights["s_fc2"][:, c * D:(c + 1) * D], c == 0, False, ff, *free)
            m = p.mm(o, core.XNT[:, i * P:(i + 1) * P], scaled, False, True, a)
        e = p.cp(p.act, core.XN[:, 4 * n:4 * n + 4, :], bank[:, :].rearrange("p (j d) -> p j d", d=D), m)
        core.work.done(slot, e)
    r = mean_square(core, NT, lambda i: core.XN[:, i, :], D, e)
    for i in range(NT):
        n = p.stt(p.dve, core.XN[:, i, :], core.XN[:, i, :], core.rs[:, i:i + 1], core.weights["s_final_bc"],
                  ALU.mult, ALU.mult, r, free=i > 0)
    p.tt(p.dve, core.X[:, :, :], core.X[:, :, :], core.XN[:, :, :], ALU.add)


def state_space(core):
    p = core.p
    PAIR = 2
    cols = PAIR * HALVES * H_SSM
    pad = D_CONV - 1
    TRI = 3 * P
    Z = Ring([tmp(core, HALVES * D_INNER) for _ in range(7)])
    dts = Ring([tmp(core, 2 * cols) for _ in range(3)])
    soft = [tmp(core, cols) for _ in range(4)]
    XC = Ring([tmp(core, CONV_CH * S) for _ in range(2)])
    xp = Ring([tmp3(core, CONV_CH * (S + pad)) for _ in range(2)])
    conv = Ring([tmp3(core, CONV_CH * S) for _ in range(2)])
    early = Ring([core.XN[:, 8 * n:8 * n + 8, :].rearrange("p i d -> p (i d)") for n in range(2)])
    gm = Ring([tmp(core, TRI) for _ in range(2)])
    xt = Ring([tmp3(core, HALVES * D_INNER) for _ in range(2)])
    xd = Ring([tmp3(core, HALVES * D_INNER) for _ in range(2)])
    skip = Ring([tmp3(core, HALVES * D_INNER) for _ in range(2)])
    wt = Ring([tmp(core, TRI) for _ in range(4)])
    yt = Ring([tmp(core, D_INNER // P * S) for _ in range(2)])
    upto = core.weights["upto"]
    zero = [p.fill(p.pool, x.rearrange("p (c s) -> p c s", c=CONV_CH)[:, :, 0:pad], 0.0) for x in xp.bufs]
    weight = lambda u: lambda n: core.weights[f"m{u // B}_{n}"]
    v4 = lambda ap: ap.rearrange("p (t h w) -> p t h w", t=HALVES, h=H_SSM)
    negA = tmp(core, M_LAYERS * H_SSM)
    for layer in range(M_LAYERS):
        negA_made = p.af(negA[:, layer * H_SSM:(layer + 1) * H_SSM], core.weights[f"m{layer}_alog"], ACT.Exp, core.came.mamba)
    steps, convolved, ready, results, scaled, entered = {}, {}, {}, {}, {}, {}

    def step_sizes(u):
        b, w = u % B, weight(u)
        buf, slot, free = dts.take()
        bank, bs, bf = core.work.take()
        n = PAIR * HALVES
        for j in range(n):
            i = b * HALVES + j
            m = p.mm(bank[:, j * H_SSM:(j + 1) * H_SSM], core.XNT[:, i * P:(i + 1) * P], w("dt"), True, True, *bf, *entered.get(u + j // HALVES, []))
        dt3, a3 = (buf[:, k * cols:(k + 1) * cols].rearrange("p (i h) -> p i h", h=H_SSM) for k in range(2))
        e = p.tt(p.dve, dt3, bank[:, 0:cols].rearrange("p (i h) -> p i h", h=H_SSM),
                 w("dtb").unsqueeze(1).to_broadcast([P, n, H_SSM]), ALU.add, m, *free, free=True)
        core.work.done(bs, e)
        yield
        o = yield from softplus(core, buf[:, 0:cols], buf[:, 0:cols], soft, [e])
        a = negA[:, u // B * H_SSM:(u // B + 1) * H_SSM]
        o = p.stt(p.dve, a3, dt3, -1.0, a.unsqueeze(1).to_broadcast([P, n, H_SSM]), ALU.mult, ALU.mult, o, negA_made, free=True)
        for k in range(PAIR):
            steps[u + k] = (dt3[:, k * HALVES:(k + 1) * HALVES, :], a3[:, k * HALVES:(k + 1) * HALVES, :], slot, o)

    def convolution(u):
        b, w = u % B, weight(u)
        tap = lambda c, k: w("cw")[:, c * D_CONV + k:c * D_CONV + k + 1]
        z, zs, zf = Z.take()
        x, xs, xf = xp.take()
        xv = x.rearrange("p (c s) -> p c s", c=CONV_CH)
        came = []
        for c0 in range(0, CONV_CH, 2):
            bank, slot, free = core.work.take()
            for c in (c0, c0 + 1):
                m = p.mm(bank[:, (c - c0) * S:(c - c0 + 1) * S], w("xbc")[:, c * P:(c + 1) * P],
                         core.XNT[:, b * S:(b + 1) * S], True, True, *free, *entered.get(u, []))
            e = p.cp(p.act, xv[:, c0:c0 + 2, pad:pad + S], bank[:, :].rearrange("p (c s) -> p c s", s=S), m, *xf, free=True)
            core.work.done(slot, e)
            came += [e, e]
            yield
        y, ys, yf = conv.take()
        yv = y.rearrange("p (c s) -> p c s", c=CONV_CH)
        summed = [p.ts(p.dve, yv[:, c, :], xv[:, c, 0:S], tap(c, 0), None, ALU.mult, None, came[c], *yf, *zero, free=True)
                  for c in range(CONV_CH)]
        yield
        for k in range(1, D_CONV):
            summed = [p.stt(p.dve, yv[:, c, :], xv[:, c, k:k + S], tap(c, k), yv[:, c, :], ALU.mult, ALU.add, summed[c], free=True)
                      for c in range(CONV_CH)]
            yield
        xp.done(xs, summed[-1])
        yield
        bank, slot, free = core.work.take()
        for t in range(HALVES):
            i = b * HALVES + t
            m = p.mm(bank[:, t * D_INNER:(t + 1) * D_INNER], core.XNT[:, i * P:(i + 1) * P], w("z"), True, True, *free)
        xc, xcs, xcf = XC.take()
        xcv = xc.rearrange("p (c s) -> p c s", s=S)
        e = [p.af(xcv[:, c, :], yv[:, c, :], ACT.Silu, summed[c], *xcf, bias=w("cb")[:, c:c + 1], free=True) for c in range(CONV_CH)]
        conv.done(ys, *e)
        zc = p.af(z, bank[:, :], ACT.Silu, m, *zf, free=True)
        core.work.done(slot, zc)
        convolved[u] = (xcv, xcs, [*e, zc], z, zs)

    def preparation(u):
        w = weight(u)
        xcv, xcs, silu, z, zs = convolved.pop(u)
        dt3, a3, _, a_made = steps[u]
        el, es, ef = early.take()
        elv = el.rearrange("p (t h s) -> p t h s", t=HALVES, h=H_SSM)
        el_made = p.tt(p.pool, elv, core.weights["after"].unsqueeze(1).unsqueeze(1).to_broadcast([P, HALVES, H_SSM, P]),
                       a3.unsqueeze(3).to_broadcast([P, HALVES, H_SSM, P]), ALU.mult, a_made, *ef, free=True)
        bank, slot, free = core.work.take()
        BT, CTt = xcv[:, 2, :], xcv[:, 3, :]
        p.mm(bank[:, 0:S], BT[:, 0:P], CTt, True, True, *silu, *free)
        m = p.mm(bank[:, S:TRI], BT[:, P:S], CTt[:, P:S], True, True)
        g, gs, gf = gm.take()
        p.tt(p.dve, g[:, 0:P], bank[:, 0:P], upto, ALU.mult, m, *gf, free=True)
        p.cp(p.dve, g[:, P:S], bank[:, P:S], free=True)
        g_made = p.tt(p.dve, g[:, S:TRI], bank[:, S:TRI], upto, ALU.mult, free=True)
        core.work.done(slot, g_made)
        yield
        bank, slot, free = core.work.take()
        for t in range(HALVES):
            for c in range(D_INNER // P):
                m = p.tr(bank[:, t * D_INNER + c * P:t * D_INNER + (c + 1) * P], xcv[:, c, t * P:(t + 1) * P],
                         core.weights["ident"], *silu, *free)
        XC.done(xcs, m)
        xtb, xts, xtf = xt.take()
        xe = p.cp(p.act, xtb, bank[:, :], m, *xtf, free=True)
        core.work.done(slot, xe)
        yield
        xdb, xds, xdf = xd.take()
        xd_made = p.tt(p.pool, v4(xdb), v4(xtb), dt3.unsqueeze(3).to_broadcast([P, HALVES, H_SSM, HP]), ALU.mult, xe, *xdf, free=True)
        sk, sks, skf = skip.take()
        sk_made = p.tt(p.pool, v4(sk), v4(xtb),
                       w("dskip_bc").unsqueeze(1).unsqueeze(3).to_broadcast([P, HALVES, H_SSM, HP]), ALU.mult, *skf, free=True)
        xt.done(xts, sk_made)
        ready[u] = ((elv, es, el_made), (g, gs, g_made), (xdb, xds, xd_made), (sk, sks, sk_made), (z, zs))

    def heads(u):
        (elv, es, el_made), (g, gs, g_made), (xdb, xds, xd_made), (sk, sks, sk_made), (z, zs) = ready.pop(u)
        dt3, a3, dt_slot, _ = steps.pop(u)
        out, oslot, ofree = core.acc.take()

        def result(h, wb, ws, e):
            xh = lambda t: xdb[:, t * D_INNER + h * HP:t * D_INNER + (h + 1) * HP]
            o = lambda t: out[:, t * D_INNER + h * HP:t * D_INNER + (h + 1) * HP]
            p.mm(o(0), wb[:, 0:P], xh(0), True, True, e, xd_made, *ofree)
            p.mm(o(1), wb[:, P:S], xh(0), True, False)
            m = p.mm(o(1), wb[:, S:TRI], xh(1), False, True)
            wt.done(ws, m)
            return m
        pending = []
        for h in range(H_SSM):
            bank, slot, free = core.work.take()
            p.mm(bank[:, 0:S], elv[:, 0, h, :], core.weights["upto2"], True, False, el_made, *free)
            p.mm(bank[:, P:S], a3[:, 1, h:h + 1].to_broadcast([P, P]), upto, False, True)
            m = p.mm(bank[:, S:TRI], elv[:, 1, h, :], upto, True, True)
            wb, ws, wf = wt.take()
            e = p.af(wb, bank[:, 0:TRI], ACT.Exp, m, *wf, free=True)
            core.work.done(slot, e)
            e = p.tt(p.dve, wb, wb, g, ALU.mult, e, g_made, free=True)
            pending.append((h, wb, ws, e))
            if len(pending) > 2:
                result(*pending.pop(0))
            yield
        early.done(es, m)
        gm.done(gs, e)
        while pending:
            m = result(*pending.pop(0))
        xd.done(xds, m)
        if u % PAIR == PAIR - 1:
            dts.done(dt_slot, m, xd_made)
        y = p.tt(p.dve, sk, out[:, :], sk, ALU.add, m, sk_made, free=True)
        core.acc.done(oslot, y)
        y = p.tt(p.pool, z, sk, z, ALU.mult, y, free=True)
        skip.done(sks, y)
        results[u] = (z, zs, y)

    def rms(u):
        n, o = PAIR * HALVES, []
        tiles = [results[u + k][0][:, t * D_INNER:(t + 1) * D_INNER] for k in range(PAIR) for t in range(HALVES)]
        for i, tile in enumerate(tiles):
            o.append(p.bnst(core.stats[:, i, :], tile, results[u + i // HALVES][2], free=True))
        yield
        o = [p.bnag(core.mv[:, i, :], core.stats[:, i, :], o[i], free=True) for i in range(n)]
        m, v = core.mv[:, 0:n, 0], core.mv[:, 0:n, 1]
        x = p.tt(p.dve, m, m, m, ALU.mult, o[-1], free=True)
        x = p.tt(p.dve, v, v, m, ALU.add, x, free=True)
        x = p.ts(p.dve, v, v, 1e-5, None, ALU.add, None, x, free=True)
        yield
        r = core.rs[:, 0:n]
        x = p.af(r, v, ACT.Sqrt, x, free=True)
        yield
        x = p.recip(r, r, x, free=True)
        o = [p.ts(p.dve, tile, tile, core.rs[:, i:i + 1], None, ALU.mult, None, x, free=True) for i, tile in enumerate(tiles)]
        for k in range(PAIR):
            scaled[u + k] = (*results.pop(u + k)[0:2], o[k * HALVES + 1])
        yield

    def project(u):
        b, w = u % B, weight(u)
        z, zs, made = scaled.pop(u)
        bank, slot, free = core.work.take()
        buf, bs, bf = yt.take()
        bv = buf.rearrange("p (c s) -> p c s", s=S)
        for c in range(D_INNER // P):
            for t in range(HALVES):
                m = p.tr(bank[:, c * S + t * P:c * S + (t + 1) * P], z[:, t * D_INNER + c * P:t * D_INNER + (c + 1) * P],
                         core.weights["ident"], made, *free)
        Z.done(zs, m)
        e = [p.ts(p.dve, bv[:, c, :], bank[:, c * S:(c + 1) * S], w("norm")[:, c:c + 1], None, ALU.mult, None, m, *bf, free=True)
             for c in range(D_INNER // P)]
        core.work.done(slot, *e)
        yield
        yield
        bank, slot, free = core.work.take()
        for c in range(D_INNER // P):
            m = p.mm(bank[:, 0:S], w("out")[:, c * D:(c + 1) * D], bv[:, c, :], c == 0, c == D_INNER // P - 1, *e, *free)
        yt.done(bs, m)
        e = p.cp(p.act, core.XNT[:, b * S:(b + 1) * S], bank[:, 0:S], m, free=True)
        core.work.done(slot, e)
        entered[u + B] = [e]

    units = M_LAYERS * B
    merge((step_sizes(0), 1))
    for n in range(units + 5):
        works = [(heads(n - 2), H_SSM)] if 0 <= n - 2 < units else []
        if 0 <= n - 1 < units:
            works.append((preparation(n - 1), 3))
        if n < units:
            works.append((convolution(n), 8))
        if n % PAIR == 1 and n + 1 < units:
            works.append((step_sizes(n + 1), 9))
        if n % PAIR == 0 and 0 <= n - 4 < units:
            works.append((rms(n - 4), 4))
        if 0 <= n - 5 < units:
            works.append((project(n - 5), 3))
        merge(*works)


def raw_attention(core):
    p = core.p
    nt = pre_norm(core)
    ready = [*nt, *core.ctx_in]

    def value_of(b, place, free):
        return [p.cp(p.pool, place(t), core.CX[:, b * HALVES + t, :].rearrange("p (g h w) -> p g h w", g=2, w=HD),
                     *free, *ready) for t in range(HALVES)]
    narrow(core, core.XNT, core.CT, None, None, None, None, value_of,
                lambda b, n: core.XNT[:, b * S:(b + 1) * S], ready)
    made = p.dve.steps[-1]
    add_product(core, lambda c, i: core.XNT[:, i * P:(i + 1) * P], lambda c: core.weights["c_proj"], lambda i: [made],
                     bias_bc=core.weights["c_b_bc"])


def recurrence(core):
    p = core.p
    pre_norm(core)
    cell = Ring([tmp(core, S) for _ in range(2)])
    f, i_, g = (tmp(core, S) for _ in range(3))
    c, cs, _ = cell.take()
    made = p.cp(p.dve, c, core.weights["g_c0"].to_broadcast([P, S]), core.came.l1b)
    for b in range(B):
        ends = []
        for wn, un, bias, dst, func in (("g_wf", "g_uf", "g_bf", f, ACT.Sigmoid), ("g_wi", "g_ui", "g_bi", i_, ACT.Sigmoid),
                                        ("g_wc", "g_uc", "g_bc", g, ACT.Tanh)):
            bank, slot, free = core.work.take()
            p.mm(bank[:, 0:S], core.weights[wn], core.XNT[:, b * S:(b + 1) * S], True, False, *free, *p.act.steps[-1:],
                 *p.dve.steps[-1:])
            m = p.mm(bank[:, 0:S], core.weights[un], c, False, True, made)
            e = p.af(dst, bank[:, 0:S], func, m, made, bias=core.weights[bias], free=True)
            core.work.done(slot, e)
            ends.append(e)
        n, ns, _ = cell.take()
        p.tt(p.dve, n, f, c, ALU.mult, *ends)
        p.tt(p.dve, i_, i_, g, ALU.mult)
        made = p.tt(p.dve, n, n, i_, ALU.add)
        cell.done(cs, made)
        c, cs = n, ns
    out = Ring([tmp(core, BANK) for _ in range(2)])
    for n in range(QUARTERS):
        bank, slot, free = core.work.take()
        for j in range(4):
            i = 4 * n + j
            o = bank[:, j * P:(j + 1) * P]
            p.mm(o, core.XNT[:, i * P:(i + 1) * P], core.weights["g_wo"], True, False, *free)
            m = p.mm(o, c[:, (i % HALVES) * P:(i % HALVES + 1) * P], core.weights["g_uo"], False, True, made)
        buf, bs, bf = out.take()
        bv = buf.rearrange("p (j d) -> p j d", d=D)
        a = p.tt(p.dve, bv, bank[:, :].rearrange("p (j d) -> p j d", d=D),
                 core.weights["g_bo_bc"].unsqueeze(1).to_broadcast([P, 4, D]), ALU.add, m, *bf)
        core.work.done(slot, a)
        e = p.af(buf, buf, ACT.Tanh, a)
        tiles = core.X[:, 4 * n:4 * n + 4, :]
        r = p.tt(p.dve, tiles, tiles, bv, ALU.add, e)
        out.done(bs, r)


def time_mixing(core):
    p = core.p
    normalise(core, core.X, core.XN)
    PADDED = S + 1
    HT = tmp(core, B * PADDED).rearrange("p (b s) -> p b s", s=PADDED)
    zero = p.fill(p.pool, HT[:, :, 0:1], 0.0)
    O = tmp(core, NT * D).rearrange("p (i d) -> p i d", d=D)
    folded = {}
    for name, mix, cols in (("r_wk", "r_mk", D), ("r_wv", "r_mv", D), ("r_wr", "r_mr", D), ("r_wkc", "r_ck", 4 * D),
                            ("r_wrc", "r_cr", D)):
        now, prev, less = tmp2(core, cols), tmp2(core, cols), tmp2(core, 1)
        p.ts(p.pool, less, core.weights[mix], -1.0, 1.0, ALU.mult, ALU.add, core.came.l2)
        p.ts(p.pool, now, core.weights[name], core.weights[mix], None, ALU.mult, None)
        made = p.ts(p.pool, prev, core.weights[name], less, None, ALU.mult, None)
        folded[name] = (now, prev, made)

    def affine_turn(src, n, gname, bname):
        out = []
        for q in range(QUARTERS):
            bank, slot, free = core.work.take()
            for j in range(4):
                i = 4 * q + j
                m = p.tr(bank[:, j * P:(j + 1) * P], src[:, i, :], core.weights["ident"], n, *free)
            e = p.ts(p.dve, HT[:, 2 * q:2 * q + 2, 1:PADDED], bank[:, :].rearrange("p (b s) -> p b s", s=S),
                     core.weights[gname], core.weights[bname], ALU.mult, ALU.add, m, free=True)
            core.work.done(slot, e)
            out.append(e)
        return out
    n = normalise(core, core.XN, O)[-1]
    h = affine_turn(O, n, "r_g1", "r_b1")
    HALF = B // 2
    N = HALF * S
    mark = core.used
    k, v, r, pm, d, c, m_, num = (tmp(core, N) for _ in range(8))
    b3 = lambda ap: ap.rearrange("p (b s) -> p b s", s=S)
    pads = [tmp2(core, HALF * PADDED) for _ in range(3)]
    pmp, sp, aap = (x.rearrange("p (b s) -> p b s", s=PADDED) for x in pads)
    p.fill(p.pool, pmp[:, :, 0:1], BEFORE_ALL)
    p.fill(p.pool, sp[:, :, 0:1], 0.0)
    z = p.fill(p.pool, aap[:, :, 0:1], 0.0)
    last_use = []
    for half in range(2):
        b0 = half * HALF
        for name, dst, func in (("r_wk", k, ACT.Copy), ("r_wv", v, ACT.Copy), ("r_wr", r, ACT.Sigmoid)):
            now, prev, made = folded[name]
            for n2 in range(N // BANK):
                bb = b0 + 2 * n2
                bank, slot, free = core.work.take()
                p.mm(bank[:, :], now, HT[:, bb:bb + 2, 1:PADDED], True, False, *free, made, zero, *h)
                m = p.mm(bank[:, :], prev, HT[:, bb:bb + 2, 0:S], False, True)
                e = p.af(dst[:, n2 * BANK:(n2 + 1) * BANK], bank[:, :], func, m, *last_use, free=True)
                core.work.done(slot, e)
        proj = e
        k3, v3 = b3(k), b3(v)
        P1, S1, A1 = pmp[:, :, 1:PADDED], sp[:, :, 1:PADDED], aap[:, :, 1:PADDED]
        P0, S0, A0 = pmp[:, :, 0:S], sp[:, :, 0:S], aap[:, :, 0:S]
        for j in range(HALF):
            p.scan(pmp[:, j, 1:PADDED], k3[:, j, :], k3[:, j, :], BEFORE_ALL, ALU.max, ALU.max, proj, z, free=j > 0)
        p.tt(p.dve, b3(d), P0, P1, ALU.subtract)
        a = p.tt(p.dve, b3(c), k3, P1, ALU.subtract)
        p.af(d, d, ACT.Exp, a)
        e = p.af(c, c, ACT.Exp)
        for j in range(HALF):
            p.scan(sp[:, j, 1:PADDED], b3(d)[:, j, :], b3(c)[:, j, :], 0.0, ALU.mult, ALU.add, e, free=j > 0)
        p.tt(p.dve, b3(m_), b3(d), S0, ALU.mult)
        p.tt(p.dve, m_, m_, c, ALU.max)
        p.stt(p.dve, c, m_, 1e-8, c, ALU.mult, ALU.add)
        for j in range(HALF):
            s = p.scan(sp[:, j, 1:PADDED], b3(d)[:, j, :], b3(c)[:, j, :], 0.0, ALU.mult, ALU.add, free=j > 0)
        e = p.af(b3(m_), S1, ACT.Ln, s)
        p.tt(p.dve, P1, P1, b3(m_), ALU.add, e)
        p.tt(p.dve, b3(m_), P0, k3, ALU.max)
        p.tt(p.dve, b3(d), P0, b3(m_), ALU.subtract)
        a = p.tt(p.dve, c, k, m_, ALU.subtract)
        p.af(d, d, ACT.Exp, a)
        e = p.af(c, c, ACT.Exp)
        p.tt(p.dve, c, c, v, ALU.mult, e)
        for j in range(HALF):
            p.scan(aap[:, j, 1:PADDED], b3(d)[:, j, :], b3(c)[:, j, :], 0.0, ALU.mult, ALU.add, free=j > 0)
        p.ts(p.dve, k, k, core.weights["r_u"], None, ALU.add, None)
        p.tt(p.dve, b3(m_), P0, k3, ALU.max)
        p.tt(p.dve, b3(d), P0, b3(m_), ALU.subtract)
        a = p.tt(p.dve, c, k, m_, ALU.subtract)
        p.af(d, d, ACT.Exp, a)
        e = p.af(c, c, ACT.Exp)
        p.tt(p.dve, b3(num), b3(d), A0, ALU.mult, e)
        p.tt(p.dve, v, v, c, ALU.mult)
        p.tt(p.dve, num, num, v, ALU.add)
        p.stt(p.dve, d, d, 1e-8, c, ALU.add, ALU.add)
        p.recip(d, d)
        p.tt(p.dve, num, num, d, ALU.mult)
        o = p.tt(p.dve, num, num, r, ALU.mult)
        for n2 in range(N // BANK):
            bank, slot, free = core.work.take()
            for j in range(4):
                m = p.tr(bank[:, j * P:(j + 1) * P], num[:, n2 * BANK + j * P:n2 * BANK + (j + 1) * P], core.weights["ident"], o, *free)
            i = b0 * HALVES + 4 * n2
            xn = core.XN[:, i:i + 4, :]
            e = p.tt(p.dve, xn, xn, bank[:, :].rearrange("p (j d) -> p j d", d=D), ALU.add, m, free=True)
            core.work.done(slot, e)
        last_use = [e]
    core.used = mark
    n = normalise(core, core.XN, O)[-1]
    h = affine_turn(O, n, "r_g2", "r_b2")
    KC = Ring([tmp(core, 4 * BANK) for _ in range(2)])
    RC = Ring([tmp(core, BANK) for _ in range(2)])
    now, prev, made = folded["r_wkc"]
    rnow, rprev, rmade = folded["r_wrc"]
    for q in range(QUARTERS):
        kc, ks, kf = KC.take()
        for g in range(4):
            bank, slot, free = core.work.take()
            p.mm(bank[:, :], now[:, g * P:(g + 1) * P], HT[:, 2 * q:2 * q + 2, 1:PADDED], True, False, *free, made, *h)
            m = p.mm(bank[:, :], prev[:, g * P:(g + 1) * P], HT[:, 2 * q:2 * q + 2, 0:S], False, True)
            kg = kc[:, g * BANK:(g + 1) * BANK]
            a = p.af(kg, bank[:, :], ACT.Relu, m, *kf, *h, free=True)
            core.work.done(slot, a)
            sq = p.tt(p.pool, kg, kg, kg, ALU.mult, a, free=True)
        vb, vs, vf = core.work.take()
        rb, rs_, rf = core.work.take()
        for j in range(4):
            bb, s0 = 2 * q + j // 2, (j % 2) * P
            for g in range(4):
                m = p.mm(vb[:, j * P:(j + 1) * P], kc[:, g * BANK + j * P:g * BANK + (j + 1) * P],
                         core.weights["r_wvc"][:, g * D:(g + 1) * D], g == 0, g == 3, sq, *vf)
            p.mm(rb[:, j * P:(j + 1) * P], HT[:, bb, 1 + s0:1 + s0 + P], rnow, True, False, *rf, rmade)
            m = p.mm(rb[:, j * P:(j + 1) * P], HT[:, bb, s0:s0 + P], rprev, False, True)
        KC.done(ks, m)
        rc, rcs, rcf = RC.take()
        e = p.af(rc, rb[:, :], ACT.Sigmoid, m, *rcf, free=True)
        core.work.done(rs_, e)
        x = p.tt(p.dve, rc, rc, vb[:, :], ALU.mult, e, m)
        core.work.done(vs, x)
        tiles, xn = core.X[:, 4 * q:4 * q + 4, :], core.XN[:, 4 * q:4 * q + 4, :]
        p.tt(p.pool, tiles, tiles, xn, ALU.add)
        x = p.tt(p.dve, tiles, tiles, rc.rearrange("p (j d) -> p j d", d=D), ALU.add, p.pool.steps[-1])
        RC.done(rcs, x)

class Job:

    def __init__(self, src, w, norm, t, view, free, out, keep):
        self.src, self.w, self.norm, self.t = src, w, norm, t
        self.view, self.free, self.out, self.keep = view, free, out, keep
        self.x, self.slot, self.scaled = None, None, None



def wide_attention(core):
    p = core.p
    nt = pre_norm(core)
    SCALE = HW ** -0.5
    qr = Ring([tmp(core, NWIDE * S) for _ in range(2)])
    kr = Ring([tmp2(core, NWIDE * S) for _ in range(2)])
    vr = Ring([tmp2(core, HALVES * H * P), tmp(core, HALVES * H * P)])
    ones = [p.fill(p.pool, columns_of(v, HW, (2 * P, HALVES * H // 2), (1, P)), 1.0) for v in vr.bufs]
    lens_i = tmp(core, B)
    lens = tmp(core, B)
    got = p.dma(lens_i.bitcast(mybir.dt.int32), core.lens_dram)
    p.cp(p.dve, lens, lens_i.bitcast(mybir.dt.int32), got)
    rowm = tmp(core, B * S, BF16).rearrange("p (b s) -> p b s", s=S)
    colm = tmp(core, B * HALVES).rearrange("p (b t) -> p b t", t=HALVES)
    keep = tmp(core, B * S, BF16).rearrange("p (b s) -> p b s", s=S)
    beyond = tmp(core, S)
    steps = core.weights["steps"]
    for b in range(B):
        p.ts(p.dve, keep[:, b, :], steps, lens[:, b:b + 1], None, ALU.is_lt, None)
        p.ts(p.dve, beyond, steps, lens[:, b:b + 1], core.weights["neg_parts"], ALU.is_ge, ALU.mult)
        p.cp(p.dve, rowm[:, b, :], beyond)
        masks = p.ts(p.dve, colm[:, b, :], core.weights["w_pos"], lens[:, b:b + 1], NEG_INF, ALU.is_ge, ALU.mult, core.came.l2x)
    masked = {"row": lambda b: rowm[:, b, :].unsqueeze(1).to_broadcast([P, BANK // S, S]), "ready": [masks, *core.const_ready],
              "column": lambda b, c: colm[:, b, c:c + 1]}
    raw = Ring([core.XN[:, 8 * n:8 * n + 8, :].rearrange("p i d -> p (i d)") for n in range(2)])
    sq = Ring([tmp2(core, H * HW)])
    ms = Ring([tmp(core, H) for _ in range(2)])
    held = {}
    ready0 = [*nt, *core.ctx_in, core.came.l2x, masks, *ones]

    def project(job):
        x, xs, xf = raw.take()
        s2, ss, sf = sq.take()
        for n in range(H * HW // BANK):
            bank, bs, bf = core.work.take()
            cols = slice(n * BANK, (n + 1) * BANK)
            m = p.mm(bank[:, :], job.src, job.w[:, cols], True, True, *bf, *ready0)
            e = p.cp(p.act, x[:, cols], bank[:, :], m, *xf, free=True)
            core.work.done(bs, e)
            yield
        s_ = p.tt(p.pool, s2, x, x, ALU.mult, e, *sf, free=True)
        yield
        r, rs_, rf = ms.take()
        a = p.red(r, s2.rearrange("p (h w) -> p h w", w=HW), ALU.add, s_, *rf, free=True)
        sq.done(ss, a)
        a = p.ts(p.dve, r, r, 1.0 / HW, 1e-5, ALU.mult, ALU.add, a, free=True)
        a = p.af(r, r, ACT.Sqrt, a, free=True)
        yield
        a = p.recip(r, r, a, free=True)
        x3 = x.rearrange("p (h w) -> p h w", w=HW)
        o = p.tt(p.dve, x3, x3, r.unsqueeze(2).to_broadcast([P, H, HW]), ALU.mult, a, free=True)
        ms.done(rs_, o)
        yield
        job.x, job.slot, job.scaled = x, xs, o

    def turned(job):
        t = slice(job.t * P, (job.t + 1) * P)
        for g in range(0, NWIDE, 4):
            bank, bs, bf = core.work.take()
            for j in range(4):
                m = p.tr(bank[:, j * P:(j + 1) * P], job.x[:, (g + j) * P:(g + j + 1) * P], core.weights["ident"], job.scaled, *bf)
            bv = bank[:, :].rearrange("p (w s) -> p w s", s=P)
            if job.keep is not None:
                e = p.stt(p.dve, job.view[:, g:g + 4, t], bv, job.norm, job.keep.unsqueeze(1).to_broadcast([P, 4, P]),
                          ALU.mult, ALU.mult, m, *job.free, free=True)
            else:
                e = p.af(job.view[:, g:g + 4, t], bv, ACT.Copy, m, *job.free, scale=job.norm, free=True)
            core.work.done(bs, e)
            job.out.append(e)
            yield
        raw.done(job.slot, m)

    def prepare(b):
        jobs, slots, views, out = [], [], [], []
        for src, w, norm, ring, keys in ((core.XNT, "w_q", "w_qn", qr, False), (core.CT, "w_k", "w_kn", kr, True)):
            buf, slot, free = ring.take()
            slots.append(slot)
            views.append(buf.rearrange("p (w s) -> p w s", s=S))
            for t in range(HALVES):
                jobs.append(Job(src=src[:, b * S + t * P:b * S + (t + 1) * P], w=core.weights[w], norm=core.weights[norm], t=t,
                                view=views[-1], free=free, out=out, keep=keep[:, b, t * P:(t + 1) * P] if keys else None))
        for n, job in enumerate(jobs):
            yield from project(job)
            if n:
                yield from turned(jobs[n - 1])
        yield from turned(jobs[-1])
        held[b] = slots
        q, k = views
        at = lambda tiles, h: tiles[HW * (h % 2):HW * (h % 2 + 1), h // 2, :]
        return (lambda h: at(q, h)), (lambda h: at(k, h)), out

    def values(b):
        v, slot, free = vr.take()
        out = []
        for t in range(HALVES):
            for n in range(H * HW // BANK):
                bank, bs, bf = core.work.take()
                m = p.mm(bank[:, :], core.CT[:, b * S + t * P:b * S + (t + 1) * P], core.weights["w_v"][:, n * BANK:(n + 1) * BANK],
                         True, True, *bf, *ready0)
                at = columns_of(v, (t * H + n * 8) * P, (2 * P, 4), (P + HW, 2), (1, HW))
                e = p.cp(p.act, at, bank[:, :].rearrange("p (w o d) -> p w o d", o=2, d=HW), m, *free, free=True)
                core.work.done(bs, e)
                out.append(e)
                yield
        held[b].append(slot)
        return (lambda h: [(h % 2, lambda c: v[:, (c * H + h) * P:(c * H + h + 1) * P])]), out
    OT = Ring([tmp(core, NWIDE * S)])
    took = {}

    def dst(b, n):
        if n == 0:
            took[b] = OT.take()
            p.dve.pending += took[b][2]
        return took[b][0][:, n * S:(n + 1) * S]
    divide = divided(core, dst)

    def finish(b, n, bank, last):
        r, _ = divide(b, n, bank, last)
        if n < NWIDE - 1:
            return r, None
        out, slot, _ = took.pop(b)

        def project_back():
            for t in range(HALVES):
                bank2, bs, bf = core.work.take()
                for w in range(NWIDE):
                    m = p.mm(bank2[:, 0:D], out[:, w * S + t * P:w * S + (t + 1) * P], core.weights["w_o"][:, w * D:(w + 1) * D],
                             w == 0, w == NWIDE - 1, r, *bf)
                x = core.X[:, b * HALVES + t, :]
                e = p.tt(p.dve, x, x, bank2[:, 0:D], ALU.add, m, free=True)
                core.work.done(bs, e)
            OT.done(slot, m)
        return r, project_back

    def done(b, last):
        for ring, slot in zip((qr, kr, vr), held.pop(b)):
            ring.done(slot, last)
    attention(core, H, 1, SCALE, prepare, values, finish, done, 32, masked=masked, exps=3)


def route(core, wr, floor):
    p = core.p
    N = NT * E8
    e3 = lambda ap: ap.rearrange("p (i e) -> p i e", e=E8)
    pr, sel, wgt, m, s = tmp(core, N), tmp(core, N), tmp(core, N), tmp(core, NT), tmp(core, NT)
    bank, slot, free = core.work.take()
    for i in range(NT):
        k = p.mm(bank[:, i * E8:(i + 1) * E8], core.XNT[:, i * P:(i + 1) * P], wr, True, True, *free)
    bc = lambda ap: ap.unsqueeze(2).to_broadcast([P, NT, E8])
    p.red(m, e3(bank[:, 0:N]), ALU.max, k)
    a = p.tt(p.dve, e3(pr), e3(bank[:, 0:N]), bc(m), ALU.subtract)
    core.work.done(slot, a)
    e = p.af(pr, pr, ACT.Exp, a)
    p.red(s, e3(pr), ALU.add, e)
    p.recip(s, s)
    p.tt(p.dve, e3(pr), e3(pr), bc(s), ALU.mult)
    cmp_ = tmp(core, N * E8).rearrange("p (i e j) -> p i e j", e=E8, j=E8)
    eq = tmp(core, N * E8).rearrange("p (i e j) -> p i e j", e=E8, j=E8)
    pj = e3(pr).unsqueeze(2).to_broadcast([P, NT, E8, E8])
    pe_ = e3(pr).unsqueeze(3).to_broadcast([P, NT, E8, E8])
    p.tt(p.dve, cmp_, pj, pe_, ALU.is_gt)
    p.tt(p.dve, eq, pj, pe_, ALU.is_equal)
    before = core.weights["before"].rearrange("p (e j) -> p e j", j=E8).unsqueeze(1).to_broadcast([P, NT, E8, E8])
    p.tt(p.dve, eq, eq, before, ALU.mult)
    p.tt(p.dve, cmp_, cmp_, eq, ALU.add)
    p.red(e3(sel), cmp_, ALU.add)
    p.ts(p.dve, sel, sel, 2.0, None, ALU.is_lt, None)
    p.tt(p.dve, wgt, sel, pr, ALU.mult)
    p.red(s, e3(wgt), ALU.add)
    p.ts(p.dve, s, s, 1e-9, None, floor, None)
    p.recip(s, s)
    r = p.tt(p.dve, e3(wgt), e3(wgt), bc(s), ALU.mult)
    return e3(sel), e3(wgt), r


def expert(core, width, w1, b1, w2, func, weight, Y, first, ready, hid):
    p = core.p
    chunks = width // P
    for n in range(QUARTERS):
        buf, bs, bf = hid.take()
        ev = []
        for c in range(chunks):
            bank, slot, free = core.work.take()
            m = p.mm(bank[:, :], w1[:, c * P:(c + 1) * P], core.XNT[:, n * BANK:(n + 1) * BANK], True, True, *free, *ready)
            h = buf[:, c * BANK:(c + 1) * BANK]
            if func is ACT.Relu and c % 2:
                e = p.ts(p.dve, h, bank[:, :], b1[:, c:c + 1], 0.0, ALU.add, ALU.max, m, *bf, free=True)
            else:
                e = p.af(h, bank[:, :], func, m, *bf, bias=b1[:, c:c + 1], free=True)
            core.work.done(slot, e)
            ev.append(e)
        bank, slot, free = core.acc.take()
        for j in range(4):
            for c in range(chunks):
                m = p.mm(bank[:, j * P:(j + 1) * P], buf[:, c * BANK + j * P:c * BANK + (j + 1) * P],
                         w2[:, c * D:(c + 1) * D], c == 0, c == chunks - 1, *free, *ev)
        hid.done(bs, m)
        for j in range(4):
            i = 4 * n + j
            y = Y[:, i, :]
            e = p.stt(p.dve, y, bank[:, j * P:(j + 1) * P], weight(i), y, ALU.mult, ALU.add, m, *first, free=j > 0)
        core.acc.done(slot, e)


def expert_biases(core, wgt, made, b2, Y, ready):
    p = core.p
    wt = tmp(core, T)
    for n in range(QUARTERS):
        bank, slot, free = core.work.take()
        for j in range(4):
            m = p.tr(bank[0:E8, j * P:(j + 1) * P], wgt[:, 4 * n + j, :], core.weights["ident"], made, *free)
        e = p.cp(p.act, wt[0:E8, n * BANK:(n + 1) * BANK], bank[0:E8, :], m, free=True)
        core.work.done(slot, e)
    out = []
    for n in range(QUARTERS):
        bank, slot, free = core.work.take()
        for j in range(4):
            i = 4 * n + j
            m = p.mm(bank[:, j * P:(j + 1) * P], wt[0:E8, i * P:(i + 1) * P], b2[0:E8, :], True, True, e, *free, *ready)
        y = Y[:, 4 * n:4 * n + 4, :]
        e2 = p.tt(p.dve, y, y, bank[:, :].rearrange("p (j d) -> p j d", d=D), ALU.add, m)
        core.work.done(slot, e2)
    return e2


def mixture(core):
    p = core.p
    nt = pre_norm(core)
    p.pe.pending = [*nt, core.came.l2f]
    sel, wgt, made = route(core, core.weights["e_wg"], ALU.add)
    hid = Ring([tmp(core, MOE2_H // P * BANK) for _ in range(2)])
    y = expert_biases(core, wgt, made, core.weights["e_b2"], core.X, [])
    C = MOE2_H // P
    for e in range(E8):
        expert(core, MOE2_H, core.weights["e_w1"][:, e * MOE2_H:(e + 1) * MOE2_H], core.weights["e_b1"][:, e * C:(e + 1) * C],
                    core.weights["e_w2"][:, e * C * D:(e + 1) * C * D], ACT.Relu, lambda i: wgt[:, i, e:e + 1], core.X, [y],
                    [], hid)


def wave_kernels(core):
    p = core.p
    got = core.came.l3a
    col = lambda n: core.weights[n][0:H, :]
    t = core.weights["steps"][0:H, :]
    alpha, damp = tmp(core, 1)[0:H, :], tmp(core, 1)[0:H, :]
    copied = p.cp(p.dve, damp, col("v_damp"), got)
    a = finished(softplus(core, alpha, damp, [tmp(core, 1)[0:H, :] for _ in range(4)], [copied]))
    p.ts(p.dve, alpha, alpha, -1.0, None, ALU.mult, None)
    env, arg, n, ker, s = tmp(core, S)[0:H, :], tmp(core, S)[0:H, :], tmp(core, S)[0:H, :], core.kern[:, :], tmp(core, 1)[0:H, :]
    a = p.dve.steps[-1]
    e = p.af(env, t, ACT.Exp, a, scale=alpha)
    p.ts(p.dve, arg, t, col("v_freq"), col("v_phase"), ALU.mult, ALU.add)
    ROUND = 12582912.0
    p.ts(p.dve, n, arg, 1.0 / (2 * np.pi), 0.25, ALU.mult, ALU.add)
    p.ts(p.dve, n, n, ROUND, None, ALU.add, None)
    p.ts(p.dve, n, n, -ROUND, None, ALU.add, None)
    c1 = 6.28125
    c2 = float(np.float32(np.round((2 * np.pi - c1) * 2 ** 21) / 2 ** 21))
    c3 = float(2 * np.pi - c1 - c2)
    for c in (c1, c2, c3):
        p.stt(p.dve, arg, n, -c, arg, ALU.mult, ALU.add)
    top = float(np.nextafter(np.float32(np.pi), np.float32(0)))
    p.ts(p.dve, arg, arg, float(np.pi / 2), top, ALU.add, ALU.min)
    a = p.ts(p.dve, arg, arg, -top, None, ALU.max, None)
    e2 = p.af(arg, arg, ACT.Sin, a)
    p.tt(p.dve, ker, env, arg, ALU.mult, e, e2)
    p.red(s, ker, ALU.add, mag=True)
    p.ts(p.dve, s, s, 1e-8, None, ALU.max, None)
    p.recip(s, s)
    k = p.ts(p.dve, ker, ker, s, None, ALU.mult, None)
    zero = core.kern_zero[:, :]
    z = p.fill(p.pool, zero, 0.0)
    core.kern_out = [p.dma(core.kern_dram[:, P:P + S], ker, k), p.dma(core.kern_dram[:, 0:P], zero, z)]


def wave(core):
    p = core.p
    nt = pre_norm(core)
    T0 = tmp3(core, H * S).rearrange("p (h s) -> p h s", s=S)
    T1 = tmp3(core, H * P).rearrange("p (h s) -> p h s", s=P)
    kd = core.kern_dram
    diag = lambda parts, shift, n: diagonals(kd, parts, 1 + shift, n)
    there = [*core.kern_out, core.came.l2x, core.came.l2f]
    toe = [p.dma(T0[:, :, :], diag(P, 0, S), *there),
           p.dma(T1[1:P, :, :], diag(P - 1, 1, P), *there),
           p.dma(T1[0:1, :, :], diag(1, 1, P), *there)]
    p.cp(p.pool, T0[:, :, S - 1:S], T0[:, :, S - 2:S - 1], *toe)
    toe = p.cp(p.pool, T1[:, :, P - 1:P], T1[:, :, P - 2:P - 1])
    turned = tmp(core, T)
    by_tile = lambda a: a.rearrange("p (i n) -> p i n", n=P)
    turn = p.cp(p.dve, by_tile(turned), backwards(by_tile(core.XNT[:, :])), *nt)
    F = tmp(core, NT * D).rearrange("p (i d) -> p i d", d=D)
    t1 = Ring([tmp(core, 2 * BANK) for _ in range(2)])
    t2 = Ring([tmp(core, BANK) for _ in range(2)])
    wl = core.came.l3a
    for q in range(NT // 2):
        bank, slot, free = core.work.take()
        for j in range(2):
            i = 2 * q + j
            for n, w in enumerate(("v_wk", "v_wv")):
                m = p.mm(bank[:, n * 2 * P + j * P:n * 2 * P + (j + 1) * P], turned[:, i * P:(i + 1) * P], core.weights[w], True, True, *free, turn, wl)
        kv, ks, kf = t1.take()
        e = p.tt(p.dve, kv[:, 0:BANK].rearrange("p (n j d) -> p n j d", n=2, d=D), bank[:, :].rearrange("p (n j d) -> p n j d", n=2, d=D),
                 core.weights["v_bkv_bc"].rearrange("p (n d) -> p n d", d=D).unsqueeze(2).to_broadcast([P, 2, 2, D]), ALU.add, m, *kf)
        core.work.done(slot, e)
        k, v = kv[:, 0:2 * P], kv[:, 2 * P:4 * P]
        x = kv[:, BANK:BANK + 2 * P]
        a = p.ts(p.dve, x, k, 0.0, None, ALU.min, None)
        e = p.af(x, x, ACT.Exp, a)
        p.stt(p.dve, x, k, 0.0, x, ALU.max, ALU.add, e)
        f = p.tt(p.dve, F[:, 2 * q:2 * q + 2, :], x.rearrange("p (j d) -> p j d", d=D), v.rearrange("p (j d) -> p j d", d=D), ALU.mult)
        t1.done(ks, f)
    Fv = F.rearrange("p (b t) (h d) -> p b t h d", t=HALVES, d=HD)
    CV = tmp(core, NT * D).rearrange("p (i d) -> p i d", d=D)
    CVv = CV.rearrange("p (b t) (h d) -> p t h b d", t=HALVES, d=HD)
    for t in range(HALVES):
        for h0 in range(0, H, 8):
            bank, slot, free = core.work.take()
            for h in range(h0, h0 + 8):
                o = bank[:, (h - h0) * HW:(h - h0 + 1) * HW].rearrange("p (b d) -> p b d", d=HD)
                m = p.mm(o, T0[:, h, t * P:(t + 1) * P], Fv[:, :, 0, h, :], True, t == 0, *free, toe, f)
                if t:
                    m = p.mm(o, T1[:, h, :], Fv[:, :, 1, h, :], False, True)
            q = alternate(p, h0 // 8)
            e = p.cp(q, CVv[:, t, h0:h0 + 8, :, :], bank[:, :].rearrange("p (h b d) -> p h b d", h=8, d=HD), m)
            core.work.done(slot, e)
    convolved = [p.dve.steps[-1], p.act.steps[-1]]
    cp_, cm, ct = tmp(core, H)[0:H, :], tmp(core, 1)[0:H, :], tmp(core, H)[0:H, :]
    C = core.weights["v_coup"][0:H, :]
    p.red(cm, C, ALU.max)
    a = p.ts(p.dve, cp_, C, cm, None, ALU.subtract, None)
    e = p.af(cp_, cp_, ACT.Exp, a)
    p.red(cm, cp_, ALU.add, e)
    p.recip(cm, cm)
    a = p.ts(p.dve, cp_, cp_, cm, None, ALU.mult, None)
    bank, slot, free = core.work.take()
    m = p.tr(bank[0:H, 0:H], cp_, core.weights["ident"][0:H, 0:H], a, *free)
    e = p.cp(p.act, ct, bank[0:H, 0:H], m)
    core.work.done(slot, e)
    bank, slot, free = core.work.take()
    m = p.mm(bank[:, 0:H], core.weights["head_rows"][0:H, :], ct, True, True, e, *free)
    mix = tmp(core, D)
    u = tmp(core, H)
    e = p.cp(p.act, u, bank[:, 0:H], m)
    core.work.done(slot, e)
    mixed = p.tt(p.dve, mix.rearrange("p (i d) -> p i d", d=HD), u.unsqueeze(2).to_broadcast([P, H, HD]),
                 core.weights["same_d"].unsqueeze(1).to_broadcast([P, H, HD]), ALU.mult, e)
    CT_ = tmp(core, T)
    cv = transpose_all(core, lambda i: CV[:, i, :], lambda q: CT_[:, q * BANK:(q + 1) * BANK], lambda i: convolved[0])
    p.pe.pending = convolved
    G = tmp(core, T)
    for q in range(QUARTERS):
        cols = slice(q * BANK, (q + 1) * BANK)
        bank, slot, free = core.work.take()
        m = p.mm(bank[:, :], core.weights["v_wg"], core.XNT[:, cols], True, True, *free)
        e = p.af(G[:, cols], bank[:, :], ACT.Sigmoid, m, bias=core.weights["v_bg"], free=True)
        core.work.done(slot, e)
    for q in range(QUARTERS):
        cols = slice(q * BANK, (q + 1) * BANK)
        bank, slot, free = core.work.take()
        m = p.mm(bank[:, :], core.weights["v_wq"], core.XNT[:, cols], True, True, *free)
        kv, ks, kf = t1.take()
        x, y = kv[:, 0:BANK], kv[:, BANK:2 * BANK]
        p.ts(p.dve, x, bank[:, :], core.weights["v_bq"], 0.0, ALU.add, ALU.min, m, *kf)
        a = p.ts(p.dve, y, bank[:, :], core.weights["v_bq"], 0.0, ALU.add, ALU.max)
        core.work.done(slot, a)
        e2 = p.af(x, x, ACT.Exp, a)
        p.tt(p.dve, x, x, y, ALU.add, e2)
        g = p.tt(p.dve, G[:, cols], G[:, cols], x, ALU.mult, e)
        t1.done(ks, g)
        bank, slot, free = core.work.take()
        m = p.mm(bank[:, :], mix, CT_[:, cols], True, True, mixed, cv[q], *free)
        g = p.tt(p.dve, G[:, cols], G[:, cols], bank[:, :], ALU.mult, m)
        core.work.done(slot, g)
    add_product(core, lambda c, i: G[:, i * P:(i + 1) * P], lambda c: core.weights["v_wo"], lambda i: [g], bias_bc=core.weights["v_bo_bc"])


def guarded_attention(core):
    p = core.p
    nt = pre_norm(core)
    ready = [*nt, core.came.l3x]
    narrow(core, core.XNT, core.CT, core.weights["y_wq"], core.weights["y_wk"], core.weights["y_bq"], core.weights["y_bk"],
                project_values(core, core.CT, core.weights["y_wv"], core.weights["y_bv_bc"], ready),
                lambda b, n: core.XNT[:, b * S:(b + 1) * S], ready)
    above = tmp(core, T)
    p.ts(p.dve, above, core.XNT[:, :], 0.0, None, ALU.max, None)
    made = p.stt(p.dve, core.XNT[:, :], core.XNT[:, :], 0.0, above, ALU.min, ALU.add)
    add_product(core, lambda c, i: core.XNT[:, i * P:(i + 1) * P], lambda c: core.weights["y_wo"], lambda i: [made],
                     bias_bc=core.weights["y_bo_bc"])


def capped_mixture(core):
    p = core.p
    nt = pre_norm(core)
    p.pe.pending = [*nt, core.came.l3f]
    sel, wgt, made = route(core, core.weights["z_wr"], ALU.max)
    N = NT
    el, keep, inc, rank, live = (tmp(core, N) for _ in range(5))
    p.fill(p.dve, live, 1.0)
    for e in range(E8):
        a = p.tt(p.dve, el, sel[:, :, e], live, ALU.mult)
        bank, slot, free = core.work.take()
        p.mm(bank[:, 0:N], core.weights["upto"], el, True, True, a, *free)
        m = p.mm(bank[:, N:2 * N], core.weights["ones"], el, True, True)
        p.cp(p.dve, rank, bank[:, N:2 * N], m)
        p.scan(inc, core.weights["ones"][:, 0:N], rank, 0.0, ALU.mult, ALU.add)
        p.tt(p.dve, rank, inc, rank, ALU.subtract)
        r = p.tt(p.dve, rank, rank, bank[:, 0:N], ALU.add)
        core.work.done(slot, r)
        p.stt(p.dve, keep, rank, float(CAP), el, ALU.is_le, ALU.mult)
        p.tt(p.dve, wgt[:, :, e], wgt[:, :, e], keep, ALU.mult)
        p.tt(p.dve, el, el, keep, ALU.subtract)
        p.tt(p.dve, live, live, el, ALU.subtract)
    made = p.tt(p.dve, wgt, wgt, live.unsqueeze(2).to_broadcast([P, NT, E8]), ALU.mult)
    lost = tmp(core, N)
    p.ts(p.dve, lost, live, -1.0, 1.0, ALU.mult, ALU.add)
    y = expert_biases(core, wgt, made, core.weights["z_b2"], core.X, [])
    for i in range(NT):
        y = p.stt(p.dve, core.X[:, i, :], core.weights["z_fb2_bc"], lost[:, i:i + 1], core.X[:, i, :], ALU.mult, ALU.add, y, free=i > 0)
    hid = Ring([tmp(core, MOE3_H // P * BANK) for _ in range(2)])
    C = MOE3_H // P
    for e in range(E8):
        expert(core, MOE3_H, core.weights["z_w1"][:, e * MOE3_H:(e + 1) * MOE3_H], core.weights["z_b1"][:, e * C:(e + 1) * C],
                    core.weights["z_w2"][:, e * C * D:(e + 1) * C * D], ACT.Gelu, lambda i: wgt[:, i, e:e + 1], core.X, [y], [], hid)
    expert(core, MOE3_H, core.weights["z_fw1"], core.weights["z_fb1"], core.weights["z_fw2"], ACT.Gelu, lambda i: lost[:, i:i + 1], core.X, [y], [], hid)


def begin(core, steps):
    for q in (core.p.pe, core.p.dve, core.p.act, core.p.pool):
        q.pending += steps


def run_blocks(core, blocks):
    p = core.p
    begin(core, [core.x_in, *core.const_ready])
    every = [(product_attention, lambda came: []),
             (context_attention, lambda came: [came.l0]),
             (sign_product, lambda came: [came.l0]),
             (hybrid, lambda came: [came.l1, came.mamba]),
             (raw_attention, lambda came: [came.l1b]),
             (recurrence, lambda came: [came.l1b]),
             (time_mixing, lambda came: [came.l2]),
             (wide_attention, lambda came: [came.l2x]),
             (mixture, lambda came: [came.l2f]),
             (wave, lambda came: [came.l3a]),
             (guarded_attention, lambda came: [came.l3x, came.l2x, came.l2f]),
             (capped_mixture, lambda came: [came.l3f])]
    for n, (block, needs) in enumerate(every):
        stage(core)
        if n == 6:
            wave_kernels(core)
            stage(core)
        if n in blocks:
            if n > 0:
                begin(core, needs(core.came))
            block(core)
        if n == 5:
            stage(core)
            core.came.l2x = load(core, "l2x")
            core.came.l2f = load(core, "l2f")
        if n == 7:
            stage(core)
            core.came.l3f = load(core, "l3f")
    stage(core)
    p.dma(core.out_dram, core.X[:, :, :])


def diagonals(kern, parts, first, n):
    return bass.AP(kern.tensor, kern.offset + first, [[1, parts], [P + S, H], [1, n]])


def backwards(ap):
    *outer, (step, n) = ap.ap
    return bass.AP(ap.tensor, ap.offset + step * (n - 1), [*outer, (-step, n)])


def build(nc, x, ctx_tok, ctx_feat, lens, sel, packs, out, blocks=tuple(range(12))):
    ctx = ExitStack()
    with ctx:
        kern = nc.dram_tensor("wave_kernels", [H, P + S], F32, kind="Internal").ap()
        core = Core()
        start(core, nc, ctx, packs, x, ctx_tok, ctx_feat, lens, kern, out, sel)
        run_blocks(core, blocks)
        block = ctx.enter_context(nc.Block())
        core.p.finish(block)


def tiled(a):
    return np.ascontiguousarray(a.reshape(NT, P, D).transpose(1, 0, 2))


def spread_matrices():
    out = np.zeros((P, 2, 2, 3, P), mybir.dt.np(BF16))
    f = np.arange(P)
    for n, parts in enumerate((QUERY_PARTS, KEY_PARTS)):
        for j, c in enumerate(parts):
            out[f, n, f // (2 * HD) % 2, c, HW * (f // HD % 2) + j * HD + f % HD] = 1
    return out.reshape(P, SPREADS, P)


def col(b):
    return np.ascontiguousarray(b.reshape(-1, P).T) if b.size >= P else b.reshape(-1, 1)


def rep(b):
    return np.broadcast_to(b.reshape(1, -1), (P, b.size))


def chunks(w):
    k, n = w.shape
    return w.reshape(k // P, P, n).transpose(1, 0, 2).reshape(P, -1)


def kernel(**inputs):
    import concourse.bacc as _bacc
    from concourse.bass_utils import run_bass_kernel_spmd as _run
    g = {k: np.asarray(v) for k, v in inputs.items()}
    s = np.arange(S, dtype=np.float32)
    i = np.arange(P)
    vals = {"ident": np.eye(P), "upto": i[:, None] <= i[None, :], "ones": np.ones((P, P)), "after": i[:, None] > i[None, :],
            "steps": np.broadcast_to(s, (P, S)),
            "head_rows": (i[None, :] // HD) == np.arange(H)[:, None], "same_d": (i[:, None] % HD) == np.arange(HD)[None, :],
            "before": np.broadcast_to((np.arange(E8)[None, :] < np.arange(E8)[:, None]).reshape(1, -1), (P, E8 * E8)),
            "w_pos": np.stack([i, i + P], 1), "lower": (i < HW)[:, None], "upper": (i >= HW)[:, None]}
    rest, parts = np.float32(NEG_INF * HW ** 0.5), []
    for _ in range(3):
        parts.append((np.array([rest]).view(np.uint32) & 0xFFFF0000).view(np.float32)[0])
        rest = np.float32(rest - parts[-1])
    vals["neg_parts"] = np.array(parts)[:, None]
    a = "L0_attn_"
    for n in ("q1", "q2", "k1", "k2", "v", "out"):
        vals["a_" + n] = g[a + "W_" + n]
    vals["a_bias_bc"] = rep(np.concatenate([g[a + "b_" + n] for n in ("q1", "q2", "k1", "k2", "v")]))
    vals.update(a_bout_bc=rep(g[a + "b_out"]), a_g=col(g[a + "ln_g"]), a_b=col(g[a + "ln_b"]))
    a = "L0_xattn_"
    vals.update(x_wq=g[a + "Wq"].T, x_wk=g[a + "Wk"].T, x_wv=g[a + "Wv"].T, x_wf=g[a + "Wf"].T, x_bq=col(g[a + "bq"]),
                x_bk=col(g[a + "bk"]), x_bv_bc=rep(g[a + "bv"]), x_bf_bc=rep(g[a + "bf"]), f_w=g["L0_ffn_weight"].T)
    a = "L1_attn_"
    w, b = g[a + "Wqkv_w"].T, g[a + "Wqkv_b"]
    vals.update(s_wq=w[:, :D], s_wk=w[:, D:2 * D], s_wv=w[:, 2 * D:], s_bq=col(b[:D]), s_bk=col(b[D:2 * D]),
                s_bv_bc=rep(b[2 * D:]), s_wo=g[a + "attn_out_w"].T, s_bo_bc=rep(g[a + "attn_out_b"]),
                s_norm=col(g[a + "attn_norm_w"]), s_normf_bc=rep(g[a + "normf_w"]), s_final_bc=rep(g[a + "final_norm_w"]),
                s_fc1=g[a + "fc1_w"].T, s_fc2=chunks(g[a + "fc2_w"].T))
    conv = D_INNER + 2 * D_STATE
    for l in range(M_LAYERS):
        w = g[a + "m_in_w"][l].T
        m = {"z": w[:, :D_INNER], "xbc": w[:, D_INNER:D_INNER + conv], "dt": w[:, D_INNER + conv:],
             "cw": g[a + "m_conv_w"][l].reshape(CONV_CH, P, D_CONV).transpose(1, 0, 2).reshape(P, -1),
             "cb": col(g[a + "m_conv_b"][l]), "dtb": rep(g[a + "m_dt_bias"][l]), "alog": rep(g[a + "m_A_log"][l]),
             "dskip_bc": rep(g[a + "m_D"][l]), "norm": col(g[a + "m_norm_w"][l]), "out": chunks(g[a + "m_out_w"][l].T)}
        vals.update({f"m{l}_{k}": v for k, v in m.items()})
    a = "L1_ffn_"
    vals.update(c_proj=g["L1_xattn_w_proj"].T, c_b_bc=rep(g["L1_xattn_b_proj"]), g_c0=col(g[a + "in_c"]), g_bo_bc=rep(g[a + "bo"]))
    for n in "fico":
        vals["g_w" + n], vals["g_u" + n] = g[a + "w" + n].T, g[a + "u" + n].T
        if n != "o":
            vals["g_b" + n] = col(g[a + "b" + n])
    a = "L2_attn_"
    vals.update(r_u=col(g[a + "time_first"]), r_wk=g[a + "Wk_t"].T, r_wv=g[a + "Wv_t"].T, r_wr=g[a + "Wr_t"].T,
                r_wkc=g[a + "Wk_c"].T, r_wvc=chunks(g[a + "Wv_c"].T), r_wrc=g[a + "Wr_c"].T, r_g1=col(g[a + "ln1_g"]),
                r_b1=col(g[a + "ln1_b"]), r_g2=col(g[a + "ln2_g"]), r_b2=col(g[a + "ln2_b"]), r_mk=col(g[a + "mix_k"]),
                r_mv=col(g[a + "mix_v"]), r_mr=col(g[a + "mix_r"]), r_ck=col(g[a + "cmix_k"]), r_cr=col(g[a + "cmix_r"]))
    a = "L2_xattn_"
    vals.update(w_q=g[a + "Wq"], w_k=g[a + "Wk"], w_v=g[a + "Wv"], w_o=chunks(g[a + "Wo"]),
                w_qn=np.concatenate([g[a + "q_norm_w"]] * 2)[:, None], w_kn=np.concatenate([g[a + "k_norm_w"]] * 2)[:, None])
    a = "L2_ffn_"
    vals.update(e_wg=g[a + "Wg"], e_w1=g[a + "W1"].transpose(1, 0, 2).reshape(P, -1), e_b1=col(g[a + "b1"].ravel()),
                e_w2=np.concatenate([chunks(w) for w in g[a + "W2"]], 1), e_b2=g[a + "b2"])
    a = "L3_attn_"
    w, b = g[a + "Wqkvg"].T, g[a + "bqkvg"]
    vals.update(v_wq=w[:, :D], v_wk=w[:, D:2 * D], v_wv=w[:, 2 * D:3 * D], v_wg=w[:, 3 * D:], v_bq=col(b[:D]),
                v_bkv_bc=rep(b[D:3 * D]), v_bg=col(b[3 * D:]), v_freq=col(g[a + "wave_frequency"]),
                v_damp=col(g[a + "wave_damping"]), v_phase=col(g[a + "wave_phase"]), v_coup=g[a + "field_coupling"],
                v_wo=g[a + "Wout"].T, v_bo_bc=rep(g[a + "bout"]))
    a = "L3_xattn_"
    vals.update(y_wq=g[a + "Wq"].T, y_wk=g[a + "Wk"].T, y_bq=col(g[a + "bq"]), y_bk=col(g[a + "bk"]), y_wv=g[a + "Wv"].T, y_bv_bc=rep(g[a + "bv"]), y_wo=g[a + "Wo"].T,
                y_bo_bc=rep(g[a + "bo"]))
    a = "L3_ffn_"
    vals.update(z_wr=g[a + "Wr"], z_w1=g[a + "W1"].transpose(1, 0, 2).reshape(P, -1), z_b1=col(g[a + "b1"].ravel()),
                z_w2=np.concatenate([chunks(w) for w in g[a + "W2"]], 1), z_b2=g[a + "b2"], z_fw1=g[a + "fw1"],
                z_fb1=col(g[a + "fb1"]), z_fw2=chunks(g[a + "fw2"]), z_fb2_bc=rep(g[a + "fb2"]))

    nc = _bacc.Bacc("TRN2", target_bir_lowering=False, num_devices=1)
    arrays = {"x": tiled(g["x"]), "ctx_tok": tiled(g["ctx_1024"]), "ctx_feat": np.ascontiguousarray(g["ctx_1024"].reshape(T, D).T),
              "lens": np.ascontiguousarray(np.broadcast_to(g["_lenS2"][None, :], (P, B)))}
    for name, layout, _ in PACKS:
        pack = np.zeros((P, columns(layout)), np.float32)
        o = 0
        for n, c in layout:
            v = vals[n]
            assert v.shape[1] == c, (n, v.shape, c)
            pack[:v.shape[0], o:o + c] = v
            o += c
        arrays["pack_" + name] = pack
    sel = np.zeros((P, H, P), mybir.dt.np(BF16))
    for h in range(H):
        sel[h:3 * H:H, h, :] = 1
    arrays["sel"] = np.concatenate([sel, spread_matrices()], 1)
    dram = {k: nc.dram_tensor(k, v.shape, mybir.dt.from_np(v.dtype), kind="ExternalInput").ap() for k, v in arrays.items()}
    out = nc.dram_tensor("out", (P, NT, D), F32, kind="ExternalOutput").ap()
    build(nc, dram["x"], dram["ctx_tok"], dram["ctx_feat"], dram["lens"], dram["sel"],
          {name: dram["pack_" + name] for name, _, _ in PACKS}, out)
    r = _run(nc, [arrays], core_ids=[0])
    y = r.results[0]["out"]
    return np.ascontiguousarray(y.transpose(1, 0, 2)).reshape(B, S, D)
```

```python
import numpy as np
import concourse.bass as bass
import concourse.mybir as mybir
from concourse.alu_op_type import AluOpType as ALU
from contextlib import ExitStack

F32 = mybir.dt.float32
BF16 = mybir.dt.bfloat16
ACT = mybir.ActivationFunctionType
AXX = mybir.AxisListType.X

B, S, D = 8, 256, 128
P = 128
HALVES = S // P
NT = B * HALVES
T = B * S
H = 16
HD = D // H
HW = 64
GROUP = 32
QUERY_PARTS = (0, 0, 1, 1, 0, 2, 1, 2)
KEY_PARTS = (0, 1, 0, 1, 2, 0, 2, 1)
SPREADS = 2 * 2 * 3
NWIDE = H * HW // P
BANK = 512
QUARTERS = T // BANK
M_LAYERS, D_INNER, D_STATE, H_SSM, D_CONV = 4, 256, 128, 4, 4
HP = D_INNER // H_SSM
CONV_CH = (D_INNER + 2 * D_STATE) // P
DFF = 256
ALPHA = 1.68
E8 = 8
MOE2_H = 256
MOE3_H = 512
CAP = max(int(1.25 * (1024 * 2 / E8)), 4)
NEG_INF = -1e9
BEFORE_ALL = -1e30

CONSTS = [("ident", P), ("upto", P), ("ones", P), ("after", P), 
          ("steps", S), ("head_rows", P), ("same_d", HD), ("before", E8 * E8),
          ("neg_parts", 1)]
L0_W = [("a_q1", D), ("a_q2", D), ("a_k1", D), ("a_k2", D), ("a_v", D), ("a_out", D),
        ("a_bias_bc", 5 * D), ("a_bout_bc", D), ("a_g", 1), ("a_b", 1),
        ("x_wq", D), ("x_wk", D), ("x_wv", D), ("x_wf", D), ("x_bq", 1), ("x_bk", 1),
        ("x_bv_bc", D), ("x_bf_bc", D), ("f_w", D)]
L1_W = [("s_wq", D), ("s_wk", D), ("s_bq", 1), ("s_bk", 1),
        ("s_wv", D), ("s_bv_bc", D), ("s_wo", D), ("s_bo_bc", D), ("s_norm", 1), ("s_normf_bc", D),
        ("s_final_bc", D), ("s_fc1", 2 * DFF), ("s_fc2", DFF // P * D)]
M_W = [(f"m{l}_{n}", c) for l in range(M_LAYERS) for n, c in
       [("xbc", CONV_CH * P), ("z", D_INNER), ("dt", H_SSM), ("cw", CONV_CH * D_CONV), ("cb", CONV_CH),
        ("dtb", H_SSM), ("alog", H_SSM), ("dskip_bc", H_SSM), ("norm", D_INNER // P),
        ("out", D_INNER // P * D)]]
L1_W2 = [("c_proj", D), ("c_b_bc", D),
         ("g_wf", D), ("g_uf", D), ("g_wi", D), ("g_ui", D), ("g_wc", D), ("g_uc", D), ("g_wo", D),
         ("g_uo", D), ("g_bf", 1), ("g_bi", 1), ("g_bc", 1), ("g_bo_bc", D), ("g_c0", 1)]
L2_W = [("r_u", 1), ("r_wk", D), ("r_wv", D), ("r_wr", D), ("r_wkc", 4 * D), ("r_wvc", 4 * D),
        ("r_wrc", D), ("r_g1", 1), ("r_b1", 1), ("r_g2", 1), ("r_b2", 1), ("r_mk", 1), ("r_mv", 1),
        ("r_mr", 1), ("r_ck", 1), ("r_cr", 1)]
L2_X = [("w_q", H * HW), ("w_k", H * HW), ("w_v", H * HW), ("w_o", NWIDE * D), ("w_qn", 1), ("w_kn", 1)]
L2_F = [("e_wg", E8), ("e_w1", E8 * MOE2_H), ("e_b1", E8 * MOE2_H // P), ("e_w2", E8 * MOE2_H // P * D),
        ("e_b2", D)]
L3_A = [("v_wq", D), ("v_wk", D), ("v_wv", D), ("v_wg", D), ("v_bq", 1), ("v_bkv_bc", 2 * D), ("v_bg", 1),
        ("v_freq", 1), ("v_damp", 1), ("v_phase", 1), ("v_coup", H), ("v_wo", D), ("v_bo_bc", D)]
L3_X = [("y_wq", D), ("y_wk", D), ("y_bq", 1), ("y_bk", 1), ("y_wv", D),
        ("y_bv_bc", D), ("y_wo", D), ("y_bo_bc", D)]
L3_F = [("z_wr", E8), ("z_w1", E8 * MOE3_H), ("z_b1", E8 * MOE3_H // P), ("z_w2", E8 * MOE3_H // P * D),
        ("z_b2", D), ("z_fw1", MOE3_H), ("z_fb1", MOE3_H // P), ("z_fw2", MOE3_H // P * D), ("z_fb2_bc", D)]
PACKS = [("consts", CONSTS, "keep"), ("l0", L0_W, "early"), ("l1", L1_W, "early"), ("mamba", M_W, "early"),
         ("l1b", L1_W2, "early"), ("l2", L2_W, "keep"), ("l2x", L2_X, "keep"), ("l2f", L2_F, "keep"),
         ("l3a", L3_A, "keep"), ("l3x", L3_X, "keep"), ("l3f", L3_F, "late")]


def columns(pack):
    return sum(c for _, c in pack)


class Step:

    def __init__(self, queue, issue, after):
        self.queue, self.issue, self.after = queue, issue, after
        self.count, self.sem, self.amount = 0, None, 1


class Queue:

    def __init__(self, chained):
        self.steps, self.chained = [], chained
        self.pending = []

    def put(self, issue, after, free=False):
        after = [a for a in after if a is not None]
        if self.pending:
            after += self.pending
            self.pending = []
        if self.chained and not free and self.steps:
            after.append(self.steps[-1])
        step = Step(self, issue, after)
        self.steps.append(step)
        return step

    def emit(self, engine):
        seen = {}
        for step in self.steps:
            need = {}
            for a in step.after:
                if a.count > max(seen.get(id(a.sem), 0), need.get(id(a.sem), (0, None))[0]):
                    need[id(a.sem)] = (a.count, a.sem)
            for key, (count, sem) in need.items():
                engine.wait_ge(sem, count)
                seen[key] = count
            step.issue(engine).then_inc(step.sem, step.amount)


class Ring:

    def __init__(self, bufs):
        self.bufs, self.last, self.at = bufs, [[] for _ in bufs], -1

    def take(self):
        self.at = (self.at + 1) % len(self.bufs)
        assert self.last[self.at] is not None, "the buffer is still in use"
        free, self.last[self.at] = self.last[self.at], None
        return self.bufs[self.at], self.at, free

    def done(self, slot, *readers):
        self.last[slot] = [r for r in readers if r is not None]


class Program:

    def __init__(self, nc, ctx):
        self.nc, self.ctx = nc, ctx
        self.pe, self.dve, self.act, self.pool = Queue(False), Queue(True), Queue(True), Queue(True)
        self.sp = Queue(False)
        self.dmas = []

    def mm(self, out, lhsT, rhs, start, stop, *after):
        return self.pe.put(lambda e: e.matmul(out, lhsT, rhs, start=start, stop=stop, skip_group_check=True), list(after))

    def tr(self, out, in_, ident, *after):
        return self.pe.put(lambda e: e.transpose(out, in_, ident), list(after))

    def tt(self, q, out, a, b, op, *after, free=False):
        return q.put(lambda e: e.tensor_tensor(out, a, b, op), list(after), free)

    def ts(self, q, out, a, s1, s2, op0, op1, *after, free=False):
        if op1 is None:
            return q.put(lambda e: e.tensor_scalar(out, a, s1, None, op0), list(after), free)
        return q.put(lambda e: e.tensor_scalar(out, a, s1, s2, op0, op1), list(after), free)

    def stt(self, q, out, a, s, b, op0, op1, *after, free=False):
        return q.put(lambda e: e.scalar_tensor_tensor(out=out, in0=a, scalar=s, in1=b, op0=op0, op1=op1), list(after), free)

    def cp(self, q, out, a, *after, free=False):
        if q is self.act:
            return q.put(lambda e: e.activation(out, a, ACT.Copy), list(after), free)
        return q.put(lambda e: e.tensor_copy(out, a), list(after), free)

    def af(self, out, a, func, *after, scale=1.0, bias=None, free=False):
        if bias is None:
            return self.act.put(lambda e: e.activation(out, a, func, scale=scale), list(after), free)
        return self.act.put(lambda e: e.activation(out, a, func, scale=scale, bias=bias), list(after), free)

    def red(self, out, a, op, *after, negate=None, mag=None, free=False):
        return self.dve.put(lambda e: e.tensor_reduce(out, a, AXX, op, negate=negate, apply_absolute_value=mag), list(after), free)

    def scan(self, out, a, b, init, op0, op1, *after, free=False):
        return self.dve.put(lambda e: e.tensor_tensor_scan(out, a, b, init, op0, op1), list(after), free)

    def recip(self, out, a, *after, free=False):
        return self.dve.put(lambda e: e.reciprocal(out, a), list(after), free)

    def fill(self, q, out, value, *after, free=False):
        return q.put(lambda e: e.memset(out, value), list(after), free)

    def bnst(self, out, a, *after, free=False):
        return self.dve.put(lambda e: e.bn_stats(out, a), list(after), free)

    def bnag(self, out, a, *after, free=False):
        return self.dve.put(lambda e: e.bn_aggr(out, a), list(after), free)

    def dma(self, out, in_, *after):
        step = self.sp.put(lambda e: e.dma_start(out, in_), list(after))
        step.sem, step.count, step.amount = self.ctx.enter_context(self.nc.semaphore(f"s_dma{len(self.dmas)}")), 16, 16
        self.dmas.append(step)
        return step

    def boundary(self):
        queues = [self.pe, self.dve, self.act, self.pool]
        lasts = [q.steps[-1] for q in queues if q.steps]
        for q in queues + [self.sp]:
            q.pending = q.pending + [s for s in lasts if s.queue is not q or q.chained]

    def finish(self, block):
        for q, name in ((self.pe, "s_pe"), (self.dve, "s_dve"), (self.act, "s_act"), (self.pool, "s_pool")):
            sem = self.ctx.enter_context(self.nc.semaphore(name))
            for n, step in enumerate(q.steps):
                step.sem, step.count = sem, n + 1
        for q, on in ((self.pe, block.tensor), (self.dve, block.vector), (self.act, block.scalar),
                      (self.pool, block.gpsimd), (self.sp, block.sync)):
            on(lambda engine, q=q: self.run(q, engine))

    def run(self, q, engine):
        q.emit(engine)
        if q is self.sp:
            for step in self.dmas:
                engine.wait_ge(step.sem, step.count)


def alternate(p, n):
    return p.act if n % 2 else p.dve


class Loads:
    pass


class Core:
    pass


def start(core, nc, ctx, packs, x_dram, ctx_dram, ctxt_dram, lens_dram, kern_dram, out_dram, sel_dram):
    core.nc, core.ctx = nc, ctx
    p = core.p = Program(nc, ctx)
    core.out_dram, core.kern_dram = out_dram, kern_dram
    sizes = {r: sum(columns(c) for _, c, where in PACKS if where == r) for r in ("keep", "early", "late")}
    keep = sb(core, "w_keep", [P, sizes["keep"]])
    early = sb(core, "w_early", [P, max(sizes["early"], sizes["late"])])
    core.early, core.keep, core.used2, core.used3 = early, keep, 0, 0
    core.l2x_at = columns(CONSTS) + columns(L2_W)
    core.weights, core.pack_dram = {}, packs
    came = core.came = Loads()
    at = {"keep": 0, "early": 0, "late": 0}
    core.pack_dst = {}
    for name, layout, region in PACKS:
        base, buf = at[region], keep if region == "keep" else early
        core.pack_dst[name] = buf[:, base:base + columns(layout)]
        o = base
        for n, c in layout:
            core.weights[n] = buf[:, o:o + c]
            o += c
        at[region] = o
    core.weights["upto2"] = keep[:, P:3 * P]
    core.X = sb(core, "X", [P, NT, D])
    core.XN = sb(core, "XN", [P, NT, D])
    core.XNT = sb(core, "XNT", [P, T])
    core.CT = sb(core, "CT", [P, T])
    core.CX = sb(core, "CX", [P, NT, D])
    core.SEL = sb(core, "SEL", [P, H, P], BF16)
    core.SPREAD = sb(core, "SPREAD", [P, SPREADS, P], BF16)
    core.ONE = sb(core, "ONE", [P, P], BF16)
    core.kern = sb(core, "kern", [H, S])
    core.kern_zero = sb(core, "kern_zero", [H, P])
    core.IDB = sb(core, "IDB", [P, P], BF16)
    core.stats = sb(core, "stats", [P, NT, 6])
    core.mv = sb(core, "mv", [P, NT, 2])
    core.rs = sb(core, "rs", [P, NT])
    left = nc.sbuf_bytes_remaining() if callable(nc.sbuf_bytes_remaining) else nc.sbuf_bytes_remaining
    core.scratch_cols = (left - 2048) // 4
    core.scratch = sb(core, "scratch", [P, core.scratch_cols])
    core.used = 0
    core.banks = [ctx.enter_context(nc.psum_tensor(f"bank{i}", [P, BANK], F32)) for i in range(8)]
    core.work = Ring(core.banks[0:6])
    core.acc = Ring(core.banks[6:8])
    core.x_in = p.dma(core.X[:, :, :], x_dram)
    came.consts = load(core, "consts")
    core.sel_in = p.dma(core.SEL[:, :, :], sel_dram[:, 0:H, :])
    core.spread_in = p.dma(core.SPREAD[:, :, :], sel_dram[:, H:H + SPREADS, :])
    came.l0 = load(core, "l0")
    core.ctx_in = [p.dma(core.CT[:, :], ctxt_dram), p.dma(core.CX[:, :, :], ctx_dram)]
    came.l1 = load(core, "l1")
    came.mamba = load(core, "mamba")
    came.l1b = load(core, "l1b")
    came.l2 = load(core, "l2")
    core.lens_dram = lens_dram
    came.l3a = load(core, "l3a")
    came.l3x = load(core, "l3x")
    one = p.fill(p.pool, core.ONE[:, :], 1.0)
    idb = p.cp(p.dve, core.IDB[:, :], core.weights["ident"], core.came.consts)
    core.const_ready = [one, idb, core.sel_in, core.spread_in]


def sb(core, name, shape, dt=F32):
    return core.ctx.enter_context(core.nc.sbuf_tensor(name, shape, dt))


def tmp3(core, cols):
    at, core.used3 = core.used3, core.used3 + cols
    assert core.used3 <= columns(L2_X) + columns(L2_F)
    return core.keep[:, core.l2x_at + at:core.l2x_at + at + cols]


def load(core, name, *after):
    return core.p.dma(core.pack_dst[name], core.pack_dram[name], *after)


def tmp2(core, cols, dt=F32):
    words = cols if dt == F32 else (cols + 1) // 2
    ap = core.early[:, core.used2:core.used2 + words]
    core.used2 += words
    assert core.used2 <= core.early.shape[1]
    return ap if dt == F32 else ap.bitcast(dt)


def tmp(core, cols, dt=F32):
    words = cols if dt == F32 else (cols + 1) // 2
    ap = core.scratch[:, core.used:core.used + words]
    core.used += words
    assert core.used <= core.scratch_cols, ("scratch", core.used, core.scratch_cols)
    return ap if dt == F32 else ap.bitcast(dt)


def stage(core):
    core.p.boundary()
    core.used = core.used2 = core.used3 = 0


def rstd(core, out, var, n, *after):
    p = core.p
    p.ts(p.dve, var, var, 1e-5, None, ALU.add, None, *after)
    a = p.dve.steps[-1]
    s = p.af(out, var, ACT.Sqrt, a)
    return p.recip(out, out, s)


def normalise(core, src, dst, *after):
    p = core.p
    for i in range(NT):
        p.bnst(core.stats[:, i, :], src[:, i, :], *after, free=i > 0)
    for i in range(NT):
        p.bnag(core.mv[:, i, :], core.stats[:, i, :], free=i > 0)
    r = rstd(core, core.rs[:, :], core.mv[:, :, 1], NT)
    out = []
    for i in range(NT):
        out.append(p.ts(p.dve, dst[:, i, :], src[:, i, :], core.mv[:, i, 0:1], core.rs[:, i:i + 1],
                        ALU.subtract, ALU.mult, r, free=i > 0))
    return out


def mean_square(core, tiles, src, width, *after):
    p = core.p
    for i in range(tiles):
        p.bnst(core.stats[:, i, :], src(i), *after, free=i > 0)
    for i in range(tiles):
        p.bnag(core.mv[:, i, :], core.stats[:, i, :], free=i > 0)
    m, v = core.mv[:, 0:tiles, 0], core.mv[:, 0:tiles, 1]
    p.tt(p.dve, m, m, m, ALU.mult)
    p.tt(p.dve, v, v, m, ALU.add)
    return rstd(core, core.rs[:, 0:tiles], v, tiles)


def transpose_all(core, src, dst, after, scale=None, bias=None):
    p, out = core.p, []
    for n in range(QUARTERS):
        bank, slot, free = core.work.take()
        for j in range(BANK // P):
            i = n * (BANK // P) + j
            t = p.tr(bank[:, j * P:(j + 1) * P], src(i), core.weights["ident"], after(i), core.came.consts, *free)
        d = dst(n)
        if scale is None:
            e = p.cp(alternate(p, n), d, bank[:, :], t, free=True)
        elif bias is None:
            e = p.ts(p.dve, d, bank[:, :], scale, None, ALU.mult, None, t, free=True)
        else:
            e = p.ts(p.dve, d, bank[:, :], scale, bias, ALU.mult, ALU.add, t, free=True)
        core.work.done(slot, e)
        out.append(e)
    return out


def pre_norm(core):
    n = normalise(core, core.X, core.XN)
    return transpose_all(core, lambda i: core.XN[:, i, :], lambda q: core.XNT[:, q * BANK:(q + 1) * BANK], lambda i: n[i])


def add_product(core, lhs, weight, after, pieces=1, bias_bc=None, dst=None):
    p = core.p
    dst = core.X if dst is None else dst
    out = []
    for n in range(QUARTERS):
        bank, slot, free = core.work.take()
        for j in range(BANK // P):
            i = n * (BANK // P) + j
            for c in range(pieces):
                m = p.mm(bank[:, j * P:(j + 1) * P], lhs(c, i), weight(c), c == 0, c == pieces - 1,
                         *after(i), *free)
        tiles = dst[:, n * 4:(n + 1) * 4, :]
        b = bank[:, :].rearrange("p (j d) -> p j d", d=D)
        if bias_bc is not None:
            p.tt(p.pool, tiles, tiles, bias_bc.unsqueeze(1).to_broadcast([P, 4, D]), ALU.add, p.dve.steps[-1])
        e = p.tt(p.dve, tiles, tiles, b, ALU.add, m, p.pool.steps[-1] if p.pool.steps else None, free=True)
        core.work.done(slot, e)
        out.append(e)
    return out


def merge(*works):
    works = [[g, n, 0] for g, n in works]
    while works:
        w = min(works, key=lambda w: w[2] / w[1])
        w[2] += 1
        try:
            next(w[0])
        except StopIteration:
            works.remove(w)


def finished(work):
    while True:
        try:
            next(work)
        except StopIteration as end:
            return end.value


def attention_in_two_passes(core, heads, group, scale, prepare, values, finish, done, pieces):
    p = core.p
    expo = Ring([tmp(core, BANK) for _ in range(4)])
    per_bank = BANK // S
    neg = Ring([tmp(core, HALVES * heads) for _ in range(2)])
    pads = [tmp(core, HALVES * P, BF16) for _ in range(2)]
    part = Ring(pads)
    rest = Ring([tmp(core, HALVES * heads) for _ in range(2)])
    negt = Ring([tmp(core, S, BF16) for _ in range(3)])
    for x in pads:
        cleared = p.fill(p.pool, x, 0.0)
    made = {}
    look = 2
    pending, accs, follow = [], {}, []

    def prepared(b):
        made[b] = [(yield from prepare(b))]

    def maxima(b):
        made[b].append((yield from values(b)))
        q, k, ready = made[b][0]
        ng, ns, nf = neg.take()
        ngv = ng.rearrange("p (t h) -> p t h", h=heads)
        for t in range(HALVES):
            for n in range(heads // per_bank):
                bank, slot, free = core.work.take()
                mine = [4 * (n // 2) + n % 2, 4 * (n // 2) + n % 2 + 2]
                dst = ngv[:, t, :].rearrange("p (a g) -> p g a", g=2)[:, n % 2, 2 * (n // 2):2 * (n // 2) + 2]
                for j, h in enumerate(mine):
                    m = p.mm(bank[:, j * S:(j + 1) * S], q(h)[:, t * P:(t + 1) * P], k(h), True, True, *free, *ready)
                r = p.red(dst, bank[:, 0:per_bank * S].rearrange("p (h s) -> p h s", s=S),
                          ALU.max, m, *nf, negate=True, free=True)
                core.work.done(slot, r)
                yield
        pt, ps_, pf = part.take()
        rt, rs_, rf = rest.take()
        ptv = pt.rearrange("p (t n) -> p t n", n=P)
        rtv = rt.rearrange("p (t h) -> p t h", h=heads)
        cut = lambda n: ptv[:, :, n * heads:(n + 1) * heads]
        x = p.cp(p.dve, cut(0), ngv, r, *pf, cleared, free=True)
        x = p.tt(p.dve, rtv, ngv, cut(0), ALU.subtract, x, *rf, free=True)
        y = p.cp(p.dve, cut(1), rtv, x, free=True)
        x = p.tt(p.dve, rtv, rtv, cut(1), ALU.subtract, y, free=True)
        y = p.cp(p.dve, cut(2), rtv, x, free=True)
        neg.done(ns, x)
        rest.done(rs_, y)
        yield
        yield
        bank, slot, free = core.work.take()
        bankb = bank[:, :].bitcast(BF16)
        for t in range(HALVES):
            m = p.tr(bankb[:, t * P:(t + 1) * P], ptv[:, t, :], core.IDB[:, :], y, *free)
        part.done(ps_, m)
        nt, nts, ntf = negt.take()
        e = p.cp(p.dve, nt, bankb[:, 0:S], m, *ntf, free=True)
        core.work.done(slot, e)
        made[b] += [nt, nts, e]

    def weigh(b):
        (q, k, _), (v, ready), nt, nts, cut = made.pop(b)

        def weighted(h, ex, exs, e):
            n = h // (2 * group)
            if (b, n) not in accs:
                accs[b, n] = core.acc.take()
            acc, slot, free = accs[b, n]
            for half, operand in v(h):
                for c in range(HALVES):
                    m = p.mm(acc[:, half * S:(half + 1) * S], operand(c), ex[:, c * S:(c + 1) * S],
                             c == 0 and h % group == 0, c == HALVES - 1 and h % group == group - 1, e, *free, *ready)
            expo.done(exs, m)
            if h == heads - 1 or (h + 1) % (2 * group) == 0:
                r, then = finish(b, n, acc, m)
                core.acc.done(slot, r)
                if then is not None:
                    follow.append([2, then])
            if h == heads - 1:
                negt.done(nts, m)
                done(b, m)
        for h in range(heads):
            bank, slot, free = core.work.take()
            p.mm(bank[:, :], core.SEL[:, h, :], nt.unsqueeze(1).to_broadcast([P, HALVES, S]), True, False, cut, *free)
            for c in range(HALVES):
                m = p.mm(bank[:, c * S:(c + 1) * S], k(h)[:, c * P:(c + 1) * P], q(h), False, True, cut, *free)
            ex, exs, exf = expo.take()
            e = p.af(ex, bank[:, :], ACT.Exp, m, *exf, scale=scale, free=True)
            core.work.done(slot, e)
            pending.append((weighted, h, ex, exs, e))
            drain(look)
            yield

    def drain(left):
        while len(pending) > left:
            weighted, *head = pending.pop(0)
            weighted(*head)
        for f in follow:
            f[0] -= 1
        while follow and (follow[0][0] <= 0 or not left):
            follow.pop(0)[1]()

    first = heads // per_bank * HALVES + 3
    merge((prepared(0), 1))
    merge((maxima(0), first), (prepared(1), pieces))
    for b in range(B):
        weighing = weigh(b)
        for _ in range(look):
            next(weighing)
        works = [(weighing, heads)]
        if b + 1 < B:
            works.append((maxima(b + 1), first + 2))
        if b + 2 < B:
            works.append((prepared(b + 2), pieces))
        merge(*works)
    drain(0)


def attention(core, heads, group, prepare, values, finish, free_heads, free_values, pieces, mask=None, lag=(3, 2)):
    p = core.p
    expo = Ring([tmp(core, BANK) for _ in range(lag[0] + 1)])
    turned = Ring([tmp(core, BANK) for _ in range(lag[1] + 1)])
    neg = Ring([tmp(core, HALVES) for _ in range(lag[0] + 1)])
    made, accs, behind, further, follow = {}, {}, [], [], []
    count = [0]

    def prepared(b):
        x = yield from prepare(b)
        made[b] = (x, (yield from values(b)))

    def weigh(b):
        (q, k, ready), (v, v_ready) = made.pop(b)

        def turn(h, ex, exs, e):
            bank, slot, free = core.work.take()
            for c in range(HALVES):
                for t in range(HALVES):
                    m = p.tr(bank[:, c * S + t * P:c * S + (t + 1) * P], ex[:, t * S + c * P:t * S + (c + 1) * P],
                             core.weights["ident"], e, *free)
            expo.done(exs, m)
            et, ets, etf = turned.take()
            count[0] += 1
            e = p.cp(p.act if count[0] % 3 == 0 else p.dve, et, bank[:, :], m, *etf, free=True)
            core.work.done(slot, e)
            further.append((weighted, h, et, ets, e))

        def weighted(h, et, ets, e):
            n = h // (2 * group)
            if (b, n) not in accs:
                accs[b, n] = core.acc.take()
            acc, slot, free = accs[b, n]
            for half, operand in v(h):
                for c in range(HALVES):
                    m = p.mm(acc[:, half * S:(half + 1) * S], operand(c), et[:, c * S:(c + 1) * S],
                             c == 0 and h % group == 0, c == HALVES - 1 and h % group == group - 1, e, *free, *v_ready)
            turned.done(ets, m)
            if h == heads - 1 or (h + 1) % (2 * group) == 0:
                r, then = finish(b, n, acc, m)
                core.acc.done(slot, r)
                if then is not None:
                    follow.append([2, then])
            if h == heads - 1:
                free_values(b, m)
        for h in range(heads):
            bank, slot, free = core.work.take()
            if mask is not None:
                parts, mask_ready = mask(b)
                p.mm(bank[:, :], core.ONE[:, :], parts, True, False, *free, *mask_ready)
            for t in range(HALVES):
                m = p.mm(bank[:, t * S:(t + 1) * S], q(h)[:, t * P:(t + 1) * P], k(h), mask is None, True, *free, *ready)
            ng, ns, nf = neg.take()
            r = p.red(ng, bank[:, :].rearrange("p (t s) -> p t s", s=S), ALU.max, m, *nf, negate=True, free=True)
            ex, exs, exf = expo.take()
            for t in range(HALVES):
                e = p.af(ex[:, t * S:(t + 1) * S], bank[:, t * S:(t + 1) * S], ACT.Exp, r, *exf, bias=ng[:, t:t + 1], free=True)
            core.work.done(slot, e)
            neg.done(ns, e)
            if h == heads - 1:
                free_heads(b, m)
            behind.append((turn, h, ex, exs, e))
            drain(*lag)
            yield

    def drain(left, left_further):
        while len(behind) > left:
            turn, *head = behind.pop(0)
            turn(*head)
        while len(further) > left_further:
            weighted, *head = further.pop(0)
            weighted(*head)
        for f in follow:
            f[0] -= 1
        while follow and (follow[0][0] <= 0 or not left):
            follow.pop(0)[1]()

    merge((prepared(0), 1))
    for b in range(B):
        works = [(weigh(b), heads)]
        if b + 1 < B:
            works.append((prepared(b + 1), pieces))
        merge(*works)
    for left in reversed(range(lag[0])):
        drain(left, lag[1])
    drain(0, 0)


def divided(core, dst):
    p = core.p
    inverse = Ring([tmp(core, S) for _ in range(2)])

    def finish(b, n, bank, last):
        inv, slot, free = inverse.take()
        low, high = slice(0, HW), slice(HW, P)
        out = dst(b, n)
        p.cp(p.act, inv[low, :], bank[high, 0:S], last, *free, free=True)
        r = p.cp(p.act, inv[high, :], bank[low, S:2 * S], last, free=True)
        r = p.recip(inv, inv, r, free=True)
        p.tt(p.dve, out[low, :], bank[low, 0:S], inv[low, :], ALU.mult, r, free=True)
        r = p.tt(p.dve, out[high, :], bank[high, S:2 * S], inv[high, :], ALU.mult, r, free=True)
        inverse.done(slot, r)
        return r, None
    return finish


def columns_of(buf, first, *dims):
    return bass.AP(buf.tensor, buf.offset + first, [buf.ap[0], *([step, n] for step, n in dims)])


class NarrowValues:

    COLS = HALVES * H * P

    def __init__(self, core, bufs):
        p = core.p
        self.ring, self.ones = Ring(bufs), []
        half, head = H // 2 * P, P + HD
        for buf in bufs:
            zero = p.fill(p.pool, buf, 0.0)
            for t in range(HALVES):
                self.ones.append(p.fill(p.pool, columns_of(buf, t * H * P + HW, (half - HW, 2), (head, H // 2), (1, HD)), 1.0, zero))

    def place(self, buf, t):
        return columns_of(buf, t * H * P, (H // 2 * P + HW, 2), (P + HD, H // 2), (1, HD))

    def operand(self, buf):
        return lambda h: [(h // (H // 2), lambda c: buf[:, (c * H + h) * P:(c * H + h + 1) * P])]



def narrow(core, qsrc, ksrc, wq, wk, bq, bk, value_of, dst, ready):
    p = core.p
    WIDE = H // 2
    stacks = Ring([tmp(core, 2 * WIDE * S, BF16) for _ in range(3)])
    flat = Ring([tmp(core, 2 * S) for _ in range(2)])
    pieces = Ring([tmp(core, 3 * 2 * S, BF16) for _ in range(2)])
    narrow_values = NarrowValues(core, [tmp3(core, NarrowValues.COLS) for _ in range(2)])
    held = {}

    def prepare(b):
        cols = slice(b * S, (b + 1) * S)
        fl, fs, ff = flat.take()
        x, got = fl.rearrange("p (n s) -> p n s", s=S), []
        if wq is None:
            for n, src in enumerate((qsrc, ksrc)):
                got.append(p.cp(p.pool, x[:, n, :], src[:, cols], *ff, *ready, free=True))
        else:
            bank, bs, bf = core.work.take()
            for n, (src, w) in enumerate(((qsrc, wq), (ksrc, wk))):
                m = p.mm(bank[:, n * S:(n + 1) * S], w, src[:, cols], True, True, *bf, *ready)
            for n, bias in enumerate((bq, bk)):
                got.append(p.af(x[:, n, :], bank[:, n * S:(n + 1) * S], ACT.Identity, m, *ff, bias=bias, free=True))
            core.work.done(bs, got[-1])
        yield
        yield
        pc, pcs, pcf = pieces.take()
        part = lambda c: pc[:, c * 2 * S:(c + 1) * 2 * S]
        o = p.cp(p.dve, part(0), fl, *got, *pcf, free=True)
        o = p.tt(p.dve, fl, fl, part(0), ALU.subtract, o, free=True)
        yield
        o = p.cp(p.dve, part(1), fl, o, free=True)
        o = p.tt(p.dve, part(2), fl, part(1), ALU.subtract, o, free=True)
        flat.done(fs, o)
        yield
        yield
        st, ss, sf = stacks.take()
        view = st.rearrange("p (n w s) -> p n w s", n=2, s=S)
        out = []
        for n in range(2):
            for w0 in range(0, WIDE, 2):
                rows = slice(w0 // 2 * GROUP, (w0 // 2 + 1) * GROUP)
                bank, bs, bf = core.work.take()
                for j in range(2):
                    for c in range(3):
                        m = p.mm(bank[:, j * S:(j + 1) * S], core.SPREAD[rows, (n * 2 + j) * 3 + c, :],
                                 part(c)[rows, n * S:(n + 1) * S], c == 0, c == 2, o, *bf)
                e = p.cp(p.act, view[:, n, w0:w0 + 2, :], bank[:, :].rearrange("p (w s) -> p w s", s=S), m, *sf, free=True)
                core.work.done(bs, e)
                out.append(e)
                yield
        pieces.done(pcs, m)
        held[b] = [ss]
        at = lambda n, h: view[HW * (h % 2):HW * (h % 2 + 1), n, h // 2, :]
        return (lambda h: at(0, h)), (lambda h: at(1, h)), out

    def values(b):
        buf, slot, free = narrow_values.ring.take()
        e = value_of(b, lambda t: narrow_values.place(buf, t), [*free, *narrow_values.ones])
        held[b].append(slot)
        yield
        return narrow_values.operand(buf), e

    def done(b, last):
        for ring, slot in zip((stacks, narrow_values.ring), held.pop(b)):
            ring.done(slot, last)
    attention_in_two_passes(core, H, H // 2, HD ** -0.5, prepare, values, divided(core, dst), done, 14)


def project_values(core, src, w, bias_bc, ready):
    p = core.p

    def value_of(b, place, free):
        bank, bs, bf = core.work.take()
        for t in range(HALVES):
            m = p.mm(bank[:, t * P:(t + 1) * P], src[:, b * S + t * P:b * S + (t + 1) * P], w, True, True, *bf, *ready)
        split = lambda ap: ap.rearrange("p (g h w) -> p g h w", g=2, w=HD)
        out = [p.tt(p.dve, place(t), split(bank[:, t * P:(t + 1) * P]), split(bias_bc), ALU.add, m, *free, free=True)
               for t in range(HALVES)]
        core.work.done(bs, *out)
        return out
    return value_of


def product_attention(core):
    p = core.p
    nt = pre_norm(core)
    O = core.XN
    wsum = tmp(core, 5 * D)
    names = ["a_q1", "a_q2", "a_k1", "a_k2", "a_v"]
    for n, name in enumerate(names):
        weff = p.tt(p.pool, wsum[:, n * D:(n + 1) * D], core.weights[name], core.weights["ident"], ALU.add,
                    core.came.l0, core.came.consts, free=True)
    bias = core.weights["a_bias_bc"]
    flatr = Ring([tmp(core, 4 * D) for _ in range(2)])
    kron = Ring([tmp(core, H * HW) for _ in range(2)])
    qr = Ring([tmp(core, NWIDE * S) for _ in range(2)])
    kr = Ring([tmp3(core, NWIDE * S) for _ in range(2)])
    narrow_values = NarrowValues(core, [tmp(core, NarrowValues.COLS), tmp3(core, NarrowValues.COLS)])
    held, value_slots = {}, {}

    def prepare(b):
        bufs = [r.take() for r in (qr, kr)]
        ready = []
        for t in range(HALVES):
            i = b * HALVES + t
            x = core.XNT[:, i * P:(i + 1) * P]
            bank, bs, bf = core.work.take()
            m = p.mm(bank[:, :], x, wsum[:, 0:4 * D], True, True, *bf, weff, *nt)
            fl, fs, ff = flatr.take()
            e = p.tt(p.dve, fl, bank[:, :], bias[:, 0:4 * D], ALU.add, m, *ff, core.came.l0, free=True)
            core.work.done(bs, e)
            yield
            used = []
            for n, q in ((0, p.dve), (1, p.pool)):
                kb, kbs, kf = kron.take()
                a = fl[:, 2 * n * D:(2 * n + 1) * D].rearrange("p (h i) -> p h i", i=HD).unsqueeze(3).to_broadcast([P, H, HD, HD])
                c = fl[:, (2 * n + 1) * D:(2 * n + 2) * D].rearrange("p (h j) -> p h j", j=HD).unsqueeze(2).to_broadcast([P, H, HD, HD])
                o = p.tt(q, kb.rearrange("p (h i j) -> p h i j", i=HD, j=HD), a, c, ALU.mult, e, *kf)
                used.append(o)
                dst, _, df = bufs[n]
                dv = dst.rearrange("p (w s) -> p w s", s=S)
                for g in range(0, NWIDE, 4):
                    bank, bs, bf = core.work.take()
                    for j in range(4):
                        m = p.tr(bank[:, j * P:(j + 1) * P], kb[:, (g + j) * P:(g + j + 1) * P], core.weights["ident"], o, *bf)
                    bv = bank[:, :].rearrange("p (w s) -> p w s", s=P)
                    ee = p.cp(p.act, dv[:, g:g + 4, t * P:(t + 1) * P], bv, m, *df, free=True)
                    core.work.done(bs, ee)
                    ready.append(ee)
                    yield
                kron.done(kbs, m)
            flatr.done(fs, *used)
        q = bufs[0][0].rearrange("p (w s) -> p w s", s=S)
        k = bufs[1][0].rearrange("p (w s) -> p w s", s=S)
        held[b] = [bufs[0][1], bufs[1][1]]
        at = lambda tiles, h: tiles[HW * (h % 2):HW * (h % 2 + 1), h // 2, :]
        return (lambda h: at(q, h)), (lambda h: at(k, h)), ready
    project = project_values(core, core.XNT, wsum[:, 4 * D:5 * D], bias[:, 4 * D:5 * D], [weff, *nt, core.came.l0])

    def values(b):
        buf, slot, free = narrow_values.ring.take()
        e = project(b, lambda t: narrow_values.place(buf, t), [*free, *narrow_values.ones])
        value_slots[b] = slot
        yield
        return narrow_values.operand(buf), e

    def free_heads(b, last):
        for ring, slot in zip((qr, kr), held.pop(b)):
            ring.done(slot, last)

    def free_values(b, last):
        narrow_values.ring.done(value_slots.pop(b), last)
    attention(core, H, H // 2, prepare, values, divided(core, lambda b, n: core.XNT[:, b * S:(b + 1) * S]),
              free_heads, free_values, 12, lag=(2, 1))
    last = p.dve.steps[-1]
    tr = transpose_all(core, lambda i: core.XNT[:, i * P:(i + 1) * P], lambda q: O[:, 4 * q:4 * q + 4, :].rearrange("p i d -> p (i d)"),
                       lambda i: last)
    p.dve.pending = list(tr)
    n = normalise(core, O, O)
    g = transpose_all(core, lambda i: O[:, i, :], lambda q: core.XNT[:, q * BANK:(q + 1) * BANK], lambda i: n[i],
                  core.weights["a_g"], core.weights["a_b"])
    add_product(core, lambda c, i: core.XNT[:, i * P:(i + 1) * P], lambda c: core.weights["a_out"],
                     lambda i: [g[i // 4]], bias_bc=core.weights["a_bout_bc"])


def context_attention(core):
    p = core.p
    nt = pre_norm(core)
    qr = Ring([tmp(core, S) for _ in range(4)])
    kr = Ring([tmp(core, S) for _ in range(4)])
    vr = Ring([tmp(core, HALVES * D) for _ in range(5)])
    inverse = Ring([tmp(core, S) for _ in range(2)])
    held, value_slots = {}, {}
    scale = 1.0 / 8.0
    bias = tmp(core, 1)
    scaled_bias = p.ts(p.dve, bias, core.weights["x_bq"], scale, None, ALU.mult, None, core.came.l0)
    ready = [*nt, *core.ctx_in, core.came.l0]

    def prepare(b):
        out, slots, aps = [], [], []
        for ring, src, w, shift, factor in ((qr, core.XNT, "x_wq", bias, scale), (kr, core.CT, "x_wk", core.weights["x_bk"], 1.0)):
            buf, slot, free = ring.take()
            bank, bs, bf = core.work.take()
            m = p.mm(bank[:, 0:S], core.weights[w], src[:, b * S:(b + 1) * S], True, True, *bf, *ready)
            e = p.af(buf, bank[:, 0:S], ACT.Identity, m, *free, scaled_bias, scale=factor, bias=shift, free=True)
            core.work.done(bs, e)
            out.append(e)
            slots.append(slot)
            aps.append(buf)
            yield
        held[b] = slots
        q, k = aps
        return (lambda h: q), (lambda h: k), out

    def values(b):
        v, slot, free = vr.take()
        bank, bs, bf = core.work.take()
        for t in range(HALVES):
            m = p.mm(bank[:, t * P:(t + 1) * P], core.CT[:, b * S + t * P:b * S + (t + 1) * P], core.weights["x_wv"], True, True, *bf)
        vv = v.rearrange("p (t w) -> p t w", t=HALVES)
        e = p.tt(p.dve, vv, bank[:, 0:S].rearrange("p (t w) -> p t w", t=HALVES),
                 core.weights["x_bv_bc"].unsqueeze(1).to_broadcast([P, HALVES, D]), ALU.add, m, *free, free=True)
        core.work.done(bs, e)
        value_slots[b] = slot
        yield
        return (lambda h: [(0, lambda c: vv[:, c, :]), (1, lambda c: core.weights["ones"])]), [e]

    def finish(b, n, bank, last):
        inv, slot, free = inverse.take()
        r = p.recip(inv, bank[:, S:2 * S], last, *free, free=True)
        r = p.tt(p.dve, core.XNT[:, b * S:(b + 1) * S], bank[:, 0:S], inv, ALU.mult, r, free=True)
        inverse.done(slot, r)
        return r, None

    def free_heads(b, last):
        for ring, slot in zip((qr, kr), held.pop(b)):
            ring.done(slot, last)

    def free_values(b, last):
        vr.done(value_slots.pop(b), last)
    attention(core, 1, 1, prepare, values, finish, free_heads, free_values, 4, lag=(1, 1))
    made = p.dve.steps[-1]
    act_in = Ring([tmp(core, BANK) for _ in range(2)])
    for n in range(QUARTERS):
        bank, slot, free = core.work.take()
        for j in range(4):
            i = 4 * n + j
            m = p.mm(bank[:, j * P:(j + 1) * P], core.XNT[:, i * P:(i + 1) * P], core.weights["x_wf"], True, True, *free, made)
        buf, bs, bf = act_in.take()
        bv = buf.rearrange("p (j d) -> p j d", d=D)
        a = p.tt(p.dve, bv, bank[:, :].rearrange("p (j d) -> p j d", d=D),
                 core.weights["x_bf_bc"].unsqueeze(1).to_broadcast([P, 4, D]), ALU.add, m, *bf)
        core.work.done(slot, a)
        e = p.af(buf, buf, ACT.Gelu, a)
        tiles = core.X[:, 4 * n:4 * n + 4, :]
        p.tt(p.dve, tiles, tiles, bv, ALU.add, e)
        r = p.tt(p.dve, tiles, tiles, core.CX[:, 4 * n:4 * n + 4, :], ALU.add)
        act_in.done(bs, r)


def sign_product(core):
    p = core.p
    nt = pre_norm(core)
    pos, sign = tmp(core, D), tmp(core, D)
    p.ts(p.dve, pos, core.weights["f_w"], 0.0, None, ALU.is_gt, None, core.came.l0)
    s = p.stt(p.dve, sign, core.weights["f_w"], 0.0, pos, ALU.is_lt, ALU.subtract)
    s = p.ts(p.dve, sign, sign, -1.0, None, ALU.mult, None)
    add_product(core, lambda c, i: core.XNT[:, i * P:(i + 1) * P], lambda c: sign, lambda i: [nt[i // 4], s])


def softplus(core, out, v, bufs, ready):
    p = core.p
    z, w, w2, s = bufs
    o = p.ts(p.dve, z, v, -1.0, None, ALU.mult, None, *ready, free=True)
    o = p.tt(p.dve, z, z, v, ALU.min, o, free=True)
    yield
    o = p.af(z, z, ACT.Exp, o, free=True)
    yield
    o = p.ts(p.dve, w, z, 2.0, None, ALU.add, None, o, free=True)
    o = p.recip(w, w, o, free=True)
    o = p.tt(p.dve, w, w, z, ALU.mult, o, free=True)
    yield
    o = p.tt(p.dve, w2, w, w, ALU.mult, o, free=True)
    o = p.ts(p.dve, s, w2, 1.0 / 17, None, ALU.mult, None, o, free=True)
    yield
    for n in (15, 13, 11, 9, 7, 5, 3):
        o = p.stt(p.dve, s, s, 1.0 / n, w2, ALU.add, ALU.mult, o, free=True)
        if n % 4 == 3:
            yield
    o = p.stt(p.dve, s, s, 1.0, w, ALU.add, ALU.mult, o, free=True)
    o = p.ts(p.dve, z, v, 0.0, None, ALU.max, None, o, free=True)
    return p.stt(p.dve, out, s, 2.0, z, ALU.mult, ALU.add, o, free=True)


def hybrid(core):
    p = core.p
    nt = pre_norm(core)
    O = tmp(core, NT * D).rearrange("p (i d) -> p i d", d=D)
    HT = tmp(core, T)
    r = mean_square(core, NT, lambda i: core.XN[:, i, :], D, *nt)
    for i in range(NT):
        n = p.ts(p.dve, O[:, i, :], core.XN[:, i, :], core.rs[:, i:i + 1], None, ALU.mult, None, r, free=i > 0)
    h = transpose_all(core, lambda i: O[:, i, :], lambda q: HT[:, q * BANK:(q + 1) * BANK], lambda i: n, core.weights["s_norm"])
    ready = [*h, core.came.l1]
    narrow(core, HT, HT, core.weights["s_wq"], core.weights["s_wk"], core.weights["s_bq"], core.weights["s_bk"],
                project_values(core, HT, core.weights["s_wv"], core.weights["s_bv_bc"], ready),
                lambda b, n: HT[:, b * S:(b + 1) * S], ready)
    made = p.dve.steps[-1]
    add_product(core, lambda c, i: HT[:, i * P:(i + 1) * P], lambda c: core.weights["s_wo"], lambda i: [made],
                     bias_bc=core.weights["s_bo_bc"], dst=core.XN)
    r = mean_square(core, NT, lambda i: core.XN[:, i, :], D)
    for i in range(NT):
        n = p.stt(p.dve, core.XN[:, i, :], core.XN[:, i, :], core.rs[:, i:i + 1], core.weights["s_normf_bc"],
                  ALU.mult, ALU.mult, r, free=i > 0)
    transpose_all(core, lambda i: core.XN[:, i, :], lambda q: core.XNT[:, q * BANK:(q + 1) * BANK], lambda i: n)
    stage(core)
    state_space(core)
    stage(core)
    G = tmp(core, DFF // P * T).rearrange("p (c t) -> p c t", t=T)
    sg = Ring([tmp(core, BANK) for _ in range(2)])
    for c in range(DFF // P):
        for n in range(QUARTERS):
            gate, gs, gf = core.work.take()
            m = p.mm(gate[:, :], core.weights["s_fc1"][:, DFF + c * P:DFF + (c + 1) * P], core.XNT[:, n * BANK:(n + 1) * BANK],
                     True, True, *gf)
            buf, bs, bf = sg.take()
            e = p.af(buf, gate[:, :], ACT.Silu, m, *bf, free=True)
            core.work.done(gs, e)
            y, ys, yf = core.work.take()
            m = p.mm(y[:, :], core.weights["s_fc1"][:, c * P:(c + 1) * P], core.XNT[:, n * BANK:(n + 1) * BANK], True, True, *yf)
            ff = p.tt(p.dve, G[:, c, n * BANK:(n + 1) * BANK], y[:, :], buf, ALU.mult, m, e, free=True)
            core.work.done(ys, ff)
            sg.done(bs, ff)
    scaled = tmp(core, D)
    a = p.ts(p.pool, scaled, core.weights["ident"], ALPHA, None, ALU.mult, None)
    for n in range(QUARTERS):
        bank, slot, free = core.work.take()
        for j in range(4):
            i = 4 * n + j
            o = bank[:, j * P:(j + 1) * P]
            for c in range(DFF // P):
                p.mm(o, G[:, c, i * P:(i + 1) * P], core.weights["s_fc2"][:, c * D:(c + 1) * D], c == 0, False, ff, *free)
            m = p.mm(o, core.XNT[:, i * P:(i + 1) * P], scaled, False, True, a)
        e = p.cp(p.act, core.XN[:, 4 * n:4 * n + 4, :], bank[:, :].rearrange("p (j d) -> p j d", d=D), m)
        core.work.done(slot, e)
    r = mean_square(core, NT, lambda i: core.XN[:, i, :], D, e)
    for i in range(NT):
        n = p.stt(p.dve, core.XN[:, i, :], core.XN[:, i, :], core.rs[:, i:i + 1], core.weights["s_final_bc"],
                  ALU.mult, ALU.mult, r, free=i > 0)
    p.tt(p.dve, core.X[:, :, :], core.X[:, :, :], core.XN[:, :, :], ALU.add)


def state_space(core):
    p = core.p
    PAIR = 2
    cols = PAIR * HALVES * H_SSM
    pad = D_CONV - 1
    TRI = 3 * P
    Z = Ring([tmp(core, HALVES * D_INNER) for _ in range(7)])
    dts = Ring([tmp(core, 2 * cols) for _ in range(3)])
    soft = [tmp(core, cols) for _ in range(4)]
    XC = Ring([tmp(core, CONV_CH * S) for _ in range(2)])
    xp = Ring([tmp3(core, CONV_CH * (S + pad)) for _ in range(2)])
    conv = Ring([tmp3(core, CONV_CH * S) for _ in range(2)])
    early = Ring([core.XN[:, 8 * n:8 * n + 8, :].rearrange("p i d -> p (i d)") for n in range(2)])
    gm = Ring([tmp(core, TRI) for _ in range(2)])
    xt = Ring([tmp3(core, HALVES * D_INNER) for _ in range(2)])
    xd = Ring([tmp3(core, HALVES * D_INNER) for _ in range(2)])
    skip = Ring([tmp3(core, HALVES * D_INNER) for _ in range(2)])
    wt = Ring([tmp(core, TRI) for _ in range(4)])
    yt = Ring([tmp(core, D_INNER // P * S) for _ in range(2)])
    upto = core.weights["upto"]
    zero = [p.fill(p.pool, x.rearrange("p (c s) -> p c s", c=CONV_CH)[:, :, 0:pad], 0.0) for x in xp.bufs]
    weight = lambda u: lambda n: core.weights[f"m{u // B}_{n}"]
    v4 = lambda ap: ap.rearrange("p (t h w) -> p t h w", t=HALVES, h=H_SSM)
    negA = tmp(core, M_LAYERS * H_SSM)
    for layer in range(M_LAYERS):
        negA_made = p.af(negA[:, layer * H_SSM:(layer + 1) * H_SSM], core.weights[f"m{layer}_alog"], ACT.Exp, core.came.mamba)
    steps, convolved, ready, results, scaled, entered = {}, {}, {}, {}, {}, {}

    def step_sizes(u):
        b, w = u % B, weight(u)
        buf, slot, free = dts.take()
        bank, bs, bf = core.work.take()
        n = PAIR * HALVES
        for j in range(n):
            i = b * HALVES + j
            m = p.mm(bank[:, j * H_SSM:(j + 1) * H_SSM], core.XNT[:, i * P:(i + 1) * P], w("dt"), True, True, *bf, *entered.get(u + j // HALVES, []))
        dt3, a3 = (buf[:, k * cols:(k + 1) * cols].rearrange("p (i h) -> p i h", h=H_SSM) for k in range(2))
        e = p.tt(p.dve, dt3, bank[:, 0:cols].rearrange("p (i h) -> p i h", h=H_SSM),
                 w("dtb").unsqueeze(1).to_broadcast([P, n, H_SSM]), ALU.add, m, *free, free=True)
        core.work.done(bs, e)
        yield
        o = yield from softplus(core, buf[:, 0:cols], buf[:, 0:cols], soft, [e])
        a = negA[:, u // B * H_SSM:(u // B + 1) * H_SSM]
        o = p.stt(p.dve, a3, dt3, -1.0, a.unsqueeze(1).to_broadcast([P, n, H_SSM]), ALU.mult, ALU.mult, o, negA_made, free=True)
        for k in range(PAIR):
            steps[u + k] = (dt3[:, k * HALVES:(k + 1) * HALVES, :], a3[:, k * HALVES:(k + 1) * HALVES, :], slot, o)

    def convolution(u):
        b, w = u % B, weight(u)
        tap = lambda c, k: w("cw")[:, c * D_CONV + k:c * D_CONV + k + 1]
        z, zs, zf = Z.take()
        x, xs, xf = xp.take()
        xv = x.rearrange("p (c s) -> p c s", c=CONV_CH)
        came = []
        for c0 in range(0, CONV_CH, 2):
            bank, slot, free = core.work.take()
            for c in (c0, c0 + 1):
                m = p.mm(bank[:, (c - c0) * S:(c - c0 + 1) * S], w("xbc")[:, c * P:(c + 1) * P],
                         core.XNT[:, b * S:(b + 1) * S], True, True, *free, *entered.get(u, []))
            e = p.cp(p.act, xv[:, c0:c0 + 2, pad:pad + S], bank[:, :].rearrange("p (c s) -> p c s", s=S), m, *xf, free=True)
            core.work.done(slot, e)
            came += [e, e]
            yield
        y, ys, yf = conv.take()
        yv = y.rearrange("p (c s) -> p c s", c=CONV_CH)
        summed = [p.ts(p.dve, yv[:, c, :], xv[:, c, 0:S], tap(c, 0), None, ALU.mult, None, came[c], *yf, *zero, free=True)
                  for c in range(CONV_CH)]
        yield
        for k in range(1, D_CONV):
            summed = [p.stt(p.dve, yv[:, c, :], xv[:, c, k:k + S], tap(c, k), yv[:, c, :], ALU.mult, ALU.add, summed[c], free=True)
                      for c in range(CONV_CH)]
            yield
        xp.done(xs, summed[-1])
        yield
        bank, slot, free = core.work.take()
        for t in range(HALVES):
            i = b * HALVES + t
            m = p.mm(bank[:, t * D_INNER:(t + 1) * D_INNER], core.XNT[:, i * P:(i + 1) * P], w("z"), True, True, *free)
        xc, xcs, xcf = XC.take()
        xcv = xc.rearrange("p (c s) -> p c s", s=S)
        e = [p.af(xcv[:, c, :], yv[:, c, :], ACT.Silu, summed[c], *xcf, bias=w("cb")[:, c:c + 1], free=True) for c in range(CONV_CH)]
        conv.done(ys, *e)
        zc = p.af(z, bank[:, :], ACT.Silu, m, *zf, free=True)
        core.work.done(slot, zc)
        convolved[u] = (xcv, xcs, [*e, zc], z, zs)

    def preparation(u):
        w = weight(u)
        xcv, xcs, silu, z, zs = convolved.pop(u)
        dt3, a3, _, a_made = steps[u]
        el, es, ef = early.take()
        elv = el.rearrange("p (t h s) -> p t h s", t=HALVES, h=H_SSM)
        el_made = p.tt(p.pool, elv, core.weights["after"].unsqueeze(1).unsqueeze(1).to_broadcast([P, HALVES, H_SSM, P]),
                       a3.unsqueeze(3).to_broadcast([P, HALVES, H_SSM, P]), ALU.mult, a_made, *ef, free=True)
        bank, slot, free = core.work.take()
        BT, CTt = xcv[:, 2, :], xcv[:, 3, :]
        p.mm(bank[:, 0:S], BT[:, 0:P], CTt, True, True, *silu, *free)
        m = p.mm(bank[:, S:TRI], BT[:, P:S], CTt[:, P:S], True, True)
        g, gs, gf = gm.take()
        p.tt(p.dve, g[:, 0:P], bank[:, 0:P], upto, ALU.mult, m, *gf, free=True)
        p.cp(p.dve, g[:, P:S], bank[:, P:S], free=True)
        g_made = p.tt(p.dve, g[:, S:TRI], bank[:, S:TRI], upto, ALU.mult, free=True)
        core.work.done(slot, g_made)
        yield
        bank, slot, free = core.work.take()
        for t in range(HALVES):
            for c in range(D_INNER // P):
                m = p.tr(bank[:, t * D_INNER + c * P:t * D_INNER + (c + 1) * P], xcv[:, c, t * P:(t + 1) * P],
                         core.weights["ident"], *silu, *free)
        XC.done(xcs, m)
        xtb, xts, xtf = xt.take()
        xe = p.cp(p.act, xtb, bank[:, :], m, *xtf, free=True)
        core.work.done(slot, xe)
        yield
        xdb, xds, xdf = xd.take()
        xd_made = p.tt(p.pool, v4(xdb), v4(xtb), dt3.unsqueeze(3).to_broadcast([P, HALVES, H_SSM, HP]), ALU.mult, xe, *xdf, free=True)
        sk, sks, skf = skip.take()
        sk_made = p.tt(p.pool, v4(sk), v4(xtb),
                       w("dskip_bc").unsqueeze(1).unsqueeze(3).to_broadcast([P, HALVES, H_SSM, HP]), ALU.mult, *skf, free=True)
        xt.done(xts, sk_made)
        ready[u] = ((elv, es, el_made), (g, gs, g_made), (xdb, xds, xd_made), (sk, sks, sk_made), (z, zs))

    def heads(u):
        (elv, es, el_made), (g, gs, g_made), (xdb, xds, xd_made), (sk, sks, sk_made), (z, zs) = ready.pop(u)
        _, a3, dt_slot, _ = steps.pop(u)
        out, oslot, ofree = core.acc.take()
        multiplied = []

        def result(h, wb, ws, e):
            xh = lambda t: xdb[:, t * D_INNER + h * HP:t * D_INNER + (h + 1) * HP]
            o = lambda t: out[:, t * D_INNER + h * HP:t * D_INNER + (h + 1) * HP]
            p.mm(o(0), wb[:, 0:P], xh(0), True, True, e, xd_made, *ofree)
            p.mm(o(1), wb[:, P:S], xh(0), True, False)
            m = p.mm(o(1), wb[:, S:TRI], xh(1), False, True)
            wt.done(ws, m)
            return m
        pending = []
        for h in range(H_SSM):
            bank, slot, free = core.work.take()
            p.mm(bank[:, 0:S], elv[:, 0, h, :], core.weights["upto2"], True, False, el_made, *free)
            p.mm(bank[:, P:S], a3[:, 1, h:h + 1].to_broadcast([P, P]), upto, False, True)
            m = p.mm(bank[:, S:TRI], elv[:, 1, h, :], upto, True, True)
            wb, ws, wf = wt.take()
            e = p.af(wb, bank[:, 0:TRI], ACT.Exp, m, *wf, free=True)
            core.work.done(slot, e)
            e = p.tt(p.pool if h % 2 else p.dve, wb, wb, g, ALU.mult, e, g_made, free=True)
            multiplied.append(e)
            pending.append((h, wb, ws, e))
            if len(pending) > 2:
                result(*pending.pop(0))
            yield
        early.done(es, m)
        gm.done(gs, *multiplied[-2:])
        while pending:
            m = result(*pending.pop(0))
        xd.done(xds, m)
        if u % PAIR == PAIR - 1:
            dts.done(dt_slot, m, xd_made)
        y = p.tt(p.dve, sk, out[:, :], sk, ALU.add, m, sk_made, free=True)
        core.acc.done(oslot, y)
        y = p.tt(p.pool, z, sk, z, ALU.mult, y, free=True)
        skip.done(sks, y)
        results[u] = (z, zs, y)

    def rms(u):
        n, o = PAIR * HALVES, []
        tiles = [results[u + k][0][:, t * D_INNER:(t + 1) * D_INNER] for k in range(PAIR) for t in range(HALVES)]
        for i, tile in enumerate(tiles):
            o.append(p.bnst(core.stats[:, i, :], tile, results[u + i // HALVES][2], free=True))
        yield
        o = [p.bnag(core.mv[:, i, :], core.stats[:, i, :], o[i], free=True) for i in range(n)]
        m, v = core.mv[:, 0:n, 0], core.mv[:, 0:n, 1]
        x = p.tt(p.dve, m, m, m, ALU.mult, o[-1], free=True)
        x = p.tt(p.dve, v, v, m, ALU.add, x, free=True)
        x = p.ts(p.dve, v, v, 1e-5, None, ALU.add, None, x, free=True)
        yield
        r = core.rs[:, 0:n]
        x = p.af(r, v, ACT.Sqrt, x, free=True)
        yield
        x = p.recip(r, r, x, free=True)
        o = [p.ts(p.pool, tile, tile, core.rs[:, i:i + 1], None, ALU.mult, None, x, free=True) for i, tile in enumerate(tiles)]
        for k in range(PAIR):
            scaled[u + k] = (*results.pop(u + k)[0:2], o[k * HALVES + 1])
        yield

    def project(u):
        b, w = u % B, weight(u)
        z, zs, made = scaled.pop(u)
        bank, slot, free = core.work.take()
        buf, bs, bf = yt.take()
        bv = buf.rearrange("p (c s) -> p c s", s=S)
        for c in range(D_INNER // P):
            for t in range(HALVES):
                m = p.tr(bank[:, c * S + t * P:c * S + (t + 1) * P], z[:, t * D_INNER + c * P:t * D_INNER + (c + 1) * P],
                         core.weights["ident"], made, *free)
        Z.done(zs, m)
        e = [p.ts(p.dve, bv[:, c, :], bank[:, c * S:(c + 1) * S], w("norm")[:, c:c + 1], None, ALU.mult, None, m, *bf, free=True)
             for c in range(D_INNER // P)]
        core.work.done(slot, *e)
        yield
        yield
        bank, slot, free = core.work.take()
        for c in range(D_INNER // P):
            m = p.mm(bank[:, 0:S], w("out")[:, c * D:(c + 1) * D], bv[:, c, :], c == 0, c == D_INNER // P - 1, *e, *free)
        yt.done(bs, m)
        e = p.cp(p.act, core.XNT[:, b * S:(b + 1) * S], bank[:, 0:S], m, free=True)
        core.work.done(slot, e)
        entered[u + B] = [e]

    units = M_LAYERS * B
    merge((step_sizes(0), 1))
    for n in range(units + 5):
        works = [(heads(n - 2), H_SSM)] if 0 <= n - 2 < units else []
        if 0 <= n - 1 < units:
            works.append((preparation(n - 1), 3))
        if n < units:
            works.append((convolution(n), 8))
        if n % PAIR == 1 and n + 1 < units:
            works.append((step_sizes(n + 1), 9))
        if n % PAIR == 0 and 0 <= n - 4 < units:
            works.append((rms(n - 4), 4))
        if 0 <= n - 5 < units:
            works.append((project(n - 5), 3))
        merge(*works)


def raw_attention(core):
    p = core.p
    nt = pre_norm(core)
    ready = [*nt, *core.ctx_in]

    def value_of(b, place, free):
        return [p.cp(p.pool, place(t), core.CX[:, b * HALVES + t, :].rearrange("p (g h w) -> p g h w", g=2, w=HD),
                     *free, *ready) for t in range(HALVES)]
    narrow(core, core.XNT, core.CT, None, None, None, None, value_of,
                lambda b, n: core.XNT[:, b * S:(b + 1) * S], ready)
    made = p.dve.steps[-1]
    add_product(core, lambda c, i: core.XNT[:, i * P:(i + 1) * P], lambda c: core.weights["c_proj"], lambda i: [made],
                     bias_bc=core.weights["c_b_bc"])


def recurrence(core):
    p = core.p
    nt = pre_norm(core)
    cell = Ring([tmp(core, S) for _ in range(2)])
    f, i_, g = (tmp(core, S) for _ in range(3))
    c, cs, _ = cell.take()
    made = p.cp(p.dve, c, core.weights["g_c0"].to_broadcast([P, S]), core.came.l1b)
    first = (c, cs, made)
    gates = (("g_wf", "g_uf", "g_bf", f, ACT.Sigmoid), ("g_wi", "g_ui", "g_bi", i_, ACT.Sigmoid), ("g_wc", "g_uc", "g_bc", g, ACT.Tanh))

    def inputs(b):
        out = []
        for wn, *_ in gates:
            bank, slot, free = core.work.take()
            p.mm(bank[:, 0:S], core.weights[wn], core.XNT[:, b * S:(b + 1) * S], True, False, *free, *nt)
            out.append((bank, slot))
        return out
    state = []

    def recur():
        c, cs, made = first
        coming = inputs(0)
        for b in range(B):
            ends = []
            banks, coming = coming, inputs(b + 1) if b + 1 < B else None
            for (bank, slot), (_, un, bias, dst, func) in zip(banks, gates):
                m = p.mm(bank[:, 0:S], core.weights[un], c, False, True, made)
                e = p.af(dst, bank[:, 0:S], func, m, made, bias=core.weights[bias], free=True)
                core.work.done(slot, e)
                ends.append(e)
            n, ns, _ = cell.take()
            p.tt(p.dve, n, f, c, ALU.mult, *ends)
            p.tt(p.dve, i_, i_, g, ALU.mult)
            made = p.tt(p.dve, n, n, i_, ALU.add)
            cell.done(cs, made)
            c, cs = n, ns
            yield
        state.append((c, made))
    merge((recur(), B), (wave_kernels(core), 12))
    c, made = state[0]
    out = Ring([tmp(core, BANK) for _ in range(2)])
    for n in range(QUARTERS):
        bank, slot, free = core.work.take()
        for j in range(4):
            i = 4 * n + j
            o = bank[:, j * P:(j + 1) * P]
            p.mm(o, core.XNT[:, i * P:(i + 1) * P], core.weights["g_wo"], True, False, *free)
            m = p.mm(o, c[:, (i % HALVES) * P:(i % HALVES + 1) * P], core.weights["g_uo"], False, True, made)
        buf, bs, bf = out.take()
        bv = buf.rearrange("p (j d) -> p j d", d=D)
        a = p.tt(p.dve, bv, bank[:, :].rearrange("p (j d) -> p j d", d=D),
                 core.weights["g_bo_bc"].unsqueeze(1).to_broadcast([P, 4, D]), ALU.add, m, *bf)
        core.work.done(slot, a)
        e = p.af(buf, buf, ACT.Tanh, a)
        tiles = core.X[:, 4 * n:4 * n + 4, :]
        r = p.tt(p.dve, tiles, tiles, bv, ALU.add, e)
        out.done(bs, r)


def time_mixing(core):
    p = core.p
    normalise(core, core.X, core.XN)
    PADDED = S + 1
    HT = tmp(core, B * PADDED).rearrange("p (b s) -> p b s", s=PADDED)
    zero = p.fill(p.pool, HT[:, :, 0:1], 0.0)
    mark = core.used
    O = tmp(core, NT * D).rearrange("p (i d) -> p i d", d=D)
    folded = {}
    for name, mix, cols in (("r_wk", "r_mk", D), ("r_wv", "r_mv", D), ("r_wr", "r_mr", D), ("r_wkc", "r_ck", 4 * D),
                            ("r_wrc", "r_cr", D)):
        now, prev, less = tmp2(core, cols), tmp2(core, cols), tmp2(core, 1)
        p.ts(p.pool, less, core.weights[mix], -1.0, 1.0, ALU.mult, ALU.add, core.came.l2)
        p.ts(p.pool, now, core.weights[name], core.weights[mix], None, ALU.mult, None)
        made = p.ts(p.pool, prev, core.weights[name], less, None, ALU.mult, None)
        folded[name] = (now, prev, made)

    def affine_turn(src, n, gname, bname):
        out = []
        for q in range(QUARTERS):
            bank, slot, free = core.work.take()
            for j in range(4):
                i = 4 * q + j
                m = p.tr(bank[:, j * P:(j + 1) * P], src[:, i, :], core.weights["ident"], n, *free)
            e = p.ts(p.dve, HT[:, 2 * q:2 * q + 2, 1:PADDED], bank[:, :].rearrange("p (b s) -> p b s", s=S),
                     core.weights[gname], core.weights[bname], ALU.mult, ALU.add, m, free=True)
            core.work.done(slot, e)
            out.append(e)
        return out
    n = normalise(core, core.XN, O)[-1]
    h = affine_turn(O, n, "r_g1", "r_b1")
    core.used = mark
    PART = B // 4
    N = PART * S
    b3 = lambda ap: ap.rearrange("p (b s) -> p b s", s=S)

    def stream(part):
        k, v, r, d, c, m_, num = (tmp(core, N) for _ in range(7))
        pmp, sp, aap = (tmp2(core, PART * PADDED).rearrange("p (b s) -> p b s", s=PADDED) for _ in range(3))
        p.fill(p.pool, pmp[:, :, 0:1], BEFORE_ALL)
        p.fill(p.pool, sp[:, :, 0:1], 0.0)
        z = p.fill(p.pool, aap[:, :, 0:1], 0.0)
        b0 = part * PART
        last = [z]

        def then(kind, *args, **kw):
            last[:] = [kind(*args, *last, free=True, **kw)]
        for name, dst, func in (("r_wk", k, ACT.Copy), ("r_wv", v, ACT.Copy), ("r_wr", r, ACT.Sigmoid)):
            now, prev, made = folded[name]
            bank, slot, free = core.work.take()
            p.mm(bank[:, :], now, HT[:, b0:b0 + PART, 1:PADDED], True, False, *free, made, zero, *h)
            m = p.mm(bank[:, :], prev, HT[:, b0:b0 + PART, 0:S], False, True)
            last.append(p.af(dst, bank[:, :], func, m, free=True))
            core.work.done(slot, last[-1])
        yield
        k3 = b3(k)
        P1, S1 = pmp[:, :, 1:PADDED], sp[:, :, 1:PADDED]
        P0, S0, A0 = pmp[:, :, 0:S], sp[:, :, 0:S], aap[:, :, 0:S]
        for j in range(PART):
            then(p.scan, pmp[:, j, 1:PADDED], k3[:, j, :], k3[:, j, :], BEFORE_ALL, ALU.max, ALU.max)
        yield
        then(p.tt, p.dve, b3(d), P0, P1, ALU.subtract)
        yield
        then(p.tt, p.pool, b3(c), k3, P1, ALU.subtract)
        yield
        then(p.af, d, d, ACT.Exp)
        then(p.af, c, c, ACT.Exp)
        yield
        for j in range(PART):
            then(p.scan, sp[:, j, 1:PADDED], b3(d)[:, j, :], b3(c)[:, j, :], 0.0, ALU.mult, ALU.add)
        yield
        then(p.tt, p.pool, b3(m_), b3(d), S0, ALU.mult)
        yield
        then(p.tt, p.dve, m_, m_, c, ALU.max)
        then(p.stt, p.dve, c, m_, 1e-8, c, ALU.mult, ALU.add)
        yield
        for j in range(PART):
            then(p.scan, sp[:, j, 1:PADDED], b3(d)[:, j, :], b3(c)[:, j, :], 0.0, ALU.mult, ALU.add)
        yield
        then(p.af, b3(m_), S1, ACT.Ln)
        yield
        then(p.tt, p.dve, P1, P1, b3(m_), ALU.add)
        yield
        then(p.tt, p.dve, b3(m_), P0, k3, ALU.max)
        yield
        then(p.tt, p.pool, b3(d), P0, b3(m_), ALU.subtract)
        yield
        then(p.tt, p.dve, c, k, m_, ALU.subtract)
        yield
        then(p.af, d, d, ACT.Exp)
        then(p.af, c, c, ACT.Exp)
        yield
        then(p.tt, p.pool, c, c, v, ALU.mult)
        yield
        for j in range(PART):
            then(p.scan, aap[:, j, 1:PADDED], b3(d)[:, j, :], b3(c)[:, j, :], 0.0, ALU.mult, ALU.add)
        yield
        then(p.ts, p.dve, k, k, core.weights["r_u"], None, ALU.add, None)
        then(p.tt, p.dve, b3(m_), P0, k3, ALU.max)
        yield
        then(p.tt, p.pool, b3(d), P0, b3(m_), ALU.subtract)
        yield
        then(p.tt, p.dve, c, k, m_, ALU.subtract)
        yield
        then(p.af, d, d, ACT.Exp)
        then(p.af, c, c, ACT.Exp)
        yield
        then(p.tt, p.pool, b3(num), b3(d), A0, ALU.mult)
        yield
        then(p.tt, p.pool, v, v, c, ALU.mult)
        yield
        then(p.stt, p.dve, d, d, 1e-8, c, ALU.add, ALU.add)
        then(p.recip, d, d)
        yield
        then(p.tt, p.pool, num, num, v, ALU.add)
        yield
        then(p.tt, p.dve, num, num, d, ALU.mult)
        then(p.tt, p.dve, num, num, r, ALU.mult)
        yield
        bank, slot, free = core.work.take()
        for j in range(4):
            m = p.tr(bank[:, j * P:(j + 1) * P], num[:, j * P:(j + 1) * P], core.weights["ident"], *last, *free)
        i = b0 * HALVES
        xn = core.XN[:, i:i + 4, :]
        e = p.tt(p.dve, xn, xn, bank[:, :].rearrange("p (j d) -> p j d", d=D), ALU.add, m, free=True)
        core.work.done(slot, e)
    merge(*[(stream(part), 1) for part in range(4)])
    core.used = mark
    O = tmp(core, NT * D).rearrange("p (i d) -> p i d", d=D)
    n = normalise(core, core.XN, O)[-1]
    h = affine_turn(O, n, "r_g2", "r_b2")
    KC = Ring([tmp(core, 4 * BANK) for _ in range(2)])
    RC = Ring([tmp(core, BANK) for _ in range(2)])
    now, prev, made = folded["r_wkc"]
    rnow, rprev, rmade = folded["r_wrc"]
    for q in range(QUARTERS):
        kc, ks, kf = KC.take()
        for g in range(4):
            bank, slot, free = core.work.take()
            p.mm(bank[:, :], now[:, g * P:(g + 1) * P], HT[:, 2 * q:2 * q + 2, 1:PADDED], True, False, *free, made, *h)
            m = p.mm(bank[:, :], prev[:, g * P:(g + 1) * P], HT[:, 2 * q:2 * q + 2, 0:S], False, True)
            kg = kc[:, g * BANK:(g + 1) * BANK]
            a = p.af(kg, bank[:, :], ACT.Relu, m, *kf, *h, free=True)
            core.work.done(slot, a)
            sq = p.tt(p.pool, kg, kg, kg, ALU.mult, a, free=True)
        vb, vs, vf = core.work.take()
        rb, rs_, rf = core.work.take()
        for j in range(4):
            bb, s0 = 2 * q + j // 2, (j % 2) * P
            for g in range(4):
                m = p.mm(vb[:, j * P:(j + 1) * P], kc[:, g * BANK + j * P:g * BANK + (j + 1) * P],
                         core.weights["r_wvc"][:, g * D:(g + 1) * D], g == 0, g == 3, sq, *vf)
            p.mm(rb[:, j * P:(j + 1) * P], HT[:, bb, 1 + s0:1 + s0 + P], rnow, True, False, *rf, rmade)
            m = p.mm(rb[:, j * P:(j + 1) * P], HT[:, bb, s0:s0 + P], rprev, False, True)
        KC.done(ks, m)
        rc, rcs, rcf = RC.take()
        e = p.af(rc, rb[:, :], ACT.Sigmoid, m, *rcf, free=True)
        core.work.done(rs_, e)
        x = p.tt(p.dve, rc, rc, vb[:, :], ALU.mult, e, m)
        core.work.done(vs, x)
        tiles, xn = core.X[:, 4 * q:4 * q + 4, :], core.XN[:, 4 * q:4 * q + 4, :]
        p.tt(p.pool, tiles, tiles, xn, ALU.add)
        x = p.tt(p.dve, tiles, tiles, rc.rearrange("p (j d) -> p j d", d=D), ALU.add, p.pool.steps[-1])
        RC.done(rcs, x)

class Job:

    def __init__(self, src, w, norm, t, view, free, out, keep):
        self.src, self.w, self.norm, self.t = src, w, norm, t
        self.view, self.free, self.out, self.keep = view, free, out, keep
        self.x, self.slot, self.scaled = None, None, None



def wide_attention(core):
    p = core.p
    nt = pre_norm(core)
    query_norm = tmp(core, 1)
    norm_made = p.ts(p.dve, query_norm, core.weights["w_qn"], HW ** -0.5, None, ALU.mult, None, core.came.l2x)
    qr = Ring([tmp(core, NWIDE * S) for _ in range(2)])
    kr = Ring([tmp2(core, NWIDE * S) for _ in range(2)])
    vr = Ring([tmp2(core, HALVES * H * P), tmp(core, HALVES * H * P)])
    ones = [p.fill(p.pool, columns_of(v, HW, (2 * P, HALVES * H // 2), (1, P)), 1.0) for v in vr.bufs]
    lens_i = tmp(core, B)
    lens = tmp(core, B)
    got = p.dma(lens_i.bitcast(mybir.dt.int32), core.lens_dram)
    p.cp(p.dve, lens, lens_i.bitcast(mybir.dt.int32), got)
    rowm = tmp(core, B * S, BF16).rearrange("p (b s) -> p b s", s=S)
    keep = tmp(core, B * S, BF16).rearrange("p (b s) -> p b s", s=S)
    beyond = tmp(core, S)
    steps = core.weights["steps"]
    for b in range(B):
        p.ts(p.dve, keep[:, b, :], steps, lens[:, b:b + 1], None, ALU.is_lt, None)
        p.ts(p.dve, beyond, steps, lens[:, b:b + 1], core.weights["neg_parts"], ALU.is_ge, ALU.mult)
        p.cp(p.dve, rowm[:, b, :], beyond)
    masks = p.dve.steps[-1]
    raw = Ring([core.XN[:, 8 * n:8 * n + 8, :].rearrange("p i d -> p (i d)") for n in range(2)])
    sq = Ring([tmp2(core, H * HW)])
    ms = Ring([tmp(core, H) for _ in range(2)])
    held, value_slots = {}, {}
    ready0 = [*nt, *core.ctx_in, core.came.l2x, masks, norm_made, *ones]

    def project(job):
        x, xs, xf = raw.take()
        s2, ss, sf = sq.take()
        for n in range(H * HW // BANK):
            bank, bs, bf = core.work.take()
            cols = slice(n * BANK, (n + 1) * BANK)
            m = p.mm(bank[:, :], job.src, job.w[:, cols], True, True, *bf, *ready0)
            e = p.cp(p.act, x[:, cols], bank[:, :], m, *xf, free=True)
            core.work.done(bs, e)
            yield
        s_ = p.tt(p.pool, s2, x, x, ALU.mult, e, *sf, free=True)
        yield
        r, rs_, rf = ms.take()
        a = p.red(r, s2.rearrange("p (h w) -> p h w", w=HW), ALU.add, s_, *rf, free=True)
        sq.done(ss, a)
        a = p.ts(p.dve, r, r, 1.0 / HW, 1e-5, ALU.mult, ALU.add, a, free=True)
        a = p.af(r, r, ACT.Sqrt, a, free=True)
        yield
        a = p.recip(r, r, a, free=True)
        x3 = x.rearrange("p (h w) -> p h w", w=HW)
        o = p.tt(p.dve, x3, x3, r.unsqueeze(2).to_broadcast([P, H, HW]), ALU.mult, a, free=True)
        ms.done(rs_, o)
        yield
        job.x, job.slot, job.scaled = x, xs, o

    def turned(job):
        t = slice(job.t * P, (job.t + 1) * P)
        for g in range(0, NWIDE, 4):
            bank, bs, bf = core.work.take()
            for j in range(4):
                m = p.tr(bank[:, j * P:(j + 1) * P], job.x[:, (g + j) * P:(g + j + 1) * P], core.weights["ident"], job.scaled, *bf)
            bv = bank[:, :].rearrange("p (w s) -> p w s", s=P)
            if job.keep is not None:
                e = p.stt(p.dve, job.view[:, g:g + 4, t], bv, job.norm, job.keep.unsqueeze(1).to_broadcast([P, 4, P]),
                          ALU.mult, ALU.mult, m, *job.free, free=True)
            else:
                e = p.af(job.view[:, g:g + 4, t], bv, ACT.Copy, m, *job.free, scale=job.norm, free=True)
            core.work.done(bs, e)
            job.out.append(e)
            yield
        raw.done(job.slot, m)

    def prepare(b):
        jobs, slots, views, out = [], [], [], []
        for src, w, norm, ring, keys in ((core.XNT, "w_q", query_norm, qr, False), (core.CT, "w_k", core.weights["w_kn"], kr, True)):
            buf, slot, free = ring.take()
            slots.append(slot)
            views.append(buf.rearrange("p (w s) -> p w s", s=S))
            for t in range(HALVES):
                jobs.append(Job(src=src[:, b * S + t * P:b * S + (t + 1) * P], w=core.weights[w], norm=norm, t=t,
                                view=views[-1], free=free, out=out, keep=keep[:, b, t * P:(t + 1) * P] if keys else None))
        for n, job in enumerate(jobs):
            yield from project(job)
            if n:
                yield from turned(jobs[n - 1])
        yield from turned(jobs[-1])
        held[b] = slots
        q, k = views
        at = lambda tiles, h: tiles[HW * (h % 2):HW * (h % 2 + 1), h // 2, :]
        return (lambda h: at(q, h)), (lambda h: at(k, h)), out

    def values(b):
        v, slot, free = vr.take()
        out = []
        for t in range(HALVES):
            for n in range(H * HW // BANK):
                bank, bs, bf = core.work.take()
                m = p.mm(bank[:, :], core.CT[:, b * S + t * P:b * S + (t + 1) * P], core.weights["w_v"][:, n * BANK:(n + 1) * BANK],
                         True, True, *bf, *ready0)
                at = columns_of(v, (t * H + n * 8) * P, (2 * P, 4), (P + HW, 2), (1, HW))
                e = p.cp(p.act, at, bank[:, :].rearrange("p (w o d) -> p w o d", o=2, d=HW), m, *free, free=True)
                core.work.done(bs, e)
                out.append(e)
                yield
        value_slots[b] = slot
        return (lambda h: [(h % 2, lambda c: v[:, (c * H + h) * P:(c * H + h + 1) * P])]), out
    OT = Ring([tmp(core, NWIDE * S)])
    took = {}

    def dst(b, n):
        if n == 0:
            took[b] = OT.take()
            p.dve.pending += took[b][2]
        return took[b][0][:, n * S:(n + 1) * S]
    divide = divided(core, dst)

    def finish(b, n, bank, last):
        r, _ = divide(b, n, bank, last)
        if n < NWIDE - 1:
            return r, None
        out, slot, _ = took.pop(b)

        def project_back():
            for t in range(HALVES):
                bank2, bs, bf = core.work.take()
                for w in range(NWIDE):
                    m = p.mm(bank2[:, 0:D], out[:, w * S + t * P:w * S + (t + 1) * P], core.weights["w_o"][:, w * D:(w + 1) * D],
                             w == 0, w == NWIDE - 1, r, *bf)
                x = core.X[:, b * HALVES + t, :]
                e = p.tt(p.dve, x, x, bank2[:, 0:D], ALU.add, m, free=True)
                core.work.done(bs, e)
            OT.done(slot, m)
        return r, project_back

    def free_heads(b, last):
        for ring, slot in zip((qr, kr), held.pop(b)):
            ring.done(slot, last)

    def free_values(b, last):
        vr.done(value_slots.pop(b), last)
    attention(core, H, 1, prepare, values, finish, free_heads, free_values, 36,
              mask=lambda b: (rowm[:, b, :].unsqueeze(1).to_broadcast([P, BANK // S, S]), [masks, *core.const_ready]), lag=(3, 1))


def route(core, wr, floor):
    p = core.p
    N = NT * E8
    e3 = lambda ap: ap.rearrange("p (i e) -> p i e", e=E8)
    pr, sel, wgt, m, s = tmp(core, N), tmp(core, N), tmp(core, N), tmp(core, NT), tmp(core, NT)
    bank, slot, free = core.work.take()
    for i in range(NT):
        k = p.mm(bank[:, i * E8:(i + 1) * E8], core.XNT[:, i * P:(i + 1) * P], wr, True, True, *free)
    bc = lambda ap: ap.unsqueeze(2).to_broadcast([P, NT, E8])
    p.red(m, e3(bank[:, 0:N]), ALU.max, k)
    a = p.tt(p.dve, e3(pr), e3(bank[:, 0:N]), bc(m), ALU.subtract)
    core.work.done(slot, a)
    e = p.af(pr, pr, ACT.Exp, a)
    yield
    p.red(s, e3(pr), ALU.add, e)
    p.recip(s, s)
    p.tt(p.dve, e3(pr), e3(pr), bc(s), ALU.mult)
    cmp_ = tmp(core, N * E8).rearrange("p (i e j) -> p i e j", e=E8, j=E8)
    eq = tmp(core, N * E8).rearrange("p (i e j) -> p i e j", e=E8, j=E8)
    pj = e3(pr).unsqueeze(2).to_broadcast([P, NT, E8, E8])
    pe_ = e3(pr).unsqueeze(3).to_broadcast([P, NT, E8, E8])
    p.tt(p.dve, cmp_, pj, pe_, ALU.is_gt)
    yield
    p.tt(p.dve, eq, pj, pe_, ALU.is_equal)
    before = core.weights["before"].rearrange("p (e j) -> p e j", j=E8).unsqueeze(1).to_broadcast([P, NT, E8, E8])
    p.tt(p.dve, eq, eq, before, ALU.mult)
    yield
    p.tt(p.dve, cmp_, cmp_, eq, ALU.add)
    p.red(e3(sel), cmp_, ALU.add)
    yield
    p.ts(p.dve, sel, sel, 2.0, None, ALU.is_lt, None)
    p.tt(p.dve, wgt, sel, pr, ALU.mult)
    p.red(s, e3(wgt), ALU.add)
    p.ts(p.dve, s, s, 1e-9, None, floor, None)
    p.recip(s, s)
    r = p.tt(p.dve, e3(wgt), e3(wgt), bc(s), ALU.mult)
    return e3(sel), e3(wgt), r


def run_experts(core, experts, width, func, Y, routing, steps, depth):
    p = core.p
    chunks = width // P
    hid = Ring([tmp(core, chunks * BANK) for _ in range(depth + 1)])
    waiting = []

    def up(expert, n):
        w1, b1, _, _ = expert
        buf, bs, bf = hid.take()
        ev = []
        for c in range(chunks):
            bank, slot, free = core.work.take()
            m = p.mm(bank[:, :], w1[:, c * P:(c + 1) * P], core.XNT[:, n * BANK:(n + 1) * BANK], True, True, *free)
            h = buf[:, c * BANK:(c + 1) * BANK]
            if func is ACT.Relu and c % 2:
                e = p.ts(p.dve, h, bank[:, :], b1[:, c:c + 1], 0.0, ALU.add, ALU.max, m, *bf, free=True)
            else:
                e = p.af(h, bank[:, :], func, m, *bf, bias=b1[:, c:c + 1], free=True)
            core.work.done(slot, e)
            ev.append(e)
        waiting.append((expert, n, buf, bs, ev))

    def down():
        (_, _, w2, weight), n, buf, bs, ev = waiting.pop(0)
        bank, slot, free = core.acc.take()
        for j in range(4):
            for c in range(chunks):
                m = p.mm(bank[:, j * P:(j + 1) * P], buf[:, c * BANK + j * P:c * BANK + (j + 1) * P],
                         w2[:, c * D:(c + 1) * D], c == 0, c == chunks - 1, *free, *ev)
        hid.done(bs, m)
        for j in range(4):
            y = Y[:, 4 * n + j, :]
            e = p.stt(p.dve, y, bank[:, j * P:(j + 1) * P], weight(4 * n + j), y, ALU.mult, ALU.add, m, free=j > 0)
        core.acc.done(slot, e)
    jobs = [(expert, n) for expert in experts for n in range(QUARTERS)]

    def ahead():
        for expert, n in jobs[:depth]:
            up(expert, n)
            yield
    merge((routing, steps), (ahead(), depth))
    for expert, n in jobs[depth:]:
        up(expert, n)
        down()
    while waiting:
        down()


def expert_biases(core, wgt, made, b2, Y, ready):
    p = core.p
    wt = tmp(core, T)
    for n in range(QUARTERS):
        bank, slot, free = core.work.take()
        for j in range(4):
            m = p.tr(bank[0:E8, j * P:(j + 1) * P], wgt[:, 4 * n + j, :], core.weights["ident"], made, *free)
        e = p.cp(p.act, wt[0:E8, n * BANK:(n + 1) * BANK], bank[0:E8, :], m, free=True)
        core.work.done(slot, e)
    for n in range(QUARTERS):
        bank, slot, free = core.work.take()
        for j in range(4):
            i = 4 * n + j
            m = p.mm(bank[:, j * P:(j + 1) * P], wt[0:E8, i * P:(i + 1) * P], b2[0:E8, :], True, True, e, *free, *ready)
        y = Y[:, 4 * n:4 * n + 4, :]
        e2 = p.tt(p.dve, y, y, bank[:, :].rearrange("p (j d) -> p j d", d=D), ALU.add, m)
        core.work.done(slot, e2)
    return e2


def mixture(core):
    p = core.p
    nt = pre_norm(core)
    p.pe.pending = [*nt, core.came.l2f]
    routed = []

    def routing():
        _, wgt, made = yield from route(core, core.weights["e_wg"], ALU.add)
        routed.append(wgt)
        yield
        expert_biases(core, wgt, made, core.weights["e_b2"], core.X, [])
    C = MOE2_H // P
    experts = [(core.weights["e_w1"][:, e * MOE2_H:(e + 1) * MOE2_H], core.weights["e_b1"][:, e * C:(e + 1) * C],
                core.weights["e_w2"][:, e * C * D:(e + 1) * C * D], lambda i, e=e: routed[0][:, i, e:e + 1]) for e in range(E8)]
    run_experts(core, experts, MOE2_H, ACT.Relu, core.X, routing(), 6, 7)


def wave_kernels(core):
    p = core.p
    got = core.came.l3a
    col = lambda n: core.weights[n][0:H, :]
    t = core.weights["steps"][0:H, :]
    alpha, damp = tmp(core, 1)[0:H, :], tmp(core, 1)[0:H, :]
    copied = p.cp(p.dve, damp, col("v_damp"), got)
    yield from softplus(core, alpha, damp, [tmp(core, 1)[0:H, :] for _ in range(4)], [copied])
    p.ts(p.dve, alpha, alpha, -1.0, None, ALU.mult, None)
    env, arg, n, ker, s = tmp(core, S)[0:H, :], tmp(core, S)[0:H, :], tmp(core, S)[0:H, :], core.kern[:, :], tmp(core, 1)[0:H, :]
    a = p.dve.steps[-1]
    e = p.af(env, t, ACT.Exp, a, scale=alpha)
    p.ts(p.dve, arg, t, col("v_freq"), col("v_phase"), ALU.mult, ALU.add)
    ROUND = 12582912.0
    p.ts(p.dve, n, arg, 1.0 / (2 * np.pi), 0.25, ALU.mult, ALU.add)
    yield
    p.ts(p.dve, n, n, ROUND, None, ALU.add, None)
    p.ts(p.dve, n, n, -ROUND, None, ALU.add, None)
    c1 = 6.28125
    c2 = float(np.float32(np.round((2 * np.pi - c1) * 2 ** 21) / 2 ** 21))
    c3 = float(2 * np.pi - c1 - c2)
    for c in (c1, c2, c3):
        p.stt(p.dve, arg, n, -c, arg, ALU.mult, ALU.add)
        yield
    top = float(np.nextafter(np.float32(np.pi), np.float32(0)))
    p.ts(p.dve, arg, arg, float(np.pi / 2), top, ALU.add, ALU.min)
    a = p.ts(p.dve, arg, arg, -top, None, ALU.max, None)
    e2 = p.af(arg, arg, ACT.Sin, a)
    yield
    p.tt(p.dve, ker, env, arg, ALU.mult, e, e2)
    p.red(s, ker, ALU.add, mag=True)
    yield
    p.ts(p.dve, s, s, 1e-8, None, ALU.max, None)
    p.recip(s, s)
    k = p.ts(p.dve, ker, ker, s, None, ALU.mult, None)
    zero = core.kern_zero[:, :]
    z = p.fill(p.pool, zero, 0.0)
    core.kern_out = [p.dma(core.kern_dram[:, P:P + S], ker, k), p.dma(core.kern_dram[:, 0:P], zero, z)]


def wave(core):
    p = core.p
    nt = pre_norm(core)
    T0 = tmp3(core, H * S).rearrange("p (h s) -> p h s", s=S)
    T1 = tmp3(core, H * P).rearrange("p (h s) -> p h s", s=P)
    kd = core.kern_dram
    diag = lambda parts, shift, n: diagonals(kd, parts, 1 + shift, n)
    there = [*core.kern_out, core.came.l2x, core.came.l2f]
    toe = [p.dma(T0[:, :, :], diag(P, 0, S), *there),
           p.dma(T1[1:P, :, :], diag(P - 1, 1, P), *there),
           p.dma(T1[0:1, :, :], diag(1, 1, P), *there)]
    p.cp(p.pool, T0[:, :, S - 1:S], T0[:, :, S - 2:S - 1], *toe)
    toe = p.cp(p.pool, T1[:, :, P - 1:P], T1[:, :, P - 2:P - 1])
    turned = tmp(core, T)
    by_tile = lambda a: a.rearrange("p (i n) -> p i n", n=P)
    turn = p.cp(p.dve, by_tile(turned), backwards(by_tile(core.XNT[:, :])), *nt)
    F = tmp(core, NT * D).rearrange("p (i d) -> p i d", d=D)
    t1 = Ring([tmp(core, 2 * BANK) for _ in range(2)])
    wl = core.came.l3a
    for q in range(NT // 2):
        bank, slot, free = core.work.take()
        for j in range(2):
            i = 2 * q + j
            for n, w in enumerate(("v_wk", "v_wv")):
                m = p.mm(bank[:, n * 2 * P + j * P:n * 2 * P + (j + 1) * P], turned[:, i * P:(i + 1) * P], core.weights[w], True, True, *free, turn, wl)
        kv, ks, kf = t1.take()
        e = p.tt(p.dve, kv[:, 0:BANK].rearrange("p (n j d) -> p n j d", n=2, d=D), bank[:, :].rearrange("p (n j d) -> p n j d", n=2, d=D),
                 core.weights["v_bkv_bc"].rearrange("p (n d) -> p n d", d=D).unsqueeze(2).to_broadcast([P, 2, 2, D]), ALU.add, m, *kf)
        core.work.done(slot, e)
        k, v = kv[:, 0:2 * P], kv[:, 2 * P:4 * P]
        x = kv[:, BANK:BANK + 2 * P]
        a = p.ts(p.dve, x, k, 0.0, None, ALU.min, None)
        e = p.af(x, x, ACT.Exp, a)
        p.stt(p.dve, x, k, 0.0, x, ALU.max, ALU.add, e)
        f = p.tt(p.dve, F[:, 2 * q:2 * q + 2, :], x.rearrange("p (j d) -> p j d", d=D), v.rearrange("p (j d) -> p j d", d=D), ALU.mult)
        t1.done(ks, f)
    Fv = F.rearrange("p (b t) (h d) -> p b t h d", t=HALVES, d=HD)
    CV = tmp(core, NT * D).rearrange("p (i d) -> p i d", d=D)
    CVv = CV.rearrange("p (b t) (h d) -> p t h b d", t=HALVES, d=HD)
    for t in range(HALVES):
        for h0 in range(0, H, 8):
            bank, slot, free = core.work.take()
            for h in range(h0, h0 + 8):
                o = bank[:, (h - h0) * HW:(h - h0 + 1) * HW].rearrange("p (b d) -> p b d", d=HD)
                m = p.mm(o, T0[:, h, t * P:(t + 1) * P], Fv[:, :, 0, h, :], True, t == 0, *free, toe, f)
                if t:
                    m = p.mm(o, T1[:, h, :], Fv[:, :, 1, h, :], False, True)
            q = alternate(p, h0 // 8)
            e = p.cp(q, CVv[:, t, h0:h0 + 8, :, :], bank[:, :].rearrange("p (h b d) -> p h b d", h=8, d=HD), m)
            core.work.done(slot, e)
    convolved = [p.dve.steps[-1], p.act.steps[-1]]
    cp_, cm, ct = tmp(core, H)[0:H, :], tmp(core, 1)[0:H, :], tmp(core, H)[0:H, :]
    C = core.weights["v_coup"][0:H, :]
    p.red(cm, C, ALU.max)
    a = p.ts(p.dve, cp_, C, cm, None, ALU.subtract, None)
    e = p.af(cp_, cp_, ACT.Exp, a)
    p.red(cm, cp_, ALU.add, e)
    p.recip(cm, cm)
    a = p.ts(p.dve, cp_, cp_, cm, None, ALU.mult, None)
    bank, slot, free = core.work.take()
    m = p.tr(bank[0:H, 0:H], cp_, core.weights["ident"][0:H, 0:H], a, *free)
    e = p.cp(p.act, ct, bank[0:H, 0:H], m)
    core.work.done(slot, e)
    bank, slot, free = core.work.take()
    m = p.mm(bank[:, 0:H], core.weights["head_rows"][0:H, :], ct, True, True, e, *free)
    mix = tmp(core, D)
    u = tmp(core, H)
    e = p.cp(p.act, u, bank[:, 0:H], m)
    core.work.done(slot, e)
    mixed = p.tt(p.dve, mix.rearrange("p (i d) -> p i d", d=HD), u.unsqueeze(2).to_broadcast([P, H, HD]),
                 core.weights["same_d"].unsqueeze(1).to_broadcast([P, H, HD]), ALU.mult, e)
    CT_ = tmp(core, T)
    cv = transpose_all(core, lambda i: CV[:, i, :], lambda q: CT_[:, q * BANK:(q + 1) * BANK], lambda i: convolved[0])
    p.pe.pending = convolved
    G = tmp(core, T)
    for q in range(QUARTERS):
        cols = slice(q * BANK, (q + 1) * BANK)
        bank, slot, free = core.work.take()
        m = p.mm(bank[:, :], core.weights["v_wg"], core.XNT[:, cols], True, True, *free)
        e = p.af(G[:, cols], bank[:, :], ACT.Sigmoid, m, bias=core.weights["v_bg"], free=True)
        core.work.done(slot, e)
    for q in range(QUARTERS):
        cols = slice(q * BANK, (q + 1) * BANK)
        bank, slot, free = core.work.take()
        m = p.mm(bank[:, :], core.weights["v_wq"], core.XNT[:, cols], True, True, *free)
        kv, ks, kf = t1.take()
        x, y = kv[:, 0:BANK], kv[:, BANK:2 * BANK]
        p.ts(p.dve, x, bank[:, :], core.weights["v_bq"], 0.0, ALU.add, ALU.min, m, *kf)
        a = p.ts(p.dve, y, bank[:, :], core.weights["v_bq"], 0.0, ALU.add, ALU.max)
        core.work.done(slot, a)
        e2 = p.af(x, x, ACT.Exp, a)
        p.tt(p.dve, x, x, y, ALU.add, e2)
        g = p.tt(p.dve, G[:, cols], G[:, cols], x, ALU.mult, e)
        t1.done(ks, g)
        bank, slot, free = core.work.take()
        m = p.mm(bank[:, :], mix, CT_[:, cols], True, True, mixed, cv[q], *free)
        g = p.tt(p.dve, G[:, cols], G[:, cols], bank[:, :], ALU.mult, m)
        core.work.done(slot, g)
    add_product(core, lambda c, i: G[:, i * P:(i + 1) * P], lambda c: core.weights["v_wo"], lambda i: [g], bias_bc=core.weights["v_bo_bc"])


def guarded_attention(core):
    p = core.p
    nt = pre_norm(core)
    ready = [*nt, core.came.l3x]
    narrow(core, core.XNT, core.CT, core.weights["y_wq"], core.weights["y_wk"], core.weights["y_bq"], core.weights["y_bk"],
                project_values(core, core.CT, core.weights["y_wv"], core.weights["y_bv_bc"], ready),
                lambda b, n: core.XNT[:, b * S:(b + 1) * S], ready)
    above = tmp(core, T)
    p.ts(p.dve, above, core.XNT[:, :], 0.0, None, ALU.max, None)
    made = p.stt(p.dve, core.XNT[:, :], core.XNT[:, :], 0.0, above, ALU.min, ALU.add)
    add_product(core, lambda c, i: core.XNT[:, i * P:(i + 1) * P], lambda c: core.weights["y_wo"], lambda i: [made],
                     bias_bc=core.weights["y_bo_bc"])


def capped_mixture(core):
    p = core.p
    nt = pre_norm(core)
    p.pe.pending = [*nt, core.came.l3f]
    N = NT
    el, keep, inc, rank, live, lost = (tmp(core, N) for _ in range(6))
    routed = []

    def routing():
        sel, wgt, _ = yield from route(core, core.weights["z_wr"], ALU.max)
        routed.append(wgt)
        yield from cap(sel, wgt)

    def cap(sel, wgt):
        p.fill(p.dve, live, 1.0)
        for e in range(E8):
            a = p.tt(p.dve, el, sel[:, :, e], live, ALU.mult)
            bank, slot, free = core.work.take()
            p.mm(bank[:, 0:N], core.weights["upto"], el, True, True, a, *free)
            m = p.mm(bank[:, N:2 * N], core.weights["ones"], el, True, True)
            p.cp(p.dve, rank, bank[:, N:2 * N], m)
            p.scan(inc, core.weights["ones"][:, 0:N], rank, 0.0, ALU.mult, ALU.add)
            p.tt(p.dve, rank, inc, rank, ALU.subtract)
            r = p.tt(p.dve, rank, rank, bank[:, 0:N], ALU.add)
            core.work.done(slot, r)
            p.stt(p.dve, keep, rank, float(CAP), el, ALU.is_le, ALU.mult)
            p.tt(p.dve, wgt[:, :, e], wgt[:, :, e], keep, ALU.mult)
            p.tt(p.dve, el, el, keep, ALU.subtract)
            p.tt(p.dve, live, live, el, ALU.subtract)
            yield
        made = p.tt(p.dve, wgt, wgt, live.unsqueeze(2).to_broadcast([P, NT, E8]), ALU.mult)
        p.ts(p.dve, lost, live, -1.0, 1.0, ALU.mult, ALU.add)
        y = expert_biases(core, wgt, made, core.weights["z_b2"], core.X, [])
        for i in range(NT):
            y = p.stt(p.dve, core.X[:, i, :], core.weights["z_fb2_bc"], lost[:, i:i + 1], core.X[:, i, :], ALU.mult, ALU.add, y, free=i > 0)
    C = MOE3_H // P
    experts = [(core.weights["z_w1"][:, e * MOE3_H:(e + 1) * MOE3_H], core.weights["z_b1"][:, e * C:(e + 1) * C],
                core.weights["z_w2"][:, e * C * D:(e + 1) * C * D], lambda i, e=e: routed[0][:, i, e:e + 1]) for e in range(E8)]
    experts.append((core.weights["z_fw1"], core.weights["z_fb1"], core.weights["z_fw2"], lambda i: lost[:, i:i + 1]))
    run_experts(core, experts, MOE3_H, ACT.Gelu, core.X, routing(), 14, 5)


def begin(core, steps):
    for q in (core.p.pe, core.p.dve, core.p.act, core.p.pool):
        q.pending += steps


def run_blocks(core, blocks):
    p = core.p
    begin(core, [core.x_in, *core.const_ready])
    every = [(product_attention, lambda came: []),
             (context_attention, lambda came: [came.l0]),
             (sign_product, lambda came: [came.l0]),
             (hybrid, lambda came: [came.l1, came.mamba]),
             (raw_attention, lambda came: [came.l1b]),
             (recurrence, lambda came: [came.l1b]),
             (time_mixing, lambda came: [came.l2]),
             (wide_attention, lambda came: [came.l2x]),
             (mixture, lambda came: [came.l2f]),
             (wave, lambda came: [came.l3a]),
             (guarded_attention, lambda came: [came.l3x, came.l2x, came.l2f]),
             (capped_mixture, lambda came: [came.l3f])]
    for n, (block, needs) in enumerate(every):
        stage(core)
        if n == 5 and n not in blocks:
            finished(wave_kernels(core))
        if n in blocks:
            if n > 0:
                begin(core, needs(core.came))
            block(core)
        if n == 5:
            stage(core)
            core.came.l2x = load(core, "l2x")
            core.came.l2f = load(core, "l2f")
        if n == 7:
            stage(core)
            core.came.l3f = load(core, "l3f")
    stage(core)
    p.dma(core.out_dram, core.X[:, :, :])


def diagonals(kern, parts, first, n):
    return bass.AP(kern.tensor, kern.offset + first, [[1, parts], [P + S, H], [1, n]])


def backwards(ap):
    *outer, (step, n) = ap.ap
    return bass.AP(ap.tensor, ap.offset + step * (n - 1), [*outer, (-step, n)])


def build(nc, x, ctx_tok, ctx_feat, lens, sel, packs, out, blocks=tuple(range(12))):
    ctx = ExitStack()
    with ctx:
        kern = nc.dram_tensor("wave_kernels", [H, P + S], F32, kind="Internal").ap()
        core = Core()
        start(core, nc, ctx, packs, x, ctx_tok, ctx_feat, lens, kern, out, sel)
        run_blocks(core, blocks)
        block = ctx.enter_context(nc.Block())
        core.p.finish(block)


def tiled(a):
    return np.ascontiguousarray(a.reshape(NT, P, D).transpose(1, 0, 2))


def spread_matrices():
    out = np.zeros((P, 2, 2, 3, P), mybir.dt.np(BF16))
    f = np.arange(P)
    for n, parts in enumerate((QUERY_PARTS, KEY_PARTS)):
        for j, c in enumerate(parts):
            out[f, n, f // (2 * HD) % 2, c, HW * (f // HD % 2) + j * HD + f % HD] = 1
    return out.reshape(P, SPREADS, P)


def col(b):
    return np.ascontiguousarray(b.reshape(-1, P).T) if b.size >= P else b.reshape(-1, 1)


def rep(b):
    return np.broadcast_to(b.reshape(1, -1), (P, b.size))


def chunks(w):
    k, n = w.shape
    return w.reshape(k // P, P, n).transpose(1, 0, 2).reshape(P, -1)


def kernel(**inputs):
    import concourse.bacc as _bacc
    from concourse.bass_utils import run_bass_kernel_spmd as _run
    g = {k: np.asarray(v) for k, v in inputs.items()}
    s = np.arange(S, dtype=np.float32)
    i = np.arange(P)
    vals = {"ident": np.eye(P), "upto": i[:, None] <= i[None, :], "ones": np.ones((P, P)), "after": i[:, None] > i[None, :],
            "steps": np.broadcast_to(s, (P, S)),
            "head_rows": (i[None, :] // HD) == np.arange(H)[:, None], "same_d": (i[:, None] % HD) == np.arange(HD)[None, :],
            "before": np.broadcast_to((np.arange(E8)[None, :] < np.arange(E8)[:, None]).reshape(1, -1), (P, E8 * E8)),
            }
    rest, parts = np.float32(NEG_INF), []
    for _ in range(3):
        parts.append((np.array([rest]).view(np.uint32) & 0xFFFF0000).view(np.float32)[0])
        rest = np.float32(rest - parts[-1])
    vals["neg_parts"] = np.array(parts)[:, None]
    a = "L0_attn_"
    for n in ("q1", "q2", "k1", "k2", "v", "out"):
        vals["a_" + n] = g[a + "W_" + n]
    vals["a_bias_bc"] = rep(np.concatenate([g[a + "b_" + n] for n in ("q1", "q2", "k1", "k2", "v")]))
    vals.update(a_bout_bc=rep(g[a + "b_out"]), a_g=col(g[a + "ln_g"]), a_b=col(g[a + "ln_b"]))
    a = "L0_xattn_"
    vals.update(x_wq=g[a + "Wq"].T, x_wk=g[a + "Wk"].T, x_wv=g[a + "Wv"].T, x_wf=g[a + "Wf"].T, x_bq=col(g[a + "bq"]),
                x_bk=col(g[a + "bk"]), x_bv_bc=rep(g[a + "bv"]), x_bf_bc=rep(g[a + "bf"]), f_w=g["L0_ffn_weight"].T)
    a = "L1_attn_"
    w, b = g[a + "Wqkv_w"].T, g[a + "Wqkv_b"]
    vals.update(s_wq=w[:, :D], s_wk=w[:, D:2 * D], s_wv=w[:, 2 * D:], s_bq=col(b[:D]), s_bk=col(b[D:2 * D]),
                s_bv_bc=rep(b[2 * D:]), s_wo=g[a + "attn_out_w"].T, s_bo_bc=rep(g[a + "attn_out_b"]),
                s_norm=col(g[a + "attn_norm_w"]), s_normf_bc=rep(g[a + "normf_w"]), s_final_bc=rep(g[a + "final_norm_w"]),
                s_fc1=g[a + "fc1_w"].T, s_fc2=chunks(g[a + "fc2_w"].T))
    conv = D_INNER + 2 * D_STATE
    for l in range(M_LAYERS):
        w = g[a + "m_in_w"][l].T
        m = {"z": w[:, :D_INNER], "xbc": w[:, D_INNER:D_INNER + conv], "dt": w[:, D_INNER + conv:],
             "cw": g[a + "m_conv_w"][l].reshape(CONV_CH, P, D_CONV).transpose(1, 0, 2).reshape(P, -1),
             "cb": col(g[a + "m_conv_b"][l]), "dtb": rep(g[a + "m_dt_bias"][l]), "alog": rep(g[a + "m_A_log"][l]),
             "dskip_bc": rep(g[a + "m_D"][l]), "norm": col(g[a + "m_norm_w"][l]), "out": chunks(g[a + "m_out_w"][l].T)}
        vals.update({f"m{l}_{k}": v for k, v in m.items()})
    a = "L1_ffn_"
    vals.update(c_proj=g["L1_xattn_w_proj"].T, c_b_bc=rep(g["L1_xattn_b_proj"]), g_c0=col(g[a + "in_c"]), g_bo_bc=rep(g[a + "bo"]))
    for n in "fico":
        vals["g_w" + n], vals["g_u" + n] = g[a + "w" + n].T, g[a + "u" + n].T
        if n != "o":
            vals["g_b" + n] = col(g[a + "b" + n])
    a = "L2_attn_"
    vals.update(r_u=col(g[a + "time_first"]), r_wk=g[a + "Wk_t"].T, r_wv=g[a + "Wv_t"].T, r_wr=g[a + "Wr_t"].T,
                r_wkc=g[a + "Wk_c"].T, r_wvc=chunks(g[a + "Wv_c"].T), r_wrc=g[a + "Wr_c"].T, r_g1=col(g[a + "ln1_g"]),
                r_b1=col(g[a + "ln1_b"]), r_g2=col(g[a + "ln2_g"]), r_b2=col(g[a + "ln2_b"]), r_mk=col(g[a + "mix_k"]),
                r_mv=col(g[a + "mix_v"]), r_mr=col(g[a + "mix_r"]), r_ck=col(g[a + "cmix_k"]), r_cr=col(g[a + "cmix_r"]))
    a = "L2_xattn_"
    vals.update(w_q=g[a + "Wq"], w_k=g[a + "Wk"], w_v=g[a + "Wv"], w_o=chunks(g[a + "Wo"]),
                w_qn=np.concatenate([g[a + "q_norm_w"]] * 2)[:, None], w_kn=np.concatenate([g[a + "k_norm_w"]] * 2)[:, None])
    a = "L2_ffn_"
    vals.update(e_wg=g[a + "Wg"], e_w1=g[a + "W1"].transpose(1, 0, 2).reshape(P, -1), e_b1=col(g[a + "b1"].ravel()),
                e_w2=np.concatenate([chunks(w) for w in g[a + "W2"]], 1), e_b2=g[a + "b2"])
    a = "L3_attn_"
    w, b = g[a + "Wqkvg"].T, g[a + "bqkvg"]
    vals.update(v_wq=w[:, :D], v_wk=w[:, D:2 * D], v_wv=w[:, 2 * D:3 * D], v_wg=w[:, 3 * D:], v_bq=col(b[:D]),
                v_bkv_bc=rep(b[D:3 * D]), v_bg=col(b[3 * D:]), v_freq=col(g[a + "wave_frequency"]),
                v_damp=col(g[a + "wave_damping"]), v_phase=col(g[a + "wave_phase"]), v_coup=g[a + "field_coupling"],
                v_wo=g[a + "Wout"].T, v_bo_bc=rep(g[a + "bout"]))
    a = "L3_xattn_"
    vals.update(y_wq=g[a + "Wq"].T, y_wk=g[a + "Wk"].T, y_bq=col(g[a + "bq"]), y_bk=col(g[a + "bk"]), y_wv=g[a + "Wv"].T, y_bv_bc=rep(g[a + "bv"]), y_wo=g[a + "Wo"].T,
                y_bo_bc=rep(g[a + "bo"]))
    a = "L3_ffn_"
    vals.update(z_wr=g[a + "Wr"], z_w1=g[a + "W1"].transpose(1, 0, 2).reshape(P, -1), z_b1=col(g[a + "b1"].ravel()),
                z_w2=np.concatenate([chunks(w) for w in g[a + "W2"]], 1), z_b2=g[a + "b2"], z_fw1=g[a + "fw1"],
                z_fb1=col(g[a + "fb1"]), z_fw2=chunks(g[a + "fw2"]), z_fb2_bc=rep(g[a + "fb2"]))

    nc = _bacc.Bacc("TRN2", target_bir_lowering=False, num_devices=1)
    arrays = {"x": tiled(g["x"]), "ctx_tok": tiled(g["ctx_1024"]), "ctx_feat": np.ascontiguousarray(g["ctx_1024"].reshape(T, D).T),
              "lens": np.ascontiguousarray(np.broadcast_to(g["_lenS2"][None, :], (P, B)))}
    for name, layout, _ in PACKS:
        pack = np.zeros((P, columns(layout)), np.float32)
        o = 0
        for n, c in layout:
            v = vals[n]
            assert v.shape[1] == c, (n, v.shape, c)
            pack[:v.shape[0], o:o + c] = v
            o += c
        arrays["pack_" + name] = pack
    sel = np.zeros((P, H, P), mybir.dt.np(BF16))
    for h in range(H):
        sel[h:3 * H:H, h, :] = 1
    arrays["sel"] = np.concatenate([sel, spread_matrices()], 1)
    dram = {k: nc.dram_tensor(k, v.shape, mybir.dt.from_np(v.dtype), kind="ExternalInput").ap() for k, v in arrays.items()}
    out = nc.dram_tensor("out", (P, NT, D), F32, kind="ExternalOutput").ap()
    build(nc, dram["x"], dram["ctx_tok"], dram["ctx_feat"], dram["lens"], dram["sel"],
          {name: dram["pack_" + name] for name, _, _ in PACKS}, out)
    r = _run(nc, [arrays], core_ids=[0])
    y = r.results[0]["out"]
    return np.ascontiguousarray(y.transpose(1, 0, 2)).reshape(B, S, D)
```
